# Optimizing a Trainium2 kernel written in Bass

```python
import numpy as np
import jax
import jax.numpy as jnp

def _softmax(x, axis=-1):
    return jax.nn.softmax(x, axis=axis)

def _gelu(x):
    return jax.nn.gelu(x, approximate=True)

def _silu(x):
    return jax.nn.silu(x)

def _sigmoid(x):
    return jax.nn.sigmoid(x)

def _layernorm(x, axis=-1, eps=1e-05):
    m = jnp.mean(x, axis=axis, keepdims=True)
    v = jnp.var(x, axis=axis, keepdims=True)
    return (x - m) / jnp.sqrt(v + eps)

def _scatter_add(tgt, idx, src, axis=0):
    return tgt.at[idx].add(src)

def _segment_sum(src, seg, n):
    return jax.ops.segment_sum(src, seg, n)
kernel_name = 'mk_cond_resid_d4_seqx_r8_a8b869'

def setup_inputs(seed: int=0):
    np.random.seed(seed)
    _w = jnp.asarray

    def _rec_inputs():
        import jax
        import jax.numpy as jnp
        _rk = jax.random.key(seed)
        x = -0.0005207 + 1.001 * jax.random.normal(jax.random.fold_in(_rk, 1), (8, 128, 512), jnp.float32)
        _lenS = 128 - jax.random.randint(jax.random.fold_in(_rk, 7), (8,), 0, max(1, 128 // 4) + 1, jnp.int32)
        _lenS2 = 128 - jax.random.randint(jax.random.fold_in(_rk, 8), (8,), 0, max(1, 128 // 4) + 1, jnp.int32)
        itok_Bx16_0_63 = jax.random.randint(jax.random.fold_in(_rk, 11), (8, 16), 0, 64, jnp.int32)
        itok_B_207_1644 = jax.random.randint(jax.random.fold_in(_rk, 12), (8,), 207, 1645, jnp.int32)
        condB_coeff = 0.00219231 + 0.0100837 * jax.random.normal(jax.random.fold_in(_rk, 13), (8,), jnp.float32)
        itok_B_2_6 = jax.random.randint(jax.random.fold_in(_rk, 15), (8,), 2, 7, jnp.int32)
        itok_B_3_7 = jax.random.randint(jax.random.fold_in(_rk, 16), (8,), 3, 8, jnp.int32)
        _validS = jnp.arange(128)[None, :] < _lenS[:, None]
        _validS2 = jnp.arange(128)[None, :] < _lenS2[:, None]
        _causal = jnp.tril(jnp.ones((128, 128), dtype=bool))
        mask_Bx4096x4096_ik1 = jnp.where(jnp.ones((8, 512, 512), dtype=bool), 1, 0).astype(jnp.int32)
        return (x, itok_Bx16_0_63, itok_B_207_1644, condB_coeff, itok_B_2_6, itok_B_3_7, mask_Bx4096x4096_ik1)
    x, itok_Bx16_0_63, itok_B_207_1644, condB_coeff, itok_B_2_6, itok_B_3_7, mask_Bx4096x4096_ik1 = _rec_inputs()

    def _L0_cond_setup():
        import jax, jax.numpy as jnp
        import numpy as np
        B, S, HID = (4, 128, 512)
        D, HQ, HK = (128, 32, 8)
        PAGES, PSIZE, NPP = (64, 32, 16)
        THETA = 10000.0
        EPS = 1e-06
        SCALE = 1.0 / float(np.sqrt(D))

        def _rmsnorm(t, w):
            var = jnp.mean(t * t, axis=-1, keepdims=True)
            return t * jax.lax.rsqrt(var + EPS) * w

        def _rope(t, pos):
            inv_freq = 1.0 / THETA ** (jnp.arange(0, D, 2, dtype=jnp.float32) / D)
            freqs = pos[..., None].astype(jnp.float32) * inv_freq
            cos = jnp.cos(freqs)[:, :, None, :]
            sin = jnp.sin(freqs)[:, :, None, :]
            t1, t2 = (t[..., :D // 2], t[..., D // 2:])
            return jnp.concatenate([t1 * cos - t2 * sin, t2 * cos + t1 * sin], axis=-1)
        key = jax.random.key(seed)
        ks = jax.random.split(key, 10)
        x = jax.random.normal(ks[0], (B, S, HID), jnp.float32)
        Wq = jax.random.normal(ks[1], (HQ * D, HID), jnp.float32) * 0.02
        Wk = jax.random.normal(ks[2], (HK * D, HID), jnp.float32) * 0.02
        Wv = jax.random.normal(ks[3], (HK * D, HID), jnp.float32) * 0.02
        Wo = jax.random.normal(ks[4], (HID, HQ * D), jnp.float32) * 0.02
        q_norm_w = jax.random.uniform(ks[5], (D,), jnp.float32)
        k_norm_w = jax.random.uniform(ks[6], (D,), jnp.float32)
        k_cache = jax.random.normal(ks[7], (PAGES, PSIZE, HK, D), jnp.float32)
        v_cache = jax.random.normal(ks[8], (PAGES, PSIZE, HK, D), jnp.float32)
        block_table = jnp.arange(B * NPP, dtype=jnp.int32).reshape(B, NPP)
        cache_seqlens = jax.random.randint(ks[9], (B,), 0, 475).astype(jnp.int32)
        return dict(x=x, Wq=Wq, Wk=Wk, Wv=Wv, Wo=Wo, q_norm_w=q_norm_w, k_norm_w=k_norm_w, k_cache=k_cache, v_cache=v_cache, block_table=block_table, cache_seqlens=cache_seqlens)
    _L0_cond_all = _L0_cond_setup()
    _L0_cond_in = {k: v for k, v in _L0_cond_all.items() if k in ('Wq', 'Wk', 'Wv', 'Wo', 'q_norm_w', 'k_norm_w', 'k_cache', 'v_cache')}
    del _L0_cond_all

    def _L1_cond_setup():
        import jax, jax.numpy as jnp
        import numpy as np
        B, S, D_IN, D_OUT = (4, 64, 512, 512)
        key = jax.random.key(seed)
        k1, k2, k3, k4, k5 = jax.random.split(key, 5)
        hidden_states = jax.random.normal(k1, (B, S, D_IN), dtype=jnp.float32)
        W = jax.random.normal(k2, (D_OUT, D_IN), dtype=jnp.float32) * 0.02
        b = jax.random.normal(k3, (D_OUT,), dtype=jnp.float32) * 0.02
        coeff = jax.random.normal(k4, (B,), dtype=jnp.float32) * 0.01
        mask = jax.random.randint(k5, (B, D_IN, D_OUT), 0, 2, dtype=jnp.int32)
        return {'hidden_states': hidden_states, 'W': W, 'b': b, 'coeff': coeff, 'mask': mask}
    _L1_cond_all = _L1_cond_setup()
    _L1_cond_in = {k: v for k, v in _L1_cond_all.items() if k in ('W', 'b')}
    del _L1_cond_all

    def _L2_cond_setup():
        import jax, jax.numpy as jnp
        import numpy as np
        B, N, H, F = (4, 64, 512, 1376)
        L, R, RANK = (1, 16, 16)
        SCALE = 0.5
        key = jax.random.key(seed)
        ks = jax.random.split(key, 12)
        nrm = lambda k, shape, fan: jax.random.normal(k, shape, jnp.float32) * fan ** (-0.5)
        inp = {'x': jax.random.normal(ks[0], (B, N, H), jnp.float32), 'W_gate': nrm(ks[1], (F, H), H), 'W_up': nrm(ks[2], (F, H), H), 'W_down': nrm(ks[3], (H, F), F), 'A_gate': nrm(ks[4], (L, R, RANK, H), H), 'B_gate': nrm(ks[5], (L, R, F, RANK), RANK), 'A_up': nrm(ks[6], (L, R, RANK, H), H), 'B_up': nrm(ks[7], (L, R, F, RANK), RANK), 'A_down': nrm(ks[8], (L, R, RANK, F), F), 'B_down': nrm(ks[9], (L, R, H, RANK), RANK), 'lora_indices': jax.random.randint(ks[10], (B,), 0, R), 'layer_idx': 0}
        return inp
    _L2_cond_all = _L2_cond_setup()
    _L2_cond_in = {k: v for k, v in _L2_cond_all.items() if k in ('W_gate', 'W_up', 'W_down', 'A_gate', 'B_gate', 'A_up', 'B_up', 'A_down', 'B_down')}
    del _L2_cond_all

    def _L3_cond_setup():
        import jax, jax.numpy as jnp
        import numpy as np
        MAX_LORAS, OUT, IN = (8, 512, 512)
        B, S = (4, 256)
        key = jax.random.key(seed)
        k1, k2, k3 = jax.random.split(key, 3)
        x = jax.random.normal(k1, (B, S, IN), dtype=jnp.float32)
        weight = jax.random.normal(k2, (MAX_LORAS, OUT, IN), dtype=jnp.float32) * 0.02
        adapter_ids = jax.random.randint(k3, (B,), 0, MAX_LORAS, dtype=jnp.int32)
        return {'x': x, 'weight': weight, 'adapter_ids': adapter_ids}
    _L3_cond_all = _L3_cond_setup()
    _L3_cond_in = {k: v for k, v in _L3_cond_all.items() if k in ('weight',)}
    del _L3_cond_all
    return {'x': x, 'itok_Bx16_0_63': itok_Bx16_0_63, 'itok_B_207_1644': itok_B_207_1644, 'condB_coeff': condB_coeff, 'itok_B_2_6': itok_B_2_6, 'itok_B_3_7': itok_B_3_7, 'mask_Bx4096x4096_ik1': mask_Bx4096x4096_ik1, 'L0_cond_Wq': _L0_cond_in['Wq'], 'L0_cond_Wk': _L0_cond_in['Wk'], 'L0_cond_Wv': _L0_cond_in['Wv'], 'L0_cond_Wo': _L0_cond_in['Wo'], 'L0_cond_q_norm_w': _L0_cond_in['q_norm_w'], 'L0_cond_k_norm_w': _L0_cond_in['k_norm_w'], 'L0_cond_k_cache': _L0_cond_in['k_cache'], 'L0_cond_v_cache': _L0_cond_in['v_cache'], 'L1_cond_W': _L1_cond_in['W'], 'L1_cond_b': _L1_cond_in['b'], 'L2_cond_W_gate': _L2_cond_in['W_gate'], 'L2_cond_W_up': _L2_cond_in['W_up'], 'L2_cond_W_down': _L2_cond_in['W_down'], 'L2_cond_A_gate': _L2_cond_in['A_gate'], 'L2_cond_B_gate': _L2_cond_in['B_gate'], 'L2_cond_A_up': _L2_cond_in['A_up'], 'L2_cond_B_up': _L2_cond_in['B_up'], 'L2_cond_A_down': _L2_cond_in['A_down'], 'L2_cond_B_down': _L2_cond_in['B_down'], 'L3_cond_weight': _L3_cond_in['weight']}

def reference(x, itok_Bx16_0_63, itok_B_207_1644, condB_coeff, itok_B_2_6, itok_B_3_7, mask_Bx4096x4096_ik1, L0_cond_Wq, L0_cond_Wk, L0_cond_Wv, L0_cond_Wo, L0_cond_q_norm_w, L0_cond_k_norm_w, L0_cond_k_cache, L0_cond_v_cache, L1_cond_W, L1_cond_b, L2_cond_W_gate, L2_cond_W_up, L2_cond_W_down, L2_cond_A_gate, L2_cond_B_gate, L2_cond_A_up, L2_cond_B_up, L2_cond_A_down, L2_cond_B_down, L3_cond_weight):
    import jax
    import jax.numpy as jnp

    def _L0_cond_ref(x, Wq, Wk, Wv, Wo, q_norm_w, k_norm_w, k_cache, v_cache, block_table, cache_seqlens):
        import jax, jax.numpy as jnp
        import numpy as np
        B, S, HID = (4, 128, 512)
        D, HQ, HK = (128, 32, 8)
        PAGES, PSIZE, NPP = (64, 32, 16)
        THETA = 10000.0
        EPS = 1e-06
        SCALE = 1.0 / float(np.sqrt(D))

        def _rmsnorm(t, w):
            var = jnp.mean(t * t, axis=-1, keepdims=True)
            return t * jax.lax.rsqrt(var + EPS) * w

        def _rope(t, pos):
            inv_freq = 1.0 / THETA ** (jnp.arange(0, D, 2, dtype=jnp.float32) / D)
            freqs = pos[..., None].astype(jnp.float32) * inv_freq
            cos = jnp.cos(freqs)[:, :, None, :]
            sin = jnp.sin(freqs)[:, :, None, :]
            t1, t2 = (t[..., :D // 2], t[..., D // 2:])
            return jnp.concatenate([t1 * cos - t2 * sin, t2 * cos + t1 * sin], axis=-1)
        bsz, seqlen, _ = x.shape
        q = jnp.einsum('bsd,ed->bse', x, Wq).reshape(bsz, seqlen, HQ, D)
        k = jnp.einsum('bsd,ed->bse', x, Wk).reshape(bsz, seqlen, HK, D)
        v = jnp.einsum('bsd,ed->bse', x, Wv).reshape(bsz, seqlen, HK, D)
        q = _rmsnorm(q, q_norm_w)
        k = _rmsnorm(k, k_norm_w)
        pos = cache_seqlens[:, None] + jnp.arange(seqlen)[None, :]
        q = _rope(q, pos)
        k = _rope(k, pos)
        L = NPP * PSIZE
        kc = k_cache[block_table].reshape(bsz, L, HK, D)
        vc = v_cache[block_table].reshape(bsz, L, HK, D)
        k_all = jnp.concatenate([kc, k], axis=1)
        v_all = jnp.concatenate([vc, v], axis=1)
        valid_c = jnp.arange(L)[None, :] < cache_seqlens[:, None]
        valid = jnp.concatenate([valid_c, jnp.ones((bsz, seqlen), dtype=bool)], axis=1)
        rep = HQ // HK
        k_all = jnp.repeat(k_all, rep, axis=2)
        v_all = jnp.repeat(v_all, rep, axis=2)
        scores = jnp.einsum('bqhd,bkhd->bhqk', q, k_all) * SCALE
        scores = jnp.where(valid[:, None, None, :], scores, -1e+30)
        probs = jax.nn.softmax(scores, axis=-1)
        o = jnp.einsum('bhqk,bkhd->bqhd', probs, v_all)
        o = o.reshape(bsz, seqlen, HQ * D)
        return jnp.einsum('bse,de->bsd', o, Wo)

    def _L1_cond_ref(hidden_states, W, b, coeff, mask):
        import jax, jax.numpy as jnp
        import numpy as np
        B, S, D_IN, D_OUT = (4, 64, 512, 512)
        output = jnp.einsum('bsi,oi->bso', hidden_states, W) + b
        sign = (2 * mask - 1).astype(hidden_states.dtype)
        diff = jnp.einsum('bsi,bio->bso', hidden_states, sign)
        return output + diff * coeff[:, None, None]

    def _L2_cond_ref(x, W_gate, W_up, W_down, A_gate, B_gate, A_up, B_up, A_down, B_down, lora_indices, layer_idx):
        import jax, jax.numpy as jnp
        import numpy as np
        B, N, H, F = (4, 64, 512, 1376)
        L, R, RANK = (1, 16, 16)
        SCALE = 0.5

        def lora_add(base, inp, A, B):
            Ab = A[layer_idx][lora_indices]
            Bb = B[layer_idx][lora_indices]
            t = jnp.einsum('bri,bni->bnr', Ab, inp)
            return base + jnp.einsum('bor,bnr->bno', Bb, t) * SCALE
        gate = lora_add(jnp.einsum('bnh,fh->bnf', x, W_gate), x, A_gate, B_gate)
        up = lora_add(jnp.einsum('bnh,fh->bnf', x, W_up), x, A_up, B_up)
        act = jax.nn.silu(gate) * up
        down = lora_add(jnp.einsum('bnf,hf->bnh', act, W_down), act, A_down, B_down)
        return down

    def _L3_cond_ref(x, weight, adapter_ids):
        import jax, jax.numpy as jnp
        import numpy as np
        MAX_LORAS, OUT, IN = (8, 512, 512)
        B, S = (4, 256)
        w = weight[adapter_ids]
        return jnp.einsum('bsi,boi->bso', x, w)
    x = x + _L0_cond_ref(x, L0_cond_Wq, L0_cond_Wk, L0_cond_Wv, L0_cond_Wo, L0_cond_q_norm_w, L0_cond_k_norm_w, L0_cond_k_cache, L0_cond_v_cache, itok_Bx16_0_63, itok_B_207_1644)
    x = x + _L1_cond_ref(x, L1_cond_W, L1_cond_b, condB_coeff, mask_Bx4096x4096_ik1)
    x = x + _L2_cond_ref(x, L2_cond_W_gate, L2_cond_W_up, L2_cond_W_down, L2_cond_A_gate, L2_cond_B_gate, L2_cond_A_up, L2_cond_B_up, L2_cond_A_down, L2_cond_B_down, itok_B_2_6, 0)
    x = x + _L3_cond_ref(x, L3_cond_weight, itok_B_3_7)
    return x

_drawn_inputs = setup_inputs


def setup_inputs(seed=0):
    import zlib

    import numpy as np

    out = dict(_drawn_inputs(seed))
    spreads = {}
    factors = {'L0_cond_Wk': 24.787,
     'L0_cond_Wv': 23.631,
     'L0_cond_k_norm_w': 24.424,
     'L1_cond_b': 9.797,
     'L0_cond_k_cache': 8.0,
     'L0_cond_v_cache': 5.205}
    for name, (base, spread) in spreads.items():
        noise = np.random.default_rng([zlib.crc32(name.encode()), seed]).standard_normal(out[name].shape)
        drawn = base * np.exp(spread * noise) if base else spread * noise
        out[name] = jnp.asarray(drawn.astype(out[name].dtype))
    for name, factor in factors.items():
        out[name] = (out[name] * factor).astype(out[name].dtype)
    return out
```

```python
from contextlib import ExitStack

import numpy as np

import concourse.bass as bass
from concourse import mybir

F32 = mybir.dt.float32
F32R = mybir.dt.float32r
BF16 = mybir.dt.bfloat16
I32 = mybir.dt.int32
U32 = mybir.dt.uint32
ALU = mybir.AluOpType
ACT = mybir.ActivationFunctionType

P = 128
B, S, DM = 8, 128, 512
DC = DM // P
D = 128
HK, G = 8, 4
PAGES, PSIZE, NPP = 64, 32, 16
L = NPP * PSIZE
LC = L // P
KEYS = L + S
KC = KEYS // P
EPS = 1e-6
SCALE = D ** -0.5
THETA = 10000.0
MASKED = 1e30
F = 1376
FC = -(-F // P)
FR = F - (FC - 1) * P
NFREE = 512
FN = [(n, min(NFREE, F - n)) for n in range(0, F, NFREE)]
RANK = 16
UP0 = 32
LORA_SCALE = 0.5

TWO_PI = 2 * np.pi
PI_A = 6.28125
PI_B = float(np.float32(np.round((TWO_PI - PI_A) * 2 ** 20) / 2 ** 20))
PI_C = float(np.float32(TWO_PI - PI_A - PI_B))
PI_F32 = 3.1415925
ROUND = 1.5 * 2 ** 23


def three_pass(pe, out, l_hi, l_lo, r_hi, r_lo, first, last):
    pe.matmul(out, l_hi, r_hi, start=first, stop=False)
    pe.matmul(out, l_hi, r_lo, start=False, stop=False)
    return pe.matmul(out, l_lo, r_hi, start=False, stop=last)


def wait_apart(eng, sem, count, passed):
    eng.wait_ge(sem, count)
    if not isinstance(count, int):
        eng.sem_inc(passed, 1)


def make_identity(nc, pool, ident, step):
    pool.memset(ident, 0.0).then_inc(step, 1)
    pool.wait_ge(step, 1)
    pool.affine_select(out=ident, in_=ident, compare_op=ALU.not_equal, fill=1.0, base=0,
                       pattern=[[-1, P]], channel_multiplier=1).then_inc(step, 1)


def attention(nc, x, block_table, seqlens, wq, wk, wv, wo, qw, kw, k_cache, v_cache, inv_freq, x_out):
    with ExitStack() as ctx:
        def sb(name, shape, dt=F32):
            return ctx.enter_context(nc.sbuf_tensor("at_" + name, shape, dt))

        def sem(name):
            return ctx.enter_context(nc.semaphore(name))

        ps = ctx.enter_context(nc.psum_tensor("at_ps", [P, 8 * NFREE], F32))

        def bank(n, cols=NFREE):
            return ps[:, n * NFREE:n * NFREE + cols]

        SCORE_PARTS = [(0, KEYS // 2), (KEYS // 2, KEYS)]

        def slot(h):
            at = 2 * (h % 2) * NFREE + NFREE - SCORE_PARTS[1][0]
            return ps[:, at:at + KEYS]

        Q_BANK, KV_BANK, A_BANK, B_BANK, O_BANK = 4, 5, 6, 7, 3

        ident = sb("ident", [P, P])
        xres = sb("xres", [P, B, DM])
        xT_hi = sb("xT_hi", [P, DC, B * S], F32R)
        xT_lo = sb("xT_lo", [P, DC, B * S], F32R)
        wq_raw = sb("wq_raw", [P, G, DM])
        wkv_raw = sb("wkv_raw", [P, 2, DM])
        wo_raw = sb("wo_raw", [P, DC, G * D])
        wqT_hi = sb("wqT_hi", [P, DC, G * D], F32R)
        wqT_lo = sb("wqT_lo", [P, DC, G * D], F32R)
        wkvT_hi = sb("wkvT_hi", [P, DC, 2 * D], F32R)
        wkvT_lo = sb("wkvT_lo", [P, DC, 2 * D], F32R)
        woT_hi = sb("woT_hi", [P, G, DM], F32R)
        woT_lo = sb("woT_lo", [P, G, DM], F32R)
        q_cos = sb("q_cos", [P, B, D])
        q_sin = sb("q_sin", [P, B, D])
        k_cos = sb("k_cos", [P, B, D])
        k_sin = sb("k_sin", [P, B, D])
        mask = sb("mask", [P, B, KEYS], BF16)
        k_raw = [sb(f"k_raw{j}", [P, LC, D]) for j in range(2)]
        v_raw = [sb(f"v_raw{j}", [P, LC, D]) for j in range(2)]
        kT_hi = sb("kT_hi", [P, KEYS], F32R)
        kT_lo = sb("kT_lo", [P, KEYS], F32R)
        v_hi = [sb(f"v_hi{j}", [P, KC, D], F32R) for j in range(2)]
        v_lo = [sb(f"v_lo{j}", [P, KC, D], F32R) for j in range(2)]
        qT_hi = [sb(f"qT_hi{j}", [P, G * S], F32R) for j in range(2)]
        qT_lo = [sb(f"qT_lo{j}", [P, G * S], F32R) for j in range(2)]
        u_q = sb("u_q", [P, G, D])
        w_q = sb("w_q", [P, G, D])
        q_rot = sb("q_rot", [P, G, D])
        u_k = sb("u_k", [P, D])
        w_k = sb("w_k", [P, D])
        k_rot = sb("k_rot", [P, D])
        square = sb("square", [P, G + 1, D])
        sumsq = [sb(f"sumsq{j}", [P, G + 1]) for j in range(2)]
        d_eps = sb("d_eps", [P, G])
        minus_half = sb("minus_half", [P, G])
        inv_rms = [sb(f"inv_rms{j}", [P, G + 1]) for j in range(2)]
        scores = [sb(f"scores{j}", [P, KEYS]) for j in range(2)]
        neg_max = sb("neg_max", [P, G])
        row_sum = sb("row_sum", [P, G])
        row_inv = sb("row_inv", [P, G])
        probs = sb("probs", [P, G, KEYS])
        pT_hi = [sb(f"pT_hi{j}", [P, G * S], F32R) for j in range(3)]
        pT_lo = [sb(f"pT_lo{j}", [P, G * S], F32R) for j in range(3)]
        oT_hi = sb("oT_hi", [P, G * S], F32R)
        oT_lo = sb("oT_lo", [P, G * S], F32R)
        key_row = sb("key_row", [P, B * LC])
        key_idx = [sb(f"key_idx{j}", [P, LC], U32) for j in range(2)]
        head_no = sb("head_no", [P, 1])
        seq_i = sb("seq_i", [P, B], I32)
        seq_f = sb("seq_f", [P, B])
        in_page_f = sb("in_page_f", [P, 1])
        tok_i = sb("tok_i", [P, 1], I32)
        tok_f = sb("tok_f", [P, 1])
        HALF = D // 2
        qw_sb, kw_sb, invf_sb = u_q[:, 0, :], u_q[:, 1, :], u_q[:, 2, 0:HALF]
        table_sb = u_q[:, 3, 0:B * NPP].bitcast(I32)
        angle = probs[:, 0, 0:B * HALF]
        turns = probs[:, 1, 0:B * HALF]
        sin_t = probs[:, 2, 0:B * HALF]
        cos_t = probs[:, 3, 0:B * HALF]
        key_no_i = scores[0][:, 0:L].bitcast(I32)
        key_no = scores[1][:, 0:L]

        x_loaded = sem("x_loaded")
        small_loaded = sem("small_loaded")
        ident_step = sem("ident_step")
        iota_done = sem("iota_done")
        table_step = sem("table_step")
        angles_ready = sem("angles_ready")
        sincos_ready = sem("sincos_ready")
        tables_ready = sem("tables_ready")
        rows_ready = sem("rows_ready")
        xT_in_psum = sem("xT_in_psum")
        xT_hi_done = sem("xT_hi_done")
        xT_done = sem("xT_done")
        wqkv_loaded = sem("wqkv_loaded")
        wo_loaded = sem("wo_loaded")
        wqkv_in_psum = sem("wqkv_in_psum")
        wqkv_hi_done = sem("wqkv_hi_done")
        wqkv_done = sem("wqkv_done")
        wo_in_psum = sem("wo_in_psum")
        wo_hi_done = sem("wo_hi_done")
        wo_done = sem("wo_done")
        idx_ready = sem("idx_ready")
        head_step = sem("head_step")
        k_loaded = [sem(f"k_loaded{j}") for j in range(2)]
        v_loaded = [sem(f"v_loaded{j}") for j in range(2)]
        q_in_psum = sem("q_in_psum")
        kv_in_psum = sem("kv_in_psum")
        q_turned = sem("q_turned")
        q_squared = sem("q_squared")
        q_rot_done = sem("q_rot_done")
        kv_read = sem("kv_read")
        k_turned = sem("k_turned")
        v_new_done = sem("v_new_done")
        k_rot_done = sem("k_rot_done")
        scale_ready = sem("scale_ready")
        k_scale_ready = sem("k_scale_ready")
        v_hi_done = sem("v_hi_done")
        v_cache_done = sem("v_cache_done")
        kc_in_psum = sem("kc_in_psum")
        kc_hi_done = sem("kc_hi_done")
        kc_done = sem("kc_done")
        kn_in_psum = sem("kn_in_psum")
        kn_hi_done = sem("kn_hi_done")
        kn_done = sem("kn_done")
        qT_in_psum = sem("qT_in_psum")
        qT_hi_done = sem("qT_hi_done")
        qT_done = sem("qT_done")
        scores_in_psum = sem("scores_in_psum")
        scores_done = sem("scores_done")
        exp_done = sem("exp_done")
        inv_done = sem("inv_done")
        probs_done = sem("probs_done")
        pT_in_psum = sem("pT_in_psum")
        pT_hi_done = sem("pT_hi_done")
        pT_done = sem("pT_done")
        pv_done = sem("pv_done")
        oT_hi_done = sem("oT_hi_done")
        oT_done = sem("oT_done")
        y_in_psum = sem("y_in_psum")
        y_bank_free = sem("y_bank_free")
        pool_passed = sem("pool_passed")
        dve_passed = sem("dve_passed")
        stored = sem("stored")

        QKV_GROUPS, WO_GROUPS = DC + DC // 2, G
        WEIGHT_BANKS = [A_BANK, B_BANK]

        def upto(g, b, per, k=0):
            return g * (B * per) + (b * per + k)

        def following(g, b):
            return (g, b + 1) if b + 1 < B else (g + 1, 0)

        def weight_groups(b, slot, last):
            groups = {0: {4: [0]}, 1: {0: [1], 1: [2], 2: [3]}}
            if not last:
                groups[B - 2] = {0: [0], 1: [1], 2: [2], 3: [3]}
                groups[B - 1] = {0: [4], 1: [5]}
            return groups.get(b, {}).get(slot, [])

        block = ctx.enter_context(nc.Block())

        @block.sync
        def _(sp):
            sp.dma_start(xres[:], x.rearrange("b s d -> s b d")).then_inc(x_loaded, 16)
            sp.dma_start(seq_i[:], seqlens.rearrange("(o b) -> o b", o=1).broadcast_to([P, B])).then_inc(small_loaded, 16)
            sp.dma_start(table_sb, block_table.rearrange("(o b) n -> o (b n)", o=1).broadcast_to([P, B * NPP])).then_inc(small_loaded, 16)
            sp.dma_start(qw_sb, qw.rearrange("(o d) -> o d", o=1).broadcast_to([P, D])).then_inc(small_loaded, 16)
            sp.dma_start(kw_sb, kw.rearrange("(o d) -> o d", o=1).broadcast_to([P, D])).then_inc(small_loaded, 16)
            sp.dma_start(invf_sb, inv_freq.rearrange("(o d) -> o d", o=1).broadcast_to([P, HALF])).then_inc(small_loaded, 16)

            def load_qkv(g):
                sp.dma_start(wq_raw[:], wq[bass.ds(g * (G * D), G * D), :].rearrange("(e p) d -> p e d", p=P)).then_inc(wqkv_loaded, 16)
                sp.dma_start(wkv_raw[:, 0, :], wk[bass.ds(g * D, D), :]).then_inc(wqkv_loaded, 16)
                sp.dma_start(wkv_raw[:, 1, :], wv[bass.ds(g * D, D), :]).then_inc(wqkv_loaded, 16)

            def load_wo(g):
                sp.dma_start(wo_raw[:], wo[:, bass.ds(g * (G * D), G * D)].rearrange("(n p) e -> p n e", p=P)).then_inc(wo_loaded, 16)

            load_qkv(0)
            load_wo(0)
            with sp.Fori(0, HK - 1) as g:
                sp.wait_ge(wqkv_in_psum, g * QKV_GROUPS + QKV_GROUPS)
                sp.wait_ge(wo_in_psum, g * WO_GROUPS + WO_GROUPS)
                load_qkv(g + 1)
                load_wo(g + 1)
            for b in range(B):
                sp.wait_ge(y_bank_free, 1 + upto(HK - 1, b, 1, 1))
                sp.dma_start(x_out[b], xres[:, b, :]).then_inc(stored, 16)
            sp.wait_ge(stored, 16 * B)

        @block.gpsimd
        def _(pool):
            make_identity(nc, pool, ident[:], ident_step)
            pool.wait_ge(ident_step, 2)
            pool.iota(tok_i[:], pattern=[[0, 1]], base=0, channel_multiplier=1).then_inc(iota_done, 1)
            pool.iota(key_no_i, pattern=[[1, L]], base=0, channel_multiplier=0).then_inc(iota_done, 1)
            pool.memset(d_eps[:], D * EPS).then_inc(iota_done, 1)
            pool.memset(minus_half[:], -0.5).then_inc(iota_done, 1)
            pool.memset(head_no[:], 0.0).then_inc(head_step, 1)
            pool.memset(mask[:, :, L:KEYS], 0.0).then_inc(iota_done, 1)

            def indices(b):
                return pool.tensor_scalar(key_idx[b % 2][:], key_row[:, b * LC:(b + 1) * LC], head_no[:, 0:1], None, ALU.add)

            def gather(b, cs, cache, raw, loaded):
                for c in cs:
                    pool.indirect_dma_start(
                        out=raw[b % 2][:, c, :], out_offset=None,
                        in_=cache.rearrange("a r h d -> (a r h) d"),
                        in_offset=bass.IndirectOffsetOnAxis(ap=key_idx[b % 2][:, c:c + 1], axis=0),
                    ).then_inc(loaded[b % 2], 16)

            def next_head(g):
                wait_apart(pool, idx_ready, upto(g, B - 1, 1, 1), pool_passed)
                pool.tensor_scalar(head_no[:], head_no[:], 1.0, None, ALU.add).then_inc(head_step, 1)

            def start_gather(g, b):
                wait_apart(pool, head_step, g + 1, pool_passed)
                indices(b).then_inc(idx_ready, 1)
                wait_apart(pool, idx_ready, upto(g, b, 1, 1), pool_passed)

            def rotate_k(g, b):
                pool.wait_ge(k_turned, upto(g, b, 1, 1))
                pool.tensor_tensor(k_rot[:, 0:HALF], u_k[:, 0:HALF], w_k[:, HALF:D], ALU.subtract)
                pool.tensor_tensor(k_rot[:, HALF:D], u_k[:, HALF:D], w_k[:, 0:HALF], ALU.add).then_inc(k_rot_done, 1)

            def rotate_q(g, b):
                pool.wait_ge(q_turned, upto(g, b, 1, 1))
                pool.tensor_tensor(q_rot[:, :, 0:HALF], u_q[:, :, 0:HALF], w_q[:, :, HALF:D], ALU.subtract)
                pool.tensor_tensor(q_rot[:, :, HALF:D], u_q[:, :, HALF:D], w_q[:, :, 0:HALF], ALU.add).then_inc(q_rot_done, 1)

            def key_scale(g, b):
                j = b % 2
                pool.wait_ge(kv_read, upto(g, b, 1, 1))
                pool.tensor_tensor(inv_rms[j][:, G:G + 1], sumsq[j][:, G:G + 1], d_eps[:, 0:1], ALU.add).then_inc(k_scale_ready, 1)
                pool.wait_ge(k_scale_ready, upto(g, b, 2, 1))
                pool.tensor_tensor(inv_rms[j][:, G:G + 1], inv_rms[j][:, G:G + 1], minus_half[:, 0:1], ALU.pow).then_inc(k_scale_ready, 1)

            def query_scale(g, b):
                j = b % 2
                pool.wait_ge(q_squared, upto(g, b, 1, 1))
                pool.tensor_tensor(inv_rms[j][:, 0:G], sumsq[j][:, 0:G], d_eps[:], ALU.add).then_inc(scale_ready, 1)
                pool.wait_ge(scale_ready, upto(g, b, 2, 1))
                pool.tensor_tensor(inv_rms[j][:, 0:G], inv_rms[j][:, 0:G], minus_half[:], ALU.pow).then_inc(scale_ready, 1)

            def normalise(g, b, h):
                wait_apart(pool, inv_done, upto(g, b, G, h + 1), pool_passed)
                pool.tensor_scalar(probs[:, h, :], probs[:, h, :], row_inv[:, h:h + 1], 1.0, ALU.mult, ALU.mult).then_inc(probs_done, 1)

            pool.wait_ge(iota_done, 5)
            pool.wait_ge(rows_ready, 4)
            for b in range(2):
                start_gather(0, b)
                gather(b, range(LC), k_cache, k_raw, k_loaded)
                gather(b, range(LC), v_cache, v_raw, v_loaded)
            rotate_q(0, 0)
            key_scale(0, 0)
            rotate_k(0, 0)
            query_scale(0, 0)
            rotate_q(0, 1)

            def group(g, last):
                for b in range(B):
                    g1, b1 = following(g, b)
                    g2, b2 = following(g1, b1)
                    more, more2 = not (last and b == B - 1), not (last and b >= B - 2)

                    def keys(cs):
                        if more2:
                            gather(b2, cs, k_cache, k_raw, k_loaded)

                    def values(cs):
                        if more2:
                            gather(b2, cs, v_cache, v_raw, v_loaded)

                    if more2:
                        if b2 == 0:
                            next_head(g)
                        pool.wait_ge(kc_in_psum, upto(g, b, 1, 1))
                        pool.wait_ge(v_cache_done, upto(g, b, 1, 1))
                        start_gather(g2, b2)
                    values(range(1))
                    for h in range(G):
                        normalise(g, b, h)
                    values(range(1, LC))
                    if more:
                        query_scale(g1, b1)
                        key_scale(g1, b1)
                        rotate_k(g1, b1)
                    keys(range(2))
                    if more2:
                        rotate_q(g2, b2)
                    keys(range(2, LC))

            with pool.Fori(0, HK - 1) as g:
                group(g, False)
            group(HK - 1, True)

        @block.scalar
        def _(act):
            for j, t in ((0, sin_t), (1, cos_t)):
                act.wait_ge(angles_ready, j + 1)
                act.activation(t, t, ACT.Sin).then_inc(sincos_ready, 1)
            for b in range(B):
                act.wait_ge(xT_in_psum, b + 1)
                act.activation(xT_hi[:, :, b * S:(b + 1) * S], bank(b).rearrange("p (c s) -> p c s", c=DC), ACT.Copy).then_inc(xT_hi_done, 1)

            def hi(out, src, ready, count, done):
                act.wait_ge(ready, count)
                act.activation(out, src, ACT.Copy).then_inc(done, 1)

            def qkv_group(g, n):
                out = wqT_hi[:, n, :] if n < DC else wkvT_hi[:, 2 * (n - DC):2 * (n - DC) + 2, :].rearrange("p c e -> p (c e)")
                hi(out, bank(WEIGHT_BANKS[n % 2]), wqkv_in_psum, g * QKV_GROUPS + n + 1, wqkv_hi_done)

            def wo_group(g, n):
                hi(woT_hi[:, n, :], bank(WEIGHT_BANKS[(n + 1) % 2]), wo_in_psum, g * WO_GROUPS + n + 1, wo_hi_done)

            def cached_values(g, b):
                j = b % 2
                hi(v_hi[j][:, 0:LC, :], v_raw[j][:], v_loaded[j], g * (B // 2 * LC * 16) + (b // 2 + 1) * LC * 16, v_hi_done)

            def cached_keys(g, b):
                hi(kT_hi[:, 0:L], bank(A_BANK), kc_in_psum, upto(g, b, 1, 1), kc_hi_done)

            def new_kv(g, b):
                j = b % 2
                act.wait_ge(kv_in_psum, upto(g, b, 1, 1))
                act.activation(square[:, G, :], bank(KV_BANK, D), ACT.Square, accum_out=sumsq[j][:, G:G + 1])
                act.activation(v_hi[j][:, LC, :], bank(KV_BANK)[:, D:2 * D], ACT.Copy).then_inc(kv_read, 1)

            def squares(g, b):
                j = b % 2
                act.wait_ge(q_turned, upto(g, b, 1, 1))
                for h in range(G):
                    ins = act.activation(square[:, h, :], bank(Q_BANK)[:, h * D:(h + 1) * D], ACT.Square, accum_out=sumsq[j][:, h:h + 1])
                ins.then_inc(q_squared, 1)

            def exps(g, b, h):
                act.wait_ge(scores_done, upto(g, b, G, h + 1))
                act.activation(probs[:, h, :], scores[h % 2][:], ACT.Exp, bias=neg_max[:, h:h + 1], scale=-1.0,
                               accum_out=row_sum[:, h:h + 1]).then_inc(exp_done, 1)

            def probs_T(g, b, c):
                if c >= 3:
                    act.wait_ge(pv_done, upto(g, b, KC, c - 2))
                hi(pT_hi[c % 3][:], bank([B_BANK, A_BANK][c % 2]), pT_in_psum, upto(g, b, KC, c + 1), pT_hi_done)

            def new_keys(g, b):
                hi(kT_hi[:, L:KEYS], bank(KV_BANK, S), kn_in_psum, upto(g, b, 1, 1), kn_hi_done)

            def queries(g, b):
                hi(qT_hi[b % 2][:], bank(Q_BANK), qT_in_psum, upto(g, b, 1, 1), qT_hi_done)

            for n in range(QKV_GROUPS):
                qkv_group(0, n)
            squares(0, 0)
            queries(0, 0)
            cached_keys(0, 0)
            new_kv(0, 0)
            cached_values(0, 0)
            new_keys(0, 0)

            def group(g, last):
                for b in range(B):
                    g1, b1 = following(g, b)
                    more = not (last and b == B - 1)

                    def weights(slot):
                        for n in weight_groups(b, slot, last):
                            if b < 2:
                                wo_group(g, n)
                            else:
                                qkv_group(g + 1, n)

                    if more:
                        squares(g1, b1)
                    weights(0)
                    exps(g, b, 0)
                    if more:
                        queries(g1, b1)
                    exps(g, b, 1)
                    weights(1)
                    weights(2)
                    exps(g, b, 2)
                    exps(g, b, 3)
                    weights(3)
                    weights(4)
                    if more:
                        cached_keys(g1, b1)
                    probs_T(g, b, 0)
                    probs_T(g, b, 1)
                    if more:
                        cached_values(g1, b1)
                        new_kv(g1, b1)
                    probs_T(g, b, 2)
                    probs_T(g, b, 3)
                    probs_T(g, b, 4)
                    if more:
                        new_keys(g1, b1)
                    hi(oT_hi[:], bank(O_BANK), pv_done, upto(g, b, KC, KC), oT_hi_done)

            group(0, False)
            with act.Fori(1, HK - 1) as g:
                group(g, False)
            group(HK - 1, True)

        @block.vector
        def _(dve):
            steps = [0]

            def link(ins):
                steps[0] += 1
                ins.then_inc(table_step, 1)
                dve.wait_ge(table_step, steps[0])

            dve.memset(neg_max[:], 0.0).then_inc(y_bank_free, 1)
            dve.wait_ge(small_loaded, 16 * 5)
            dve.wait_ge(iota_done, 5)
            dve.tensor_copy(seq_f[:], seq_i[:])
            dve.tensor_copy(key_no, key_no_i)
            dve.tensor_scalar(qw_sb, qw_sb, -1.0, None, ALU.mult)
            dve.tensor_scalar(kw_sb, kw_sb, float(np.sqrt(D)), None, ALU.mult)
            link(dve.tensor_copy(tok_f[:], tok_i[:]))
            for j in range(4):
                q = slice(PSIZE * j, PSIZE * j + PSIZE)
                link(dve.tensor_scalar(in_page_f[q, :], tok_f[q, :], float(-PSIZE * j), float(HK), ALU.add, ALU.mult))
                dve.tensor_scalar(key_row[q, :], table_sb[q, :].rearrange("p (n j) -> p n j", j=4)[:, :, j],
                                  float(PSIZE * HK), in_page_f[q, 0:1], ALU.mult, ALU.add).then_inc(rows_ready, 1)
            link(dve.tensor_scalar(seq_f[:], seq_f[:], tok_f[:, 0:1], None, ALU.add))
            angle3 = angle.rearrange("p (b f) -> p b f", b=B)
            link(dve.tensor_tensor(angle3, seq_f[:].unsqueeze(2).broadcast_to([P, B, HALF]),
                                   invf_sb.unsqueeze(1).broadcast_to([P, B, HALF]), ALU.mult))
            link(dve.tensor_scalar(turns, angle, 1.0 / TWO_PI, ROUND, ALU.mult, ALU.add))
            link(dve.tensor_scalar(turns, turns, -ROUND, None, ALU.add))
            for part in (PI_A, PI_B, PI_C):
                link(dve.scalar_tensor_tensor(out=angle, in0=turns, scalar=-part, in1=angle, op0=ALU.mult, op1=ALU.add))
            dve.tensor_scalar(sin_t, angle, PI_F32, -PI_F32, ALU.min, ALU.max).then_inc(angles_ready, 1)
            link(dve.scalar_tensor_tensor(out=cos_t, in0=angle, scalar=-1.0, in1=angle, op0=ALU.mult, op1=ALU.max))
            dve.tensor_scalar(cos_t, cos_t, -1.0, float(np.pi / 2), ALU.mult, ALU.add).then_inc(angles_ready, 1)
            link(dve.tensor_scalar(seq_f[:], seq_f[:], tok_f[:, 0:1], None, ALU.subtract))
            for b in range(B):
                dve.tensor_scalar(mask[:, b, 0:L], key_no, seq_f[:, b:b + 1], MASKED, ALU.is_ge, ALU.mult)
            dve.wait_ge(sincos_ready, 2)
            for t, c_out, s_out in ((qw_sb, q_cos, q_sin), (kw_sb, k_cos, k_sin)):
                for half in range(2):
                    f = slice(half * HALF, (half + 1) * HALF)
                    wb = t[:, f].unsqueeze(1).broadcast_to([P, B, HALF])
                    dve.tensor_tensor(c_out[:, :, f], cos_t.rearrange("p (b f) -> p b f", b=B), wb, ALU.mult)
                    ins = dve.tensor_tensor(s_out[:, :, f], sin_t.rearrange("p (b f) -> p b f", b=B), wb, ALU.mult)
            ins.then_inc(tables_ready, 1)
            dve.wait_ge(tables_ready, 1)

            def lo(out, src, hi_part, hi_done, count, done):
                dve.wait_ge(hi_done, count)
                dve.tensor_tensor(out, src, hi_part.bitcast(F32), ALU.subtract).then_inc(done, 1)

            for b in range(B):
                at = slice(b * S, (b + 1) * S)
                lo(xT_lo[:, :, at], bank(b).rearrange("p (c s) -> p c s", c=DC), xT_hi[:, :, at], xT_hi_done, b + 1, xT_done)

            def qkv_group(g, n):
                flat = lambda t: t[:, 2 * (n - DC):2 * (n - DC) + 2, :].rearrange("p c e -> p (c e)")
                out, h = (wqT_lo[:, n, :], wqT_hi[:, n, :]) if n < DC else (flat(wkvT_lo), flat(wkvT_hi))
                lo(out, bank(WEIGHT_BANKS[n % 2]), h, wqkv_hi_done, g * QKV_GROUPS + n + 1, wqkv_done)

            def wo_group(g, n):
                lo(woT_lo[:, n, :], bank(WEIGHT_BANKS[(n + 1) % 2]), woT_hi[:, n, :], wo_hi_done, g * WO_GROUPS + n + 1, wo_done)

            def cached_values(g, b):
                j = b % 2
                lo(v_lo[j][:, 0:LC, :], v_raw[j][:], v_hi[j][:, 0:LC, :], v_hi_done, upto(g, b, 1, 1), v_cache_done)

            def cached_keys(g, b):
                lo(kT_lo[:, 0:L], bank(A_BANK), kT_hi[:, 0:L], kc_hi_done, upto(g, b, 1, 1), kc_done)

            def turn_q(g, b, part):
                q3 = bank(Q_BANK).rearrange("p (h d) -> p h d", h=G)
                if part == 0:
                    dve.wait_ge(q_in_psum, upto(g, b, 1, 1))
                    dve.tensor_tensor(u_q[:], q3, q_cos[:, b:b + 1, :].broadcast_to([P, G, D]), ALU.mult)
                else:
                    dve.tensor_tensor(w_q[:], q3, q_sin[:, b:b + 1, :].broadcast_to([P, G, D]), ALU.mult).then_inc(q_turned, 1)

            def new_kv(g, b):
                j = b % 2
                scale = inv_rms[j][:, G:G + 1]
                dve.wait_ge(kv_read, upto(g, b, 1, 1))
                dve.tensor_tensor(v_lo[j][:, LC, :], bank(KV_BANK)[:, D:2 * D], v_hi[j][:, LC, :].bitcast(F32), ALU.subtract).then_inc(v_new_done, 1)
                dve.wait_ge(k_scale_ready, upto(g, b, 2, 2))
                dve.scalar_tensor_tensor(out=u_k[:], in0=bank(KV_BANK, D), scalar=scale, in1=k_cos[:, b, :], op0=ALU.mult, op1=ALU.mult)
                dve.scalar_tensor_tensor(out=w_k[:], in0=bank(KV_BANK, D), scalar=scale, in1=k_sin[:, b, :],
                                         op0=ALU.mult, op1=ALU.mult).then_inc(k_turned, 1)

            def mask_and_max(g, b, h):
                if h >= 2:
                    dve.wait_ge(exp_done, upto(g, b, G, h - 1))
                dve.wait_ge(scores_in_psum, upto(g, b, G, h + 1))
                wait_apart(dve, scale_ready, upto(g, b, 2, 2), dve_passed)
                dve.tensor_tensor_reduce(out=scores[h % 2][:], in0=slot(h), in1=mask[:, b, :],
                                         scale=inv_rms[b % 2][:, h:h + 1], scalar=3.0e38, op0=ALU.add, op1=ALU.min,
                                         accum_out=neg_max[:, h:h + 1]).then_inc(scores_done, 1)

            def inverse(g, b, h):
                dve.wait_ge(exp_done, upto(g, b, G, h + 1))
                dve.reciprocal(row_inv[:, h:h + 1], row_sum[:, h:h + 1]).then_inc(inv_done, 1)

            def add_y(g, b):
                at = (b - 1) % B
                dve.wait_ge(y_in_psum, upto(g, b, 1))
                dve.tensor_tensor(xres[:, at, :], bank(KV_BANK), xres[:, at, :], ALU.add).then_inc(y_bank_free, 1)

            def probs_T(g, b, c):
                lo(pT_lo[c % 3][:], bank([B_BANK, A_BANK][c % 2]), pT_hi[c % 3][:], pT_hi_done, upto(g, b, KC, c + 1), pT_done)

            def new_keys(g, b):
                lo(kT_lo[:, L:KEYS], bank(KV_BANK, S), kT_hi[:, L:KEYS], kn_hi_done, upto(g, b, 1, 1), kn_done)

            def queries(g, b):
                lo(qT_lo[b % 2][:], bank(Q_BANK), qT_hi[b % 2][:], qT_hi_done, upto(g, b, 1, 1), qT_done)

            for n in range(QKV_GROUPS):
                qkv_group(0, n)
            turn_q(0, 0, 0)
            turn_q(0, 0, 1)
            queries(0, 0)
            cached_keys(0, 0)
            new_kv(0, 0)
            cached_values(0, 0)
            turn_q(0, 1, 0)
            turn_q(0, 1, 1)
            new_keys(0, 0)

            def group(g, first, last):
                for b in range(B):
                    g1, b1 = following(g, b)
                    more, more2 = not (last and b == B - 1), not (last and b >= B - 2)

                    def weights(slot):
                        for n in weight_groups(b, slot, last):
                            if b < 2:
                                wo_group(g, n)
                            else:
                                qkv_group(g + 1, n)

                    mask_and_max(g, b, 0)
                    weights(0)
                    mask_and_max(g, b, 1)
                    inverse(g, b, 0)
                    if more:
                        queries(g1, b1)
                    inverse(g, b, 1)
                    weights(1)
                    weights(2)
                    mask_and_max(g, b, 2)
                    mask_and_max(g, b, 3)
                    inverse(g, b, 2)
                    inverse(g, b, 3)
                    weights(3)
                    if not (first and b == 0):
                        add_y(g, b)
                    weights(4)
                    if more:
                        cached_keys(g1, b1)
                    probs_T(g, b, 0)
                    probs_T(g, b, 1)
                    if more:
                        cached_values(g1, b1)
                    probs_T(g, b, 2)
                    if more:
                        new_kv(g1, b1)
                    probs_T(g, b, 3)
                    probs_T(g, b, 4)
                    if more2:
                        turn_q(*following(g1, b1), 0)
                        turn_q(*following(g1, b1), 1)
                    if more:
                        new_keys(g1, b1)
                    lo(oT_lo[:], bank(O_BANK), oT_hi[:], oT_hi_done, upto(g, b, 1, 1), oT_done)

            group(0, True, False)
            with dve.Fori(1, HK - 1) as g:
                group(g, False, False)
            group(HK - 1, False, True)
            add_y(HK, 0)

        @block.tensor
        def _(pe):
            pe.wait_ge(ident_step, 2)
            pe.wait_ge(x_loaded, 16)
            for b in range(B):
                for c in range(DC):
                    ins = pe.transpose(bank(b)[:, c * S:(c + 1) * S], xres[:, b, c * P:(c + 1) * P], ident[:])
                ins.then_inc(xT_in_psum, 1)
            pe.wait_ge(xT_done, B)

            def qkv_group(g, n):
                if n == 0:
                    pe.wait_ge(wqkv_loaded, g * 48 + 48)
                if n >= 2:
                    pe.wait_ge(wqkv_done, g * QKV_GROUPS + n - 1)
                out = bank(WEIGHT_BANKS[n % 2])
                if n < DC:
                    for e in range(G):
                        ins = pe.transpose(out[:, e * D:(e + 1) * D], wq_raw[:, e, n * P:(n + 1) * P], ident[:])
                else:
                    for m in range(4):
                        c = 2 * (n - DC) + m // 2
                        ins = pe.transpose(out[:, m * D:(m + 1) * D], wkv_raw[:, m % 2, c * P:(c + 1) * P], ident[:])
                ins.then_inc(wqkv_in_psum, 1)

            def wo_group(g, n):
                if n == 0:
                    pe.wait_ge(wo_loaded, g * 16 + 16)
                if n >= 2:
                    pe.wait_ge(wo_done, g * WO_GROUPS + n - 1)
                for c in range(DC):
                    ins = pe.transpose(bank(WEIGHT_BANKS[(n + 1) % 2])[:, c * P:(c + 1) * P], wo_raw[:, c, n * D:(n + 1) * D], ident[:])
                ins.then_inc(wo_in_psum, 1)

            def cached_keys(g, b):
                j = b % 2
                pe.wait_ge(k_loaded[j], g * (B // 2 * LC * 16) + (b // 2 + 1) * LC * 16)
                for c in range(LC):
                    ins = pe.transpose(bank(A_BANK)[:, c * P:(c + 1) * P], k_raw[j][:, c, :], ident[:])
                ins.then_inc(kc_in_psum, 1)

            def project_q(g, b, cs, first=False):
                at = slice(b * S, (b + 1) * S)
                if cs[0] == 0 and not first:
                    pe.wait_ge(qT_done, upto(g, b, 1))
                if cs[0] == 0 and b == 0:
                    pe.wait_ge(wqkv_done, g * QKV_GROUPS + DC)
                for c in cs:
                    ins = three_pass(pe, bank(Q_BANK), xT_hi[:, c, at], xT_lo[:, c, at], wqT_hi[:, c, :], wqT_lo[:, c, :], c == 0, c == DC - 1)
                if c == DC - 1:
                    ins.then_inc(q_in_psum, 1)

            def project_kv(g, b, first=False):
                at = slice(b * S, (b + 1) * S)
                if not first:
                    pe.wait_ge(y_bank_free, upto(g, b, 1))
                if b == 0:
                    pe.wait_ge(wqkv_done, g * QKV_GROUPS + QKV_GROUPS)
                for c in range(DC):
                    ins = three_pass(pe, bank(KV_BANK, 2 * D), xT_hi[:, c, at], xT_lo[:, c, at], wkvT_hi[:, c, :], wkvT_lo[:, c, :], c == 0, c == DC - 1)
                ins.then_inc(kv_in_psum, 1)

            def new_keys(g, b):
                pe.wait_ge(k_rot_done, upto(g, b, 1, 1))
                pe.wait_ge(v_new_done, upto(g, b, 1, 1))
                pe.transpose(bank(KV_BANK, S), k_rot[:], ident[:]).then_inc(kn_in_psum, 1)

            def queries(g, b):
                pe.wait_ge(q_rot_done, upto(g, b, 1, 1))
                pe.wait_ge(q_squared, upto(g, b, 1, 1))
                for h in range(G):
                    ins = pe.transpose(bank(Q_BANK)[:, h * S:(h + 1) * S], q_rot[:, h, :], ident[:])
                ins.then_inc(qT_in_psum, 1)

            def score(g, b, h, first):
                if h == 0:
                    pe.wait_ge(kc_done, upto(g, b, 1, 1))
                    pe.wait_ge(qT_done, upto(g, b, 1, 1))
                if h >= 2:
                    pe.wait_ge(scores_done, upto(g, b, G, h - 1))
                q = slice(h * S, (h + 1) * S)
                qh, ql = qT_hi[b % 2], qT_lo[b % 2]
                for part, k in enumerate(slice(*p) for p in SCORE_PARTS):
                    if part == 1 and h == 0:
                        pe.wait_ge(kn_done, upto(g, b, 1, 1))
                    if part == 1 and h == 1 and not (first and b == 0):
                        pe.wait_ge(oT_done, upto(g, b, 1))
                    ins = three_pass(pe, slot(h)[:, k], qh[:, q], ql[:, q], kT_hi[:, k], kT_lo[:, k], True, True)
                ins.then_inc(scores_in_psum, 1)

            def probs_T(g, b, c):
                if c == 0:
                    pe.wait_ge(probs_done, upto(g, b, G, G))
                if c >= 2:
                    pe.wait_ge(pT_done, upto(g, b, KC, c - 1))
                for h in range(G):
                    ins = pe.transpose(bank([B_BANK, A_BANK][c % 2])[:, h * S:(h + 1) * S], probs[:, h, c * P:(c + 1) * P], ident[:])
                ins.then_inc(pT_in_psum, 1)

            def times_v(g, b, c):
                j = b % 2
                if c == 0:
                    pe.wait_ge(v_cache_done, upto(g, b, 1, 1))
                pe.wait_ge(pT_done, upto(g, b, KC, c + 1))
                three_pass(pe, bank(O_BANK), v_hi[j][:, c, :], v_lo[j][:, c, :], pT_hi[c % 3][:], pT_lo[c % 3][:], c == 0, c == KC - 1).then_inc(pv_done, 1)

            def output(g, b, hs):
                if hs[0] == 0:
                    pe.wait_ge(oT_done, upto(g, b, 1))
                for h in hs:
                    if b == 1:
                        pe.wait_ge(wo_done, g * WO_GROUPS + h + 1)
                    q = slice(h * S, (h + 1) * S)
                    ins = three_pass(pe, bank(KV_BANK), oT_hi[:, q], oT_lo[:, q], woT_hi[:, h, :], woT_lo[:, h, :], h == 0, h == G - 1)
                if h == G - 1:
                    ins.then_inc(y_in_psum, 1)

            for n in range(QKV_GROUPS):
                qkv_group(0, n)
            project_q(0, 0, range(DC), first=True)
            pe.wait_ge(wqkv_done, QKV_GROUPS)
            cached_keys(0, 0)
            project_kv(0, 0, first=True)
            queries(0, 0)
            project_q(0, 1, range(DC))
            new_keys(0, 0)

            def group(g, first, last):
                for b in range(B):
                    g1, b1 = following(g, b)
                    more, more2 = not (last and b == B - 1), not (last and b >= B - 2)

                    def weights(slot):
                        for n in weight_groups(b, slot, last):
                            if b < 2:
                                wo_group(g, n)
                            else:
                                qkv_group(g + 1, n)

                    def output_before(hs):
                        if not (first and b == 0):
                            output(g, b, hs)

                    def project_ahead(cs):
                        if more2:
                            project_q(*following(g1, b1), cs)

                    score(g, b, 0, first)
                    weights(0)
                    score(g, b, 1, first)
                    if more:
                        queries(g1, b1)
                    weights(1)
                    output_before(range(2))
                    weights(2)
                    score(g, b, 2, first)
                    score(g, b, 3, first)
                    weights(3)
                    output_before(range(2, G))
                    weights(4)
                    new_q = b == B - 2 and not last
                    if more:
                        if b == 1:
                            pe.wait_ge(wo_done, g * WO_GROUPS + WO_GROUPS)
                        if b >= B - 2 and not last:
                            pe.wait_ge(wqkv_done, (g + 1) * QKV_GROUPS + (DC - 1 if new_q else QKV_GROUPS - 1))
                        cached_keys(g1, b1)
                    if new_q:
                        project_kv(g1, b1)
                    else:
                        project_ahead(range(2))
                    if b == 0:
                        pe.wait_ge(wo_done, g * WO_GROUPS + 1)
                    if b >= B - 2 and not last:
                        pe.wait_ge(wqkv_done, (g + 1) * QKV_GROUPS + (DC if new_q else QKV_GROUPS))
                    probs_T(g, b, 0)
                    if more:
                        pe.wait_ge(kc_done, upto(g1, b1, 1, 1))
                    probs_T(g, b, 1)
                    if new_q:
                        project_ahead(range(2))
                    elif more:
                        project_kv(g1, b1)
                    times_v(g, b, 0)
                    probs_T(g, b, 2)
                    project_ahead(range(2, 3))
                    probs_T(g, b, 3)
                    times_v(g, b, 1)
                    probs_T(g, b, 4)
                    project_ahead(range(3, 4))
                    times_v(g, b, 2)
                    times_v(g, b, 3)
                    if more:
                        new_keys(g1, b1)
                    times_v(g, b, 4)

            group(0, True, False)
            with pe.Fori(1, HK - 1) as g:
                group(g, False, False)
            group(HK - 1, False, True)
            output(HK, 0, range(G))


def dense_signed(nc, x, w, bias, coeff, mask, x_out):
    with ExitStack() as ctx:
        def sb(name, shape, dt=F32):
            return ctx.enter_context(nc.sbuf_tensor("ds_" + name, shape, dt))

        def sem(name):
            return ctx.enter_context(nc.semaphore(name))

        ps = ctx.enter_context(nc.psum_tensor("ds_ps", [P, 8, NFREE], F32))
        X_BANK, OUT_BANK, W_BANK = 0, 2, 4

        ident = sb("ident", [P, P])
        w_raw = sb("w_raw", [P, DC, DM])
        wT = sb("wT", [P, DC, DM])
        bias_sb = sb("bias_sb", [P, DM])
        coeff_sb = sb("coeff_sb", [P, B])
        coeff2 = sb("coeff2", [P, B])
        neg_coeff = sb("neg_coeff", [P, B])
        x_raw = [sb(f"x_raw{j}", [P, DM]) for j in range(2)]
        x_bias = [sb(f"x_bias{j}", [P, DM]) for j in range(2)]
        mask_raw = [sb(f"mask_raw{j}", [P, DC, DM], I32) for j in range(2)]
        xT_hi = [sb(f"xT_hi{j}", [P, DC, S], F32R) for j in range(2)]
        xT_lo = [sb(f"xT_lo{j}", [P, DC, S], F32R) for j in range(2)]
        both = [sb(f"both{j}", [P, DC, DM]) for j in range(2)]
        m_hi = [sb(f"m_hi{j}", [P, DC, DM], F32R) for j in range(2)]
        m_lo = [sb(f"m_lo{j}", [P, DC, DM], F32R) for j in range(2)]
        result = sb("result", [P, B, DM])

        ident_step = sem("ds_ident_step")
        w_loaded = sem("ds_w_loaded")
        small_loaded = sem("ds_small_loaded")
        x_loaded = [sem(f"ds_x_loaded{j}") for j in range(2)]
        mask_loaded = [sem(f"ds_mask_loaded{j}") for j in range(2)]
        w_in_psum = sem("ds_w_in_psum")
        wT_done = sem("ds_wT_done")
        coeff_ready = sem("ds_coeff_ready")
        x_in_psum = sem("ds_x_in_psum")
        xT_hi_done = sem("ds_xT_hi_done")
        xT_done = sem("ds_xT_done")
        x_bias_done = sem("ds_x_bias_done")
        both_done = sem("ds_both_done")
        m_hi_done = sem("ds_m_hi_done")
        m_done = sem("ds_m_done")
        product_done = sem("ds_product_done")
        added = sem("ds_added")
        stored = sem("ds_stored")

        PAIRS = B // 2
        block = ctx.enter_context(nc.Block())

        @block.sync
        def _(sp):
            sp.dma_start(w_raw[:], w.rearrange("(c p) i -> p c i", p=P)).then_inc(w_loaded, 16)
            sp.dma_start(bias_sb[:], bias.rearrange("(o d) -> o d", o=1).broadcast_to([P, DM])).then_inc(small_loaded, 16)
            sp.dma_start(coeff_sb[:], coeff.rearrange("(o b) -> o b", o=1).broadcast_to([P, B])).then_inc(small_loaded, 16)

            def load_x(i, j):
                sp.dma_start(x_raw[j][:], x[bass.ds(i, 1)].rearrange("o s d -> (o s) d")).then_inc(x_loaded[j], 16)

            def load_mask(i, j):
                sp.dma_start(mask_raw[j][:], mask[bass.ds(i, 1)].rearrange("o (c p) n -> p (o c) n", p=P)).then_inc(mask_loaded[j], 16)

            for j in range(2):
                load_x(j, j)
                load_mask(j, j)
            with sp.Fori(0, PAIRS - 1) as p:
                for j in range(2):
                    sp.wait_ge(both_done, p * 2 + j + 1)
                    load_mask(p * 2 + j + 2, j)
                    sp.wait_ge(added, p * 2 + j + 1)
                    load_x(p * 2 + j + 2, j)
            for i in range(B):
                sp.wait_ge(added, i + 1)
                sp.dma_start(x_out[i], result[:, i, :]).then_inc(stored, 16)
            sp.wait_ge(stored, 16 * B)

        @block.gpsimd
        def _(pool):
            make_identity(nc, pool, ident[:], ident_step)
            pool.wait_ge(small_loaded, 32)
            pool.tensor_scalar(coeff2[:], coeff_sb[:], 2.0, None, ALU.mult).then_inc(coeff_ready, 1)
            pool.tensor_scalar(neg_coeff[:], coeff_sb[:], -1.0, None, ALU.mult).then_inc(coeff_ready, 1)
            with pool.Fori(0, PAIRS) as p:
                for j in range(2):
                    pool.wait_ge(x_loaded[j], p * 16 + 16)
                    pool.tensor_tensor(x_bias[j][:], x_raw[j][:], bias_sb[:], ALU.add).then_inc(x_bias_done, 1)

        @block.scalar
        def _(act):
            for c in range(DC):
                act.wait_ge(w_in_psum, c + 1)
                act.activation(wT[:, c, :], ps[:, W_BANK + c, :], ACT.Copy).then_inc(wT_done, 1)
            with act.Fori(0, PAIRS) as p:
                for j in range(2):
                    act.wait_ge(x_in_psum, p * 2 + j + 1)
                    act.activation(xT_hi[j][:].rearrange("p c s -> p (c s)"), ps[:, X_BANK + j, :], ACT.Copy).then_inc(xT_hi_done, 1)
                    act.wait_ge(both_done, p * 2 + j + 1)
                    act.activation(m_hi[j][:], both[j][:], ACT.Identity, bias=neg_coeff[:, bass.ds(p * 2 + j, 1)]).then_inc(m_hi_done, 1)

        @block.vector
        def _(dve):
            dve.wait_ge(coeff_ready, 2)
            dve.wait_ge(wT_done, DC)
            with dve.Fori(0, PAIRS) as p:
                for j in range(2):
                    at = bass.ds(p * 2 + j, 1)
                    dve.wait_ge(mask_loaded[j], p * 16 + 16)
                    dve.scalar_tensor_tensor(out=both[j][:].rearrange("p c n -> p (c n)"), in0=mask_raw[j][:].rearrange("p c n -> p (c n)"),
                                             scalar=coeff2[:, at], in1=wT[:].rearrange("p c n -> p (c n)"),
                                             op0=ALU.mult, op1=ALU.add).then_inc(both_done, 1)
                for j in range(2):
                    at = bass.ds(p * 2 + j, 1)
                    dve.wait_ge(xT_hi_done, p * 2 + j + 1)
                    dve.tensor_tensor(xT_lo[j][:].rearrange("p c s -> p (c s)"), ps[:, X_BANK + j, :],
                                      xT_hi[j][:].rearrange("p c s -> p (c s)").bitcast(F32), ALU.subtract).then_inc(xT_done, 1)
                    dve.wait_ge(m_hi_done, p * 2 + j + 1)
                    dve.scalar_tensor_tensor(out=m_lo[j][:].rearrange("p c n -> p (c n)"), in0=both[j][:].rearrange("p c n -> p (c n)"),
                                             scalar=neg_coeff[:, at], in1=m_hi[j][:].rearrange("p c n -> p (c n)").bitcast(F32),
                                             op0=ALU.add, op1=ALU.subtract).then_inc(m_done, 1)
                for j in range(2):
                    dve.wait_ge(product_done, p * 2 + j + 1)
                    dve.wait_ge(x_bias_done, p * 2 + j + 1)
                    dve.tensor_tensor(result[:, bass.ds(p * 2 + j, 1), :].rearrange("p o d -> p (o d)"), ps[:, OUT_BANK + j, :],
                                      x_bias[j][:], ALU.add).then_inc(added, 1)

        @block.tensor
        def _(pe):
            pe.wait_ge(ident_step, 2)
            pe.wait_ge(w_loaded, 16)
            for c in range(DC):
                for o in range(DC):
                    ins = pe.transpose(ps[:, W_BANK + c, o * P:(o + 1) * P], w_raw[:, o, c * P:(c + 1) * P], ident[:])
                ins.then_inc(w_in_psum, 1)
            with pe.Fori(0, PAIRS) as p:
                for j in range(2):
                    pe.wait_ge(x_loaded[j], p * 16 + 16)
                    for c in range(DC):
                        ins = pe.transpose(ps[:, X_BANK + j, c * S:(c + 1) * S], x_raw[j][:, c * P:(c + 1) * P], ident[:])
                    ins.then_inc(x_in_psum, 1)
                for j in range(2):
                    pe.wait_ge(xT_done, p * 2 + j + 1)
                    pe.wait_ge(m_done, p * 2 + j + 1)
                    for c in range(DC):
                        ins = three_pass(pe, ps[:, OUT_BANK + j, :], xT_hi[j][:, c, :], xT_lo[j][:, c, :],
                                         m_hi[j][:, c, :], m_lo[j][:, c, :], c == 0, c == DC - 1)
                    ins.then_inc(product_done, 1)


def swiglu(nc, x, w_gate, w_up, w_down, a_gate, b_gate, a_up, b_up, a_down, b_down, lora_idx, x_out):
    with ExitStack() as ctx:
        def sb(name, shape, dt=F32):
            return ctx.enter_context(nc.sbuf_tensor("sw_" + name, shape, dt))

        def sem(name):
            return ctx.enter_context(nc.semaphore("sw_" + name))

        ps = ctx.enter_context(nc.psum_tensor("sw_ps", [P, 8, NFREE], F32))
        ident = sb("ident", [P, P])
        gT_hi = sb("gT_hi", [P, DC, F], F32R)
        gT_lo = sb("gT_lo", [P, DC, F], F32R)
        uT_hi = sb("uT_hi", [P, DC, F], F32R)
        uT_lo = sb("uT_lo", [P, DC, F], F32R)
        dT_hi = sb("dT_hi", [P, FC, DM], F32R)
        dT_lo = sb("dT_lo", [P, FC, DM], F32R)
        ident_step = sem("ident_step")

        with ExitStack() as prep:
            raws = [prep.enter_context(nc.sbuf_tensor(f"sw_raw{m}", [P, FC, DM], F32)) for m in range(2)]
            down_raw = raws[0][:].rearrange("p c d -> p (c d)")[:, 0:DC * F].rearrange("p (c f) -> p c f", c=DC)
            raw_loaded = [sem(f"raw_loaded{m}") for m in range(3)]
            tile_in_psum = sem("tile_in_psum")
            tile_hi_done = sem("tile_hi_done")
            tile_done = sem("tile_done")
            tiles = [(m, c, n, k) for m in range(2) for c in range(DC) for n, k in FN] + [(2, c, 0, DM) for c in range(FC)]

            def place(t):
                m, c, n, k = tiles[t]
                rows = P if m < 2 or c < FC - 1 else FR
                hi, lo = ((gT_hi, gT_lo), (uT_hi, uT_lo), (dT_hi, dT_lo))[m]
                return hi[0:rows, c, n:n + k], lo[0:rows, c, n:n + k], ps[0:rows, t % 8, 0:k]

            block = prep.enter_context(nc.Block())

            @block.sync
            def _(sp):
                for m, w in enumerate((w_gate, w_up)):
                    sp.dma_start(raws[m][:, 0:FC - 1, :], w[0:(FC - 1) * P].rearrange("(c p) d -> p c d", p=P)).then_inc(raw_loaded[m], 16)
                    sp.dma_start(raws[m][0:FR, FC - 1, :], w[(FC - 1) * P:F]).then_inc(raw_loaded[m], 16)
                sp.wait_ge(tile_in_psum, DC * len(FN))
                sp.dma_start(down_raw, w_down.rearrange("(c p) f -> p c f", p=P)).then_inc(raw_loaded[2], 16)

            @block.gpsimd
            def _(pool):
                make_identity(nc, pool, ident[:], ident_step)

            @block.tensor
            def _(pe):
                pe.wait_ge(ident_step, 2)
                for t, (m, c, n, k) in enumerate(tiles):
                    if t % (DC * len(FN)) == 0:
                        pe.wait_ge(raw_loaded[m], 32 if m < 2 else 16) if t <= 2 * DC * len(FN) else None
                    if t >= 8:
                        pe.wait_ge(tile_done, t - 7)
                    for at in range(n, n + k, P):
                        cols = min(P, n + k - at)
                        if m < 2:
                            src = raws[m][0:cols, at // P, c * P:(c + 1) * P]
                            ins = pe.transpose(ps[:, t % 8, at - n:at - n + cols], src, ident[0:cols, 0:cols])
                        else:
                            rows = P if c < FC - 1 else FR
                            ins = pe.transpose(ps[0:rows, t % 8, at:at + P], down_raw[:, at // P, c * P:c * P + rows], ident[:])
                    ins.then_inc(tile_in_psum, 1)

            @block.scalar
            def _(act):
                for t in range(len(tiles)):
                    hi, _, src = place(t)
                    act.wait_ge(tile_in_psum, t + 1)
                    act.activation(hi, src, ACT.Copy).then_inc(tile_hi_done, 1)

            @block.vector
            def _(dve):
                for t in range(len(tiles)):
                    hi, lo, src = place(t)
                    dve.wait_ge(tile_hi_done, t + 1)
                    dve.tensor_tensor(lo, src, hi.bitcast(F32), ALU.subtract).then_inc(tile_done, 1)

        FPAD = FC * P
        x_next = sb("x_next", [P, DM])
        x_res = sb("x_res", [P, DM])
        xT_hi = sb("xT_hi", [P, DC, S], F32R)
        xT_lo = sb("xT_lo", [P, DC, S], F32R)
        silu = sb("silu", [P, F])
        act_t = sb("act_t", [P, FPAD])
        actT_hi = sb("actT_hi", [P, FC, S], F32R)
        actT_lo = sb("actT_lo", [P, FC, S], F32R)
        R2 = UP0 + RANK
        agu_raw = sb("agu_raw", [R2, DM])
        bgu_raw = sb("bgu_raw", [P, FC, R2])
        ad_raw = sb("ad_raw", [RANK, FPAD])
        bd_raw = sb("bd_raw", [P, DC, RANK])
        aguT_hi = sb("aguT_hi", [P, DC, R2], F32R)
        aguT_lo = sb("aguT_lo", [P, DC, R2], F32R)
        bguT_hi = sb("bguT_hi", [R2, F], F32R)
        bguT_lo = sb("bguT_lo", [R2, F], F32R)
        adT_hi = sb("adT_hi", [P, FC, RANK], F32R)
        adT_lo = sb("adT_lo", [P, FC, RANK], F32R)
        bdT_hi = sb("bdT_hi", [RANK, DM], F32R)
        bdT_lo = sb("bdT_lo", [RANK, DM], F32R)
        tgu_hi = sb("tgu_hi", [R2, S], F32R)
        tgu_lo = sb("tgu_lo", [R2, S], F32R)
        td_hi = sb("td_hi", [RANK, S], F32R)
        td_lo = sb("td_lo", [RANK, S], F32R)

        zeroed = sem("zeroed")
        x_loaded = sem("x_loaded")
        lora_loaded = sem("lora_loaded")
        res_loaded = sem("res_loaded")
        in_psum = sem("in_psum")
        hi_done = sem("hi_done")
        out_done = sem("out_done")
        gu_in_psum = sem("gu_in_psum")
        silu_done = sem("silu_done")
        act_done = sem("act_done")
        down_in_psum = sem("down_in_psum")
        pe_passed = sem("pe_passed")
        added = sem("added")
        stored = sem("stored")

        ACT0, ACT1, X, AGU, BGU0, BGU1, BGU2, TGU, ACT2, TD, AD, BD = range(12)
        AHEAD = [X, AGU, BGU0, BGU1, BGU2, TGU, AD, BD]
        TURN = list(range(12))
        LAST = [ACT0, ACT1, ACT2, TD]
        NA, NT = len(AHEAD), len(TURN)
        BANKS = [4, 5, 7]
        DOWN_BANK = 6

        def number(i, step, turn):
            return (NA + i * NT if turn is not AHEAD else 0) + turn.index(step)

        def step_bank(step, turn):
            first = 0 if turn is not AHEAD else 1
            return BANKS[(first + turn.index(step)) % 3]

        def leaving(step, turn):
            bk = ps[:, step_bank(step, turn), :]
            if step in (ACT0, ACT1, ACT2):
                n = [ACT0, ACT1, ACT2].index(step)
                cs = slice(4 * n, min(4 * n + 4, FC))
                k = (cs.stop - cs.start) * S
                flat = lambda t: t[:, cs, :].rearrange("p c s -> p (c s)")
                return bk[:, 0:k], flat(actT_hi), flat(actT_lo), 1.0
            if step == X:
                return bk, xT_hi[:].rearrange("p c s -> p (c s)"), xT_lo[:].rearrange("p c s -> p (c s)"), 1.0
            if step == AGU:
                return bk[:, 0:DC * R2], aguT_hi[:].rearrange("p c r -> p (c r)"), aguT_lo[:].rearrange("p c r -> p (c r)"), 1.0
            if step in (BGU0, BGU1, BGU2):
                n, k = FN[step - BGU0]
                return bk[0:R2, 0:k], bguT_hi[:, n:n + k], bguT_lo[:, n:n + k], 1.0
            if step == TGU:
                return bk[0:R2, 0:S], tgu_hi[:], tgu_lo[:], LORA_SCALE
            if step == TD:
                return bk[0:RANK, 0:S], td_hi[:], td_lo[:], LORA_SCALE
            if step == AD:
                return bk[:, 0:FC * RANK], adT_hi[:].rearrange("p c r -> p (c r)"), adT_lo[:].rearrange("p c r -> p (c r)"), 1.0
            return bk[0:RANK, :], bdT_hi[:], bdT_lo[:], 1.0

        block = ctx.enter_context(nc.Block())

        @block.sync
        def _(sp):
            def load_next(i):
                sp.dma_start(x_next[:], x[bass.ds(i, 1)].rearrange("o s d -> (o s) d")).then_inc(x_loaded, 16)
                r = sp.value_load(lora_idx.rearrange("(o b) -> o b", o=1)[:, bass.ds(i, 1)], min_val=0, max_val=15)
                for a, b_, at in ((a_gate, b_gate, 0), (a_up, b_up, UP0)):
                    sp.dma_start(agu_raw[at:at + RANK, :], a[0, bass.ds(r, 1)].rearrange("o r d -> (o r) d")).then_inc(lora_loaded, 16)
                    bb = b_[0, bass.ds(r, 1)].rearrange("o f r -> (o f) r")
                    sp.dma_start(bgu_raw[:, 0:FC - 1, at:at + RANK], bb[0:(FC - 1) * P].rearrange("(c p) r -> p c r", p=P)).then_inc(lora_loaded, 16)
                    sp.dma_start(bgu_raw[0:FR, FC - 1, at:at + RANK], bb[(FC - 1) * P:F]).then_inc(lora_loaded, 16)
                sp.dma_start(ad_raw[:, 0:F], a_down[0, bass.ds(r, 1)].rearrange("o r f -> (o r) f")).then_inc(lora_loaded, 16)
                sp.dma_start(bd_raw[:], b_down[0, bass.ds(r, 1)].rearrange("o (c p) r -> p (o c) r", p=P)).then_inc(lora_loaded, 16)

            def load_res(i):
                sp.dma_start(x_res[:], x[bass.ds(i, 1)].rearrange("o s d -> (o s) d")).then_inc(res_loaded, 16)

            def store(i):
                sp.wait_ge(added, i + 1)
                sp.dma_start(x_out[bass.ds(i, 1)].rearrange("o s d -> (o s) d"), x_res[:]).then_inc(stored, 16)
                sp.wait_ge(stored, i * 16 + 16)

            sp.wait_ge(zeroed, 3)
            load_next(0)
            load_res(0)
            with sp.Fori(0, B - 1) as i:
                sp.wait_ge(in_psum, NA + i * NT)
                load_next(i + 1)
                store(i)
                load_res(i + 1)
            store(B - 1)

        @block.gpsimd
        def _(pool):
            pool.memset(agu_raw[:], 0.0).then_inc(zeroed, 1)
            pool.memset(bgu_raw[:], 0.0).then_inc(zeroed, 1)
            pool.memset(ad_raw[:], 0.0).then_inc(zeroed, 1)
            pool.memset(act_t[:, F:FPAD], 0.0).then_inc(zeroed, 1)

        @block.scalar
        def _(act):
            def hi(i, step, turn):
                src, out, _, scale = leaving(step, turn)
                act.wait_ge(in_psum, number(i, step, turn) + 1)
                act.activation(out, src, ACT.Copy, scale=scale).then_inc(hi_done, 1)

            def silu_of(i, n):
                at, k = FN[n]
                act.wait_ge(gu_in_psum, i * len(FN) + n + 1)
                act.activation(silu[:, at:at + k], ps[:, 2 * (n % 2), 0:k], ACT.Silu).then_inc(silu_done, 1)

            def batch(i, turn):
                silu_of(i, 0)
                silu_of(i, 1)
                hi(i, ACT0, turn)
                silu_of(i, 2)
                for step in turn[1:]:
                    hi(i, step, turn)

            for step in AHEAD:
                hi(0, step, AHEAD)
            with act.Fori(0, B - 1) as i:
                batch(i, TURN)
            batch(B - 1, LAST)

        @block.vector
        def _(dve):
            def lo(i, step, turn):
                src, h, out, scale = leaving(step, turn)
                dve.wait_ge(hi_done, number(i, step, turn) + 1)
                dve.scalar_tensor_tensor(out=out, in0=src, scalar=scale, in1=h.bitcast(F32), op0=ALU.mult, op1=ALU.subtract).then_inc(out_done, 1)

            def times_up(i, n):
                at, k = FN[n]
                dve.wait_ge(silu_done, i * len(FN) + n + 1)
                dve.tensor_tensor(act_t[:, at:at + k], ps[:, 2 * (n % 2) + 1, 0:k], silu[:, at:at + k], ALU.mult).then_inc(act_done, 1)

            def batch(i, turn):
                times_up(i, 0)
                times_up(i, 1)
                lo(i, ACT0, turn)
                times_up(i, 2)
                for step in turn[1:]:
                    if step != BD:
                        lo(i, step, turn)
                dve.wait_ge(down_in_psum, i + 1)
                dve.wait_ge(res_loaded, i * 16 + 16)
                dve.tensor_tensor(x_res[:], ps[:, DOWN_BANK, :], x_res[:], ALU.add).then_inc(added, 1)
                if BD in turn:
                    lo(i, BD, turn)

            dve.wait_ge(zeroed, 4)
            for step in AHEAD:
                lo(0, step, AHEAD)
            with dve.Fori(0, B - 1) as i:
                batch(i, TURN)
            batch(B - 1, LAST)

        @block.tensor
        def _(pe):

            def parts_done(i, step, turn):
                pe.wait_ge(out_done, number(i, step, turn) + 1)

            def free_bank(i, step, turn):
                if turn is not AHEAD or turn.index(step) >= 3:
                    wait_apart(pe, out_done, number(i, step, turn) - 2, pe_passed)

            def act_transposed(i, step, turn):
                n = [ACT0, ACT1, ACT2].index(step)
                pe.wait_ge(act_done, i * len(FN) + n + 1)
                free_bank(i, step, turn)
                bk = ps[:, step_bank(step, turn), :]
                for c in range(4 * n, min(4 * n + 4, FC)):
                    ins = pe.transpose(bk[:, (c - 4 * n) * S:(c - 4 * n + 1) * S], act_t[:, c * P:(c + 1) * P], ident[:])
                ins.then_inc(in_psum, 1)

            def next_transposed(i, step, turn, loaded):
                if step == X:
                    pe.wait_ge(x_loaded, loaded * 16 + 16)
                if step == AGU:
                    pe.wait_ge(lora_loaded, loaded * 128 + 128)
                free_bank(i, step, turn)
                bk = ps[:, step_bank(step, turn), :]
                if step == X:
                    for c in range(DC):
                        ins = pe.transpose(bk[:, c * S:(c + 1) * S], x_next[:, c * P:(c + 1) * P], ident[:])
                elif step == AGU:
                    for c in range(DC):
                        ins = pe.transpose(bk[:, c * R2:(c + 1) * R2], agu_raw[:, c * P:(c + 1) * P], ident[0:R2, 0:R2])
                elif step in (BGU0, BGU1, BGU2):
                    n, k = FN[step - BGU0]
                    for at in range(n, n + k, P):
                        rows = min(P, F - at)
                        ins = pe.transpose(bk[0:R2, at - n:at - n + rows], bgu_raw[0:rows, at // P, :], ident[0:rows, 0:rows])
                elif step == AD:
                    for c in range(FC):
                        ins = pe.transpose(bk[:, c * RANK:(c + 1) * RANK], ad_raw[:, c * P:(c + 1) * P], ident[0:RANK, 0:RANK])
                else:
                    for c in range(DC):
                        ins = pe.transpose(bk[0:RANK, c * P:(c + 1) * P], bd_raw[:, c, :], ident[:])
                ins.then_inc(in_psum, 1)

            def into_ranks(i, turn):
                parts_done(i, AGU, turn)
                free_bank(i, TGU, turn)
                for c in range(DC):
                    ins = three_pass(pe, ps[0:R2, step_bank(TGU, turn), 0:S], aguT_hi[:, c, :], aguT_lo[:, c, :],
                                     xT_hi[:, c, :], xT_lo[:, c, :], c == 0, c == DC - 1)
                ins.then_inc(in_psum, 1)

            def gate_up(i, n):
                at, k = FN[n]
                cols = slice(at, at + k)
                if n == 2:
                    pe.wait_ge(act_done, i * len(FN) + 1)
                for m, (wh, wl, r0) in enumerate(((gT_hi, gT_lo, 0), (uT_hi, uT_lo, UP0))):
                    out = ps[:, 2 * (n % 2) + m, 0:k]
                    for c in range(DC):
                        three_pass(pe, out, xT_hi[:, c, :], xT_lo[:, c, :], wh[:, c, cols], wl[:, c, cols], c == 0, False)
                    r = slice(r0, r0 + RANK)
                    ins = three_pass(pe, out, tgu_hi[r, :], tgu_lo[r, :], bguT_hi[r, cols], bguT_lo[r, cols], False, True)
                ins.then_inc(gu_in_psum, 1)

            def batch(i, turn):
                pe.wait_ge(out_done, NA + i * NT)
                gate_up(i, 0)
                gate_up(i, 1)
                act_transposed(i, ACT0, turn)
                gate_up(i, 2)
                act_transposed(i, ACT1, turn)
                if X in turn:
                    for step in (X, AGU, BGU0, BGU1, BGU2):
                        next_transposed(i, step, turn, i + 1)
                    into_ranks(i, turn)
                act_transposed(i, ACT2, turn)
                parts_done(i, ACT2, turn)
                free_bank(i, TD, turn)
                for c in range(FC):
                    rows = P if c < FC - 1 else FR
                    ins = three_pass(pe, ps[0:RANK, step_bank(TD, turn), 0:S], adT_hi[0:rows, c, :], adT_lo[0:rows, c, :],
                                     actT_hi[0:rows, c, :], actT_lo[0:rows, c, :], c == 0, c == FC - 1)
                ins.then_inc(in_psum, 1)
                for c in range(FC):
                    rows = P if c < FC - 1 else FR
                    three_pass(pe, ps[:, DOWN_BANK, :], actT_hi[0:rows, c, :], actT_lo[0:rows, c, :],
                               dT_hi[0:rows, c, :], dT_lo[0:rows, c, :], c == 0, False)
                if AD in turn:
                    next_transposed(i, AD, turn, i + 1)
                parts_done(i, TD, turn)
                three_pass(pe, ps[:, DOWN_BANK, :], td_hi[:], td_lo[:], bdT_hi[:], bdT_lo[:], False, True).then_inc(down_in_psum, 1)
                if BD in turn:
                    next_transposed(i, BD, turn, i + 1)

            for step in AHEAD:
                if step == TGU:
                    into_ranks(0, AHEAD)
                else:
                    next_transposed(0, step, AHEAD, 0)
            with pe.Fori(0, B - 1) as i:
                batch(i, TURN)
            batch(B - 1, LAST)


def adapters(nc, x, weight, ids, out):
    with ExitStack() as ctx:
        def sb(name, shape, dt=F32):
            return ctx.enter_context(nc.sbuf_tensor("ad_" + name, shape, dt))

        def sem(name):
            return ctx.enter_context(nc.semaphore("ad_" + name))

        ps = ctx.enter_context(nc.psum_tensor("ad_ps", [P, 8, NFREE], F32))
        OUT_BANK = 6
        STEPS = 1 + DC
        ident = sb("ident", [P, P])
        x_sb = [sb(f"x{j}", [P, DM]) for j in range(2)]
        w_raw = [sb(f"w_raw{j}", [P, DC, DM]) for j in range(2)]
        xT_hi = [sb(f"xT_hi{j}", [P, DC * S], F32R) for j in range(2)]
        xT_lo = [sb(f"xT_lo{j}", [P, DC * S], F32R) for j in range(2)]
        wT_hi = [sb(f"wT_hi{j}", [P, DC, DM], F32R) for j in range(2)]
        wT_lo = [sb(f"wT_lo{j}", [P, DC, DM], F32R) for j in range(2)]
        ident_step = sem("ident_step")
        x_loaded = [sem(f"x_loaded{j}") for j in range(2)]
        w_loaded = [sem(f"w_loaded{j}") for j in range(2)]
        in_psum = sem("in_psum")
        hi_done = sem("hi_done")
        parts_done = sem("parts_done")
        product_done = sem("product_done")
        added = sem("added")
        stored = [sem(f"stored{j}") for j in range(2)]

        PAIRS = B // 2

        def in_turn(prepare, finish):
            def turn(p):
                prepare(p, 1)
                finish(p, 0)
                prepare(p + 1, 0)
                finish(p, 1)
            return turn

        block = ctx.enter_context(nc.Block())

        @block.sync
        def _(sp):
            def load(i, j):
                sp.dma_start(x_sb[j][:], x[bass.ds(i, 1)].rearrange("o s d -> (o s) d")).then_inc(x_loaded[j], 16)
                a = sp.value_load(ids.rearrange("(o b) -> o b", o=1)[:, bass.ds(i, 1)], min_val=0, max_val=7)
                sp.dma_start(w_raw[j][:], weight[bass.ds(a, 1)].rearrange("o (c p) d -> p (o c) d", p=P)).then_inc(w_loaded[j], 16)

            def store(p, j):
                sp.wait_ge(added, p * 2 + j + 1)
                sp.dma_start(out[bass.ds(p * 2 + j, 1)].rearrange("o s d -> (o s) d"), x_sb[j][:]).then_inc(stored[j], 16)
                sp.wait_ge(stored[j], p * 16 + 16)

            load(0, 0)
            load(1, 1)
            with sp.Fori(0, PAIRS - 1) as p:
                for j in range(2):
                    store(p, j)
                    load(p * 2 + j + 2, j)
            for j in range(2):
                store(PAIRS - 1, j)

        @block.gpsimd
        def _(pool):
            make_identity(nc, pool, ident[:], ident_step)

        @block.scalar
        def _(act):
            def prepare(p, j):
                for s in range(STEPS):
                    act.wait_ge(in_psum, (p * 2 + j) * STEPS + s + 1)
                    act.activation(xT_hi[j][:] if s == 0 else wT_hi[j][:, s - 1, :], ps[:, s, :], ACT.Copy).then_inc(hi_done, 1)

            prepare(0, 0)
            with act.Fori(0, PAIRS - 1) as p:
                prepare(p, 1)
                prepare(p + 1, 0)
            prepare(PAIRS - 1, 1)

        @block.vector
        def _(dve):
            def prepare(p, j):
                for s in range(STEPS):
                    hi, lo = (xT_hi[j][:], xT_lo[j][:]) if s == 0 else (wT_hi[j][:, s - 1, :], wT_lo[j][:, s - 1, :])
                    dve.wait_ge(hi_done, (p * 2 + j) * STEPS + s + 1)
                    dve.tensor_tensor(lo, ps[:, s, :], hi.bitcast(F32), ALU.subtract).then_inc(parts_done, 1)

            def finish(p, j):
                dve.wait_ge(product_done, p * 2 + j + 1)
                dve.tensor_tensor(x_sb[j][:], ps[:, OUT_BANK + j, :], x_sb[j][:], ALU.add).then_inc(added, 1)

            prepare(0, 0)
            with dve.Fori(0, PAIRS - 1) as p:
                prepare(p, 1)
                finish(p, 0)
                prepare(p + 1, 0)
                finish(p, 1)
            prepare(PAIRS - 1, 1)
            finish(PAIRS - 1, 0)
            finish(PAIRS - 1, 1)

        @block.tensor
        def _(pe):
            def prepare(p, j, first=False):
                pe.wait_ge(x_loaded[j], p * 16 + 16)
                for s in range(STEPS):
                    if s == 1:
                        pe.wait_ge(w_loaded[j], p * 16 + 16)
                    if not first:
                        pe.wait_ge(parts_done, (p * 2 + j - 1) * STEPS + s + 1)
                    for c in range(DC):
                        src = x_sb[j][:, c * P:(c + 1) * P] if s == 0 else w_raw[j][:, c, (s - 1) * P:s * P]
                        ins = pe.transpose(ps[:, s, c * P:(c + 1) * P], src, ident[:])
                    ins.then_inc(in_psum, 1)

            def finish(p, j):
                pe.wait_ge(parts_done, (p * 2 + j) * STEPS + STEPS)
                for c in range(DC):
                    at = slice(c * S, (c + 1) * S)
                    ins = three_pass(pe, ps[:, OUT_BANK + j, :], xT_hi[j][:, at], xT_lo[j][:, at], wT_hi[j][:, c, :], wT_lo[j][:, c, :],
                                     c == 0, c == DC - 1)
                ins.then_inc(product_done, 1)

            pe.wait_ge(ident_step, 2)
            prepare(0, 0, first=True)
            with pe.Fori(0, PAIRS - 1) as p:
                prepare(p, 1)
                finish(p, 0)
                prepare(p + 1, 0)
                finish(p, 1)
            prepare(PAIRS - 1, 1)
            finish(PAIRS - 1, 0)
            finish(PAIRS - 1, 1)


_INS = ["x", "itok_Bx16_0_63", "itok_B_207_1644", "condB_coeff", "itok_B_2_6", "itok_B_3_7", "mask_Bx4096x4096_ik1",
        "L0_cond_Wq", "L0_cond_Wk", "L0_cond_Wv", "L0_cond_Wo", "L0_cond_q_norm_w", "L0_cond_k_norm_w",
        "L0_cond_k_cache", "L0_cond_v_cache", "L1_cond_W", "L1_cond_b", "L2_cond_W_gate", "L2_cond_W_up", "L2_cond_W_down",
        "L2_cond_A_gate", "L2_cond_B_gate", "L2_cond_A_up", "L2_cond_B_up", "L2_cond_A_down", "L2_cond_B_down",
        "L3_cond_weight"]


def kernel(**inputs):
    import concourse.bacc as bacc
    from concourse.bass_utils import run_bass_kernel_spmd

    nc = bacc.Bacc("TRN2", target_bir_lowering=False, num_devices=1)
    arrays, t = {}, {}
    for name in _INS:
        a = np.ascontiguousarray(inputs[name])
        arrays[f"in_{name}"] = a
        t[name] = nc.dram_tensor(f"in_{name}", a.shape, mybir.dt.from_np(a.dtype), kind="ExternalInput").ap()
    inv = (1.0 / np.power(np.float32(THETA), np.arange(0, D, 2, dtype=np.float32) / np.float32(D))).astype(np.float32)
    arrays["inv_freq"] = inv
    inv_freq = nc.dram_tensor("inv_freq", inv.shape, F32, kind="ExternalInput").ap()
    stage = [nc.dram_tensor(f"x_stage{n}", (B, S, DM), F32).ap() for n in range(3)]
    out = nc.dram_tensor("out", (B, S, DM), F32, kind="ExternalOutput").ap()

    attention(nc, t["x"], t["itok_Bx16_0_63"], t["itok_B_207_1644"], t["L0_cond_Wq"], t["L0_cond_Wk"], t["L0_cond_Wv"],
              t["L0_cond_Wo"], t["L0_cond_q_norm_w"], t["L0_cond_k_norm_w"], t["L0_cond_k_cache"], t["L0_cond_v_cache"],
              inv_freq, stage[0])
    dense_signed(nc, stage[0], t["L1_cond_W"], t["L1_cond_b"], t["condB_coeff"], t["mask_Bx4096x4096_ik1"], stage[1])
    swiglu(nc, stage[1], *[t[f"L2_cond_{n}"] for n in ("W_gate", "W_up", "W_down", "A_gate", "B_gate", "A_up", "B_up", "A_down", "B_down")],
           t["itok_B_2_6"], stage[2])
    adapters(nc, stage[2], t["L3_cond_weight"], t["itok_B_3_7"], out)
    r = run_bass_kernel_spmd(nc, [arrays], core_ids=[0])
    return r.results[0]["out"]
```

```python
from contextlib import ExitStack

import numpy as np

import concourse.bass as bass
from concourse import mybir

F32 = mybir.dt.float32
F32R = mybir.dt.float32r
BF16 = mybir.dt.bfloat16
I32 = mybir.dt.int32
U32 = mybir.dt.uint32
ALU = mybir.AluOpType
ACT = mybir.ActivationFunctionType

P = 128
B, S, DM = 8, 128, 512
DC = DM // P
D = 128
HK, G = 8, 4
PAGES, PSIZE, NPP = 64, 32, 16
L = NPP * PSIZE
LC = L // P
KEYS = L + S
KC = KEYS // P
EPS = 1e-6
SCALE = D ** -0.5
THETA = 10000.0
MASKED = 1e30
F = 1376
FC = -(-F // P)
FR = F - (FC - 1) * P
NFREE = 512
FN = [(n, min(NFREE, F - n)) for n in range(0, F, NFREE)]
RANK = 16
UP0 = 32
LORA_SCALE = 0.5

TWO_PI = 2 * np.pi
PI_A = 6.28125
PI_B = float(np.float32(np.round((TWO_PI - PI_A) * 2 ** 20) / 2 ** 20))
PI_C = float(np.float32(TWO_PI - PI_A - PI_B))
PI_F32 = 3.1415925
ROUND = 1.5 * 2 ** 23


def three_pass(pe, out, l_hi, l_lo, r_hi, r_lo, first, last):
    pe.matmul(out, l_hi, r_hi, start=first, stop=False)
    pe.matmul(out, l_hi, r_lo, start=False, stop=False)
    return pe.matmul(out, l_lo, r_hi, start=False, stop=last)


def wait_apart(eng, sem, count, passed):
    eng.wait_ge(sem, count)
    if not isinstance(count, int):
        eng.sem_inc(passed, 1)


def make_identity(nc, pool, ident, step):
    pool.memset(ident, 0.0).then_inc(step, 1)
    pool.wait_ge(step, 1)
    pool.affine_select(out=ident, in_=ident, compare_op=ALU.not_equal, fill=1.0, base=0,
                       pattern=[[-1, P]], channel_multiplier=1).then_inc(step, 1)


def attention(nc, x, block_table, seqlens, wq, wk, wv, wo, qw, kw, k_cache, v_cache, inv_freq, x_out):
    with ExitStack() as ctx:
        def sb(name, shape, dt=F32):
            return ctx.enter_context(nc.sbuf_tensor("at_" + name, shape, dt))

        def sem(name):
            return ctx.enter_context(nc.semaphore(name))

        ps = ctx.enter_context(nc.psum_tensor("at_ps", [P, 8 * NFREE], F32))

        def bank(n, cols=NFREE):
            return ps[:, n * NFREE:n * NFREE + cols]

        SCORE_PARTS = [(0, KEYS // 2), (KEYS // 2, KEYS)]

        def slot(h):
            at = 2 * (h % 2) * NFREE + NFREE - SCORE_PARTS[1][0]
            return ps[:, at:at + KEYS]

        Q_BANK, KV_BANK, A_BANK, B_BANK, O_BANK = 4, 5, 6, 7, 3

        ident = sb("ident", [P, P])
        xres = sb("xres", [P, B, DM])
        xT_hi = sb("xT_hi", [P, DC, B * S], F32R)
        xT_lo = sb("xT_lo", [P, DC, B * S], F32R)
        wq_raw = sb("wq_raw", [P, G, DM])
        wkv_raw = sb("wkv_raw", [P, 2, DM])
        wo_raw = sb("wo_raw", [P, DC, G * D])
        wqT_hi = sb("wqT_hi", [P, DC, G * D], F32R)
        wqT_lo = sb("wqT_lo", [P, DC, G * D], F32R)
        wkvT_hi = sb("wkvT_hi", [P, DC, 2 * D], F32R)
        wkvT_lo = sb("wkvT_lo", [P, DC, 2 * D], F32R)
        woT_hi = sb("woT_hi", [P, G, DM], F32R)
        woT_lo = sb("woT_lo", [P, G, DM], F32R)
        q_cos = sb("q_cos", [P, B, D])
        q_sin = sb("q_sin", [P, B, D])
        k_cos = sb("k_cos", [P, B, D])
        k_sin = sb("k_sin", [P, B, D])
        mask = sb("mask", [P, B, KEYS], BF16)
        k_raw = [sb(f"k_raw{j}", [P, LC, D]) for j in range(2)]
        v_raw = [sb(f"v_raw{j}", [P, LC, D]) for j in range(2)]
        kT_hi = sb("kT_hi", [P, KEYS], F32R)
        kT_lo = sb("kT_lo", [P, KEYS], F32R)
        v_hi = [sb(f"v_hi{j}", [P, KC, D], F32R) for j in range(2)]
        v_lo = [sb(f"v_lo{j}", [P, KC, D], F32R) for j in range(2)]
        qT_hi = [sb(f"qT_hi{j}", [P, G * S], F32R) for j in range(2)]
        qT_lo = [sb(f"qT_lo{j}", [P, G * S], F32R) for j in range(2)]
        u_q = sb("u_q", [P, G, D])
        w_q = sb("w_q", [P, G, D])
        q_rot = sb("q_rot", [P, G, D])
        u_k = sb("u_k", [P, D])
        w_k = sb("w_k", [P, D])
        k_rot = sb("k_rot", [P, D])
        square = sb("square", [P, G + 1, D])
        sumsq = [sb(f"sumsq{j}", [P, G + 1]) for j in range(2)]
        d_eps = sb("d_eps", [P, G])
        minus_half = sb("minus_half", [P, G])
        inv_rms = [sb(f"inv_rms{j}", [P, G + 1]) for j in range(2)]
        scores = [sb(f"scores{j}", [P, KEYS]) for j in range(2)]
        neg_max = sb("neg_max", [P, G])
        row_sum = sb("row_sum", [P, G])
        row_inv = sb("row_inv", [P, G])
        probs = sb("probs", [P, G, KEYS])
        pT_hi = [sb(f"pT_hi{j}", [P, G * S], F32R) for j in range(3)]
        pT_lo = [sb(f"pT_lo{j}", [P, G * S], F32R) for j in range(3)]
        oT_hi = sb("oT_hi", [P, G * S], F32R)
        oT_lo = sb("oT_lo", [P, G * S], F32R)
        key_row = sb("key_row", [P, B * LC])
        key_idx = [sb(f"key_idx{j}", [P, LC], U32) for j in range(2)]
        head_no = sb("head_no", [P, 1])
        seq_i = sb("seq_i", [P, B], I32)
        seq_f = sb("seq_f", [P, B])
        in_page_f = sb("in_page_f", [P, 1])
        tok_i = sb("tok_i", [P, 1], I32)
        tok_f = sb("tok_f", [P, 1])
        HALF = D // 2
        qw_sb, kw_sb, invf_sb = u_q[:, 0, :], u_q[:, 1, :], u_q[:, 2, 0:HALF]
        table_sb = u_q[:, 3, 0:B * NPP].bitcast(I32)
        angle = probs[:, 0, 0:B * HALF]
        turns = probs[:, 1, 0:B * HALF]
        sin_t = probs[:, 2, 0:B * HALF]
        cos_t = probs[:, 3, 0:B * HALF]
        key_no_i = scores[0][:, 0:L].bitcast(I32)
        key_no = scores[1][:, 0:L]

        x_loaded = sem("x_loaded")
        small_loaded = sem("small_loaded")
        ident_step = sem("ident_step")
        iota_done = sem("iota_done")
        table_step = sem("table_step")
        angles_ready = sem("angles_ready")
        sincos_ready = sem("sincos_ready")
        tables_ready = sem("tables_ready")
        rows_ready = sem("rows_ready")
        xT_in_psum = sem("xT_in_psum")
        xT_hi_done = sem("xT_hi_done")
        xT_done = sem("xT_done")
        wqkv_loaded = sem("wqkv_loaded")
        wo_loaded = sem("wo_loaded")
        wqkv_in_psum = sem("wqkv_in_psum")
        wqkv_hi_done = sem("wqkv_hi_done")
        wqkv_done = sem("wqkv_done")
        wo_in_psum = sem("wo_in_psum")
        wo_hi_done = sem("wo_hi_done")
        wo_done = sem("wo_done")
        idx_ready = sem("idx_ready")
        head_step = sem("head_step")
        k_loaded = [sem(f"k_loaded{j}") for j in range(2)]
        v_loaded = [sem(f"v_loaded{j}") for j in range(2)]
        q_in_psum = sem("q_in_psum")
        kv_in_psum = sem("kv_in_psum")
        q_turned = sem("q_turned")
        q_squared = sem("q_squared")
        q_rot_done = sem("q_rot_done")
        kv_read = sem("kv_read")
        k_turned = sem("k_turned")
        v_new_done = sem("v_new_done")
        k_rot_done = sem("k_rot_done")
        scale_ready = sem("scale_ready")
        k_scale_ready = sem("k_scale_ready")
        v_hi_done = sem("v_hi_done")
        v_cache_done = sem("v_cache_done")
        kc_in_psum = sem("kc_in_psum")
        kc_hi_done = sem("kc_hi_done")
        kc_done = sem("kc_done")
        kn_in_psum = sem("kn_in_psum")
        kn_hi_done = sem("kn_hi_done")
        kn_done = sem("kn_done")
        qT_in_psum = sem("qT_in_psum")
        qT_hi_done = sem("qT_hi_done")
        qT_done = sem("qT_done")
        scores_in_psum = sem("scores_in_psum")
        scores_done = sem("scores_done")
        exp_done = sem("exp_done")
        inv_done = sem("inv_done")
        probs_done = sem("probs_done")
        pT_in_psum = sem("pT_in_psum")
        pT_hi_done = sem("pT_hi_done")
        pT_done = sem("pT_done")
        pv_done = sem("pv_done")
        oT_hi_done = sem("oT_hi_done")
        oT_done = sem("oT_done")
        y_in_psum = sem("y_in_psum")
        y_bank_free = sem("y_bank_free")
        pool_passed = sem("pool_passed")
        dve_passed = sem("dve_passed")
        stored = sem("stored")

        QKV_GROUPS, WO_GROUPS = DC + DC // 2, G
        WEIGHT_BANKS = [A_BANK, B_BANK]

        def upto(g, b, per, k=0):
            return g * (B * per) + (b * per + k)

        def following(g, b):
            return (g, b + 1) if b + 1 < B else (g + 1, 0)

        def weight_groups(b, slot, last):
            groups = {0: {4: [0]}, 1: {0: [1], 1: [2], 2: [3]}}
            if not last:
                groups[B - 2] = {0: [0], 1: [1], 2: [2], 3: [3]}
                groups[B - 1] = {0: [4], 1: [5]}
            return groups.get(b, {}).get(slot, [])

        block = ctx.enter_context(nc.Block())

        @block.sync
        def _(sp):
            sp.dma_start(xres[:], x.rearrange("b s d -> s b d")).then_inc(x_loaded, 16)
            sp.dma_start(seq_i[:], seqlens.rearrange("(o b) -> o b", o=1).broadcast_to([P, B])).then_inc(small_loaded, 16)
            sp.dma_start(table_sb, block_table.rearrange("(o b) n -> o (b n)", o=1).broadcast_to([P, B * NPP])).then_inc(small_loaded, 16)
            sp.dma_start(qw_sb, qw.rearrange("(o d) -> o d", o=1).broadcast_to([P, D])).then_inc(small_loaded, 16)
            sp.dma_start(kw_sb, kw.rearrange("(o d) -> o d", o=1).broadcast_to([P, D])).then_inc(small_loaded, 16)
            sp.dma_start(invf_sb, inv_freq.rearrange("(o d) -> o d", o=1).broadcast_to([P, HALF])).then_inc(small_loaded, 16)

            def load_qkv(g):
                sp.dma_start(wq_raw[:], wq[bass.ds(g * (G * D), G * D), :].rearrange("(e p) d -> p e d", p=P)).then_inc(wqkv_loaded, 16)
                sp.dma_start(wkv_raw[:, 0, :], wk[bass.ds(g * D, D), :]).then_inc(wqkv_loaded, 16)
                sp.dma_start(wkv_raw[:, 1, :], wv[bass.ds(g * D, D), :]).then_inc(wqkv_loaded, 16)

            def load_wo(g):
                sp.dma_start(wo_raw[:], wo[:, bass.ds(g * (G * D), G * D)].rearrange("(n p) e -> p n e", p=P)).then_inc(wo_loaded, 16)

            load_qkv(0)
            load_wo(0)
            with sp.Fori(0, HK - 1) as g:
                sp.wait_ge(wqkv_in_psum, g * QKV_GROUPS + QKV_GROUPS)
                sp.wait_ge(wo_in_psum, g * WO_GROUPS + WO_GROUPS)
                load_qkv(g + 1)
                load_wo(g + 1)
            for b in range(B):
                sp.wait_ge(y_bank_free, 1 + upto(HK - 1, b, 1, 1))
                sp.dma_start(x_out[b], xres[:, b, :]).then_inc(stored, 16)
            sp.wait_ge(stored, 16 * B)

        @block.gpsimd
        def _(pool):
            make_identity(nc, pool, ident[:], ident_step)
            pool.wait_ge(ident_step, 2)
            pool.iota(tok_i[:], pattern=[[0, 1]], base=0, channel_multiplier=1).then_inc(iota_done, 1)
            pool.iota(key_no_i, pattern=[[1, L]], base=0, channel_multiplier=0).then_inc(iota_done, 1)
            pool.memset(d_eps[:], D * EPS).then_inc(iota_done, 1)
            pool.memset(minus_half[:], -0.5).then_inc(iota_done, 1)
            pool.memset(head_no[:], 0.0).then_inc(head_step, 1)
            pool.memset(mask[:, :, L:KEYS], 0.0).then_inc(iota_done, 1)

            def indices(b):
                return pool.tensor_scalar(key_idx[b % 2][:], key_row[:, b * LC:(b + 1) * LC], head_no[:, 0:1], None, ALU.add)

            def gather(b, cs, cache, raw, loaded):
                for c in cs:
                    pool.indirect_dma_start(
                        out=raw[b % 2][:, c, :], out_offset=None,
                        in_=cache.rearrange("a r h d -> (a r h) d"),
                        in_offset=bass.IndirectOffsetOnAxis(ap=key_idx[b % 2][:, c:c + 1], axis=0),
                    ).then_inc(loaded[b % 2], 16)

            def next_head(g):
                wait_apart(pool, idx_ready, upto(g, B - 1, 1, 1), pool_passed)
                pool.tensor_scalar(head_no[:], head_no[:], 1.0, None, ALU.add).then_inc(head_step, 1)

            def start_gather(g, b):
                wait_apart(pool, head_step, g + 1, pool_passed)
                indices(b).then_inc(idx_ready, 1)
                wait_apart(pool, idx_ready, upto(g, b, 1, 1), pool_passed)

            def rotate_k(g, b):
                pool.wait_ge(k_turned, upto(g, b, 1, 1))
                pool.tensor_tensor(k_rot[:, 0:HALF], u_k[:, 0:HALF], w_k[:, HALF:D], ALU.subtract)
                pool.tensor_tensor(k_rot[:, HALF:D], u_k[:, HALF:D], w_k[:, 0:HALF], ALU.add).then_inc(k_rot_done, 1)

            def rotate_q(g, b):
                pool.wait_ge(q_turned, upto(g, b, 1, 1))
                pool.tensor_tensor(q_rot[:, :, 0:HALF], u_q[:, :, 0:HALF], w_q[:, :, HALF:D], ALU.subtract)
                pool.tensor_tensor(q_rot[:, :, HALF:D], u_q[:, :, HALF:D], w_q[:, :, 0:HALF], ALU.add).then_inc(q_rot_done, 1)

            def key_scale(g, b):
                j = b % 2
                pool.wait_ge(kv_read, upto(g, b, 1, 1))
                pool.tensor_tensor(inv_rms[j][:, G:G + 1], sumsq[j][:, G:G + 1], d_eps[:, 0:1], ALU.add).then_inc(k_scale_ready, 1)
                pool.wait_ge(k_scale_ready, upto(g, b, 2, 1))
                pool.tensor_tensor(inv_rms[j][:, G:G + 1], inv_rms[j][:, G:G + 1], minus_half[:, 0:1], ALU.pow).then_inc(k_scale_ready, 1)

            def query_scale(g, b):
                j = b % 2
                pool.wait_ge(q_squared, upto(g, b, 1, 1))
                pool.tensor_tensor(inv_rms[j][:, 0:G], sumsq[j][:, 0:G], d_eps[:], ALU.add).then_inc(scale_ready, 1)
                pool.wait_ge(scale_ready, upto(g, b, 2, 1))
                pool.tensor_tensor(inv_rms[j][:, 0:G], inv_rms[j][:, 0:G], minus_half[:], ALU.pow).then_inc(scale_ready, 1)

            def normalise(g, b, h):
                wait_apart(pool, inv_done, upto(g, b, G, h + 1), pool_passed)
                pool.tensor_scalar(probs[:, h, :], probs[:, h, :], row_inv[:, h:h + 1], 1.0, ALU.mult, ALU.mult).then_inc(probs_done, 1)

            pool.wait_ge(iota_done, 5)
            pool.wait_ge(rows_ready, 4)
            for b in range(2):
                start_gather(0, b)
                gather(b, range(LC), k_cache, k_raw, k_loaded)
                gather(b, range(LC), v_cache, v_raw, v_loaded)
            rotate_q(0, 0)
            key_scale(0, 0)
            rotate_k(0, 0)
            query_scale(0, 0)
            rotate_q(0, 1)

            def group(g, last):
                for b in range(B):
                    g1, b1 = following(g, b)
                    g2, b2 = following(g1, b1)
                    more, more2 = not (last and b == B - 1), not (last and b >= B - 2)

                    def keys(cs):
                        if more2:
                            gather(b2, cs, k_cache, k_raw, k_loaded)

                    def values(cs):
                        if more2:
                            gather(b2, cs, v_cache, v_raw, v_loaded)

                    if more2:
                        if b2 == 0:
                            next_head(g)
                        pool.wait_ge(kc_in_psum, upto(g, b, 1, 1))
                        pool.wait_ge(v_cache_done, upto(g, b, 1, 1))
                        start_gather(g2, b2)
                    values(range(1))
                    for h in range(G):
                        normalise(g, b, h)
                    values(range(1, LC))
                    if more:
                        query_scale(g1, b1)
                        key_scale(g1, b1)
                        rotate_k(g1, b1)
                    keys(range(2))
                    if more2:
                        rotate_q(g2, b2)
                    keys(range(2, LC))

            with pool.Fori(0, HK - 1) as g:
                group(g, False)
            group(HK - 1, True)

        @block.scalar
        def _(act):
            for j, t in ((0, sin_t), (1, cos_t)):
                act.wait_ge(angles_ready, j + 1)
                act.activation(t, t, ACT.Sin).then_inc(sincos_ready, 1)
            for b in range(B):
                act.wait_ge(xT_in_psum, b + 1)
                act.activation(xT_hi[:, :, b * S:(b + 1) * S], bank(b).rearrange("p (c s) -> p c s", c=DC), ACT.Copy).then_inc(xT_hi_done, 1)

            def hi(out, src, ready, count, done):
                act.wait_ge(ready, count)
                act.activation(out, src, ACT.Copy).then_inc(done, 1)

            def qkv_group(g, n):
                out = wqT_hi[:, n, :] if n < DC else wkvT_hi[:, 2 * (n - DC):2 * (n - DC) + 2, :].rearrange("p c e -> p (c e)")
                hi(out, bank(WEIGHT_BANKS[n % 2]), wqkv_in_psum, g * QKV_GROUPS + n + 1, wqkv_hi_done)

            def wo_group(g, n):
                hi(woT_hi[:, n, :], bank(WEIGHT_BANKS[(n + 1) % 2]), wo_in_psum, g * WO_GROUPS + n + 1, wo_hi_done)

            def cached_values(g, b):
                j = b % 2
                hi(v_hi[j][:, 0:LC, :], v_raw[j][:], v_loaded[j], g * (B // 2 * LC * 16) + (b // 2 + 1) * LC * 16, v_hi_done)

            def cached_keys(g, b):
                hi(kT_hi[:, 0:L], bank(A_BANK), kc_in_psum, upto(g, b, 1, 1), kc_hi_done)

            def new_kv(g, b):
                j = b % 2
                act.wait_ge(kv_in_psum, upto(g, b, 1, 1))
                act.activation(square[:, G, :], bank(KV_BANK, D), ACT.Square, accum_out=sumsq[j][:, G:G + 1])
                act.activation(v_hi[j][:, LC, :], bank(KV_BANK)[:, D:2 * D], ACT.Copy).then_inc(kv_read, 1)

            def squares(g, b):
                j = b % 2
                act.wait_ge(q_turned, upto(g, b, 1, 1))
                for h in range(G):
                    ins = act.activation(square[:, h, :], bank(Q_BANK)[:, h * D:(h + 1) * D], ACT.Square, accum_out=sumsq[j][:, h:h + 1])
                ins.then_inc(q_squared, 1)

            def exps(g, b, h):
                act.wait_ge(scores_done, upto(g, b, G, h + 1))
                act.activation(probs[:, h, :], scores[h % 2][:], ACT.Exp, bias=neg_max[:, h:h + 1], scale=-1.0,
                               accum_out=row_sum[:, h:h + 1]).then_inc(exp_done, 1)

            def probs_T(g, b, c):
                if c >= 3:
                    act.wait_ge(pv_done, upto(g, b, KC, c - 2))
                hi(pT_hi[c % 3][:], bank([B_BANK, A_BANK][c % 2]), pT_in_psum, upto(g, b, KC, c + 1), pT_hi_done)

            def new_keys(g, b):
                hi(kT_hi[:, L:KEYS], bank(KV_BANK, S), kn_in_psum, upto(g, b, 1, 1), kn_hi_done)

            def queries(g, b):
                hi(qT_hi[b % 2][:], bank(Q_BANK), qT_in_psum, upto(g, b, 1, 1), qT_hi_done)

            for n in range(QKV_GROUPS):
                qkv_group(0, n)
            squares(0, 0)
            queries(0, 0)
            cached_keys(0, 0)
            new_kv(0, 0)
            cached_values(0, 0)
            new_keys(0, 0)

            def group(g, last):
                for b in range(B):
                    g1, b1 = following(g, b)
                    more = not (last and b == B - 1)

                    def weights(slot):
                        for n in weight_groups(b, slot, last):
                            if b < 2:
                                wo_group(g, n)
                            else:
                                qkv_group(g + 1, n)

                    if more:
                        squares(g1, b1)
                    weights(0)
                    exps(g, b, 0)
                    if more:
                        queries(g1, b1)
                    exps(g, b, 1)
                    weights(1)
                    weights(2)
                    exps(g, b, 2)
                    exps(g, b, 3)
                    weights(3)
                    weights(4)
                    if more:
                        cached_keys(g1, b1)
                    probs_T(g, b, 0)
                    probs_T(g, b, 1)
                    if more:
                        cached_values(g1, b1)
                        new_kv(g1, b1)
                    probs_T(g, b, 2)
                    probs_T(g, b, 3)
                    probs_T(g, b, 4)
                    if more:
                        new_keys(g1, b1)
                    hi(oT_hi[:], bank(O_BANK), pv_done, upto(g, b, KC, KC), oT_hi_done)

            group(0, False)
            with act.Fori(1, HK - 1) as g:
                group(g, False)
            group(HK - 1, True)

        @block.vector
        def _(dve):
            steps = [0]

            def link(ins):
                steps[0] += 1
                ins.then_inc(table_step, 1)
                dve.wait_ge(table_step, steps[0])

            dve.memset(neg_max[:], 0.0).then_inc(y_bank_free, 1)
            dve.wait_ge(small_loaded, 16 * 5)
            dve.wait_ge(iota_done, 5)
            dve.tensor_copy(seq_f[:], seq_i[:])
            dve.tensor_copy(key_no, key_no_i)
            dve.tensor_scalar(qw_sb, qw_sb, -1.0, None, ALU.mult)
            dve.tensor_scalar(kw_sb, kw_sb, float(np.sqrt(D)), None, ALU.mult)
            link(dve.tensor_copy(tok_f[:], tok_i[:]))
            for j in range(4):
                q = slice(PSIZE * j, PSIZE * j + PSIZE)
                link(dve.tensor_scalar(in_page_f[q, :], tok_f[q, :], float(-PSIZE * j), float(HK), ALU.add, ALU.mult))
                dve.tensor_scalar(key_row[q, :], table_sb[q, :].rearrange("p (n j) -> p n j", j=4)[:, :, j],
                                  float(PSIZE * HK), in_page_f[q, 0:1], ALU.mult, ALU.add).then_inc(rows_ready, 1)
            link(dve.tensor_scalar(seq_f[:], seq_f[:], tok_f[:, 0:1], None, ALU.add))
            angle3 = angle.rearrange("p (b f) -> p b f", b=B)
            link(dve.tensor_tensor(angle3, seq_f[:].unsqueeze(2).broadcast_to([P, B, HALF]),
                                   invf_sb.unsqueeze(1).broadcast_to([P, B, HALF]), ALU.mult))
            link(dve.tensor_scalar(turns, angle, 1.0 / TWO_PI, ROUND, ALU.mult, ALU.add))
            link(dve.tensor_scalar(turns, turns, -ROUND, None, ALU.add))
            for part in (PI_A, PI_B, PI_C):
                link(dve.scalar_tensor_tensor(out=angle, in0=turns, scalar=-part, in1=angle, op0=ALU.mult, op1=ALU.add))
            dve.tensor_scalar(sin_t, angle, PI_F32, -PI_F32, ALU.min, ALU.max).then_inc(angles_ready, 1)
            link(dve.scalar_tensor_tensor(out=cos_t, in0=angle, scalar=-1.0, in1=angle, op0=ALU.mult, op1=ALU.max))
            dve.tensor_scalar(cos_t, cos_t, -1.0, float(np.pi / 2), ALU.mult, ALU.add).then_inc(angles_ready, 1)
            link(dve.tensor_scalar(seq_f[:], seq_f[:], tok_f[:, 0:1], None, ALU.subtract))
            for b in range(B):
                dve.tensor_scalar(mask[:, b, 0:L], key_no, seq_f[:, b:b + 1], MASKED, ALU.is_ge, ALU.mult)
            dve.wait_ge(sincos_ready, 2)
            for t, c_out, s_out in ((qw_sb, q_cos, q_sin), (kw_sb, k_cos, k_sin)):
                for half in range(2):
                    f = slice(half * HALF, (half + 1) * HALF)
                    wb = t[:, f].unsqueeze(1).broadcast_to([P, B, HALF])
                    dve.tensor_tensor(c_out[:, :, f], cos_t.rearrange("p (b f) -> p b f", b=B), wb, ALU.mult)
                    ins = dve.tensor_tensor(s_out[:, :, f], sin_t.rearrange("p (b f) -> p b f", b=B), wb, ALU.mult)
            ins.then_inc(tables_ready, 1)
            dve.wait_ge(tables_ready, 1)

            def lo(out, src, hi_part, hi_done, count, done):
                dve.wait_ge(hi_done, count)
                dve.tensor_tensor(out, src, hi_part.bitcast(F32), ALU.subtract).then_inc(done, 1)

            for b in range(B):
                at = slice(b * S, (b + 1) * S)
                lo(xT_lo[:, :, at], bank(b).rearrange("p (c s) -> p c s", c=DC), xT_hi[:, :, at], xT_hi_done, b + 1, xT_done)

            def qkv_group(g, n):
                flat = lambda t: t[:, 2 * (n - DC):2 * (n - DC) + 2, :].rearrange("p c e -> p (c e)")
                out, h = (wqT_lo[:, n, :], wqT_hi[:, n, :]) if n < DC else (flat(wkvT_lo), flat(wkvT_hi))
                lo(out, bank(WEIGHT_BANKS[n % 2]), h, wqkv_hi_done, g * QKV_GROUPS + n + 1, wqkv_done)

            def wo_group(g, n):
                lo(woT_lo[:, n, :], bank(WEIGHT_BANKS[(n + 1) % 2]), woT_hi[:, n, :], wo_hi_done, g * WO_GROUPS + n + 1, wo_done)

            def cached_values(g, b):
                j = b % 2
                lo(v_lo[j][:, 0:LC, :], v_raw[j][:], v_hi[j][:, 0:LC, :], v_hi_done, upto(g, b, 1, 1), v_cache_done)

            def cached_keys(g, b):
                lo(kT_lo[:, 0:L], bank(A_BANK), kT_hi[:, 0:L], kc_hi_done, upto(g, b, 1, 1), kc_done)

            def turn_q(g, b, part):
                q3 = bank(Q_BANK).rearrange("p (h d) -> p h d", h=G)
                if part == 0:
                    dve.wait_ge(q_in_psum, upto(g, b, 1, 1))
                    dve.tensor_tensor(u_q[:], q3, q_cos[:, b:b + 1, :].broadcast_to([P, G, D]), ALU.mult)
                else:
                    dve.tensor_tensor(w_q[:], q3, q_sin[:, b:b + 1, :].broadcast_to([P, G, D]), ALU.mult).then_inc(q_turned, 1)

            def new_kv(g, b):
                j = b % 2
                scale = inv_rms[j][:, G:G + 1]
                dve.wait_ge(kv_read, upto(g, b, 1, 1))
                dve.tensor_tensor(v_lo[j][:, LC, :], bank(KV_BANK)[:, D:2 * D], v_hi[j][:, LC, :].bitcast(F32), ALU.subtract).then_inc(v_new_done, 1)
                dve.wait_ge(k_scale_ready, upto(g, b, 2, 2))
                dve.scalar_tensor_tensor(out=u_k[:], in0=bank(KV_BANK, D), scalar=scale, in1=k_cos[:, b, :], op0=ALU.mult, op1=ALU.mult)
                dve.scalar_tensor_tensor(out=w_k[:], in0=bank(KV_BANK, D), scalar=scale, in1=k_sin[:, b, :],
                                         op0=ALU.mult, op1=ALU.mult).then_inc(k_turned, 1)

            def mask_and_max(g, b, h):
                if h >= 2:
                    dve.wait_ge(exp_done, upto(g, b, G, h - 1))
                dve.wait_ge(scores_in_psum, upto(g, b, G, h + 1))
                wait_apart(dve, scale_ready, upto(g, b, 2, 2), dve_passed)
                dve.tensor_tensor_reduce(out=scores[h % 2][:], in0=slot(h), in1=mask[:, b, :],
                                         scale=inv_rms[b % 2][:, h:h + 1], scalar=3.0e38, op0=ALU.add, op1=ALU.min,
                                         accum_out=neg_max[:, h:h + 1]).then_inc(scores_done, 1)

            def inverse(g, b, h):
                dve.wait_ge(exp_done, upto(g, b, G, h + 1))
                dve.reciprocal(row_inv[:, h:h + 1], row_sum[:, h:h + 1]).then_inc(inv_done, 1)

            def add_y(g, b):
                at = (b - 1) % B
                dve.wait_ge(y_in_psum, upto(g, b, 1))
                dve.tensor_tensor(xres[:, at, :], bank(KV_BANK), xres[:, at, :], ALU.add).then_inc(y_bank_free, 1)

            def probs_T(g, b, c):
                lo(pT_lo[c % 3][:], bank([B_BANK, A_BANK][c % 2]), pT_hi[c % 3][:], pT_hi_done, upto(g, b, KC, c + 1), pT_done)

            def new_keys(g, b):
                lo(kT_lo[:, L:KEYS], bank(KV_BANK, S), kT_hi[:, L:KEYS], kn_hi_done, upto(g, b, 1, 1), kn_done)

            def queries(g, b):
                lo(qT_lo[b % 2][:], bank(Q_BANK), qT_hi[b % 2][:], qT_hi_done, upto(g, b, 1, 1), qT_done)

            for n in range(QKV_GROUPS):
                qkv_group(0, n)
            turn_q(0, 0, 0)
            turn_q(0, 0, 1)
            queries(0, 0)
            cached_keys(0, 0)
            new_kv(0, 0)
            cached_values(0, 0)
            turn_q(0, 1, 0)
            turn_q(0, 1, 1)
            new_keys(0, 0)

            def group(g, first, last):
                for b in range(B):
                    g1, b1 = following(g, b)
                    more, more2 = not (last and b == B - 1), not (last and b >= B - 2)

                    def weights(slot):
                        for n in weight_groups(b, slot, last):
                            if b < 2:
                                wo_group(g, n)
                            else:
                                qkv_group(g + 1, n)

                    mask_and_max(g, b, 0)
                    weights(0)
                    mask_and_max(g, b, 1)
                    inverse(g, b, 0)
                    if more:
                        queries(g1, b1)
                    inverse(g, b, 1)
                    weights(1)
                    weights(2)
                    mask_and_max(g, b, 2)
                    mask_and_max(g, b, 3)
                    inverse(g, b, 2)
                    inverse(g, b, 3)
                    if not (first and b == 0):
                        add_y(g, b)
                    weights(3)
                    weights(4)
                    if more:
                        cached_keys(g1, b1)
                    probs_T(g, b, 0)
                    probs_T(g, b, 1)
                    if more:
                        cached_values(g1, b1)
                    probs_T(g, b, 2)
                    if more:
                        new_kv(g1, b1)
                    probs_T(g, b, 3)
                    probs_T(g, b, 4)
                    if more2:
                        turn_q(*following(g1, b1), 0)
                        turn_q(*following(g1, b1), 1)
                    if more:
                        new_keys(g1, b1)
                    lo(oT_lo[:], bank(O_BANK), oT_hi[:], oT_hi_done, upto(g, b, 1, 1), oT_done)

            group(0, True, False)
            with dve.Fori(1, HK - 1) as g:
                group(g, False, False)
            group(HK - 1, False, True)
            add_y(HK, 0)

        @block.tensor
        def _(pe):
            pe.wait_ge(ident_step, 2)
            pe.wait_ge(x_loaded, 16)
            for b in range(B):
                for c in range(DC):
                    ins = pe.transpose(bank(b)[:, c * S:(c + 1) * S], xres[:, b, c * P:(c + 1) * P], ident[:])
                ins.then_inc(xT_in_psum, 1)
            pe.wait_ge(xT_done, B)

            def qkv_group(g, n):
                if n == 0:
                    pe.wait_ge(wqkv_loaded, g * 48 + 48)
                if n >= 2:
                    pe.wait_ge(wqkv_done, g * QKV_GROUPS + n - 1)
                out = bank(WEIGHT_BANKS[n % 2])
                if n < DC:
                    for e in range(G):
                        ins = pe.transpose(out[:, e * D:(e + 1) * D], wq_raw[:, e, n * P:(n + 1) * P], ident[:])
                else:
                    for m in range(4):
                        c = 2 * (n - DC) + m // 2
                        ins = pe.transpose(out[:, m * D:(m + 1) * D], wkv_raw[:, m % 2, c * P:(c + 1) * P], ident[:])
                ins.then_inc(wqkv_in_psum, 1)

            def wo_group(g, n):
                if n == 0:
                    pe.wait_ge(wo_loaded, g * 16 + 16)
                if n >= 2:
                    pe.wait_ge(wo_done, g * WO_GROUPS + n - 1)
                for c in range(DC):
                    ins = pe.transpose(bank(WEIGHT_BANKS[(n + 1) % 2])[:, c * P:(c + 1) * P], wo_raw[:, c, n * D:(n + 1) * D], ident[:])
                ins.then_inc(wo_in_psum, 1)

            def cached_keys(g, b):
                j = b % 2
                pe.wait_ge(k_loaded[j], g * (B // 2 * LC * 16) + (b // 2 + 1) * LC * 16)
                for c in range(LC):
                    ins = pe.transpose(bank(A_BANK)[:, c * P:(c + 1) * P], k_raw[j][:, c, :], ident[:])
                ins.then_inc(kc_in_psum, 1)

            def project_q(g, b, cs, first=False):
                at = slice(b * S, (b + 1) * S)
                if cs[0] == 0 and not first:
                    pe.wait_ge(qT_done, upto(g, b, 1))
                if cs[0] == 0 and b == 0:
                    pe.wait_ge(wqkv_done, g * QKV_GROUPS + DC)
                for c in cs:
                    ins = three_pass(pe, bank(Q_BANK), xT_hi[:, c, at], xT_lo[:, c, at], wqT_hi[:, c, :], wqT_lo[:, c, :], c == 0, c == DC - 1)
                if c == DC - 1:
                    ins.then_inc(q_in_psum, 1)

            def project_kv(g, b, first=False):
                at = slice(b * S, (b + 1) * S)
                if not first:
                    pe.wait_ge(y_bank_free, upto(g, b, 1))
                if b == 0:
                    pe.wait_ge(wqkv_done, g * QKV_GROUPS + QKV_GROUPS)
                for c in range(DC):
                    ins = three_pass(pe, bank(KV_BANK, 2 * D), xT_hi[:, c, at], xT_lo[:, c, at], wkvT_hi[:, c, :], wkvT_lo[:, c, :], c == 0, c == DC - 1)
                ins.then_inc(kv_in_psum, 1)

            def new_keys(g, b):
                pe.wait_ge(k_rot_done, upto(g, b, 1, 1))
                pe.wait_ge(v_new_done, upto(g, b, 1, 1))
                pe.transpose(bank(KV_BANK, S), k_rot[:], ident[:]).then_inc(kn_in_psum, 1)

            def queries(g, b):
                pe.wait_ge(q_rot_done, upto(g, b, 1, 1))
                pe.wait_ge(q_squared, upto(g, b, 1, 1))
                for h in range(G):
                    ins = pe.transpose(bank(Q_BANK)[:, h * S:(h + 1) * S], q_rot[:, h, :], ident[:])
                ins.then_inc(qT_in_psum, 1)

            def score(g, b, h, first):
                if h == 0:
                    pe.wait_ge(kc_done, upto(g, b, 1, 1))
                    pe.wait_ge(qT_done, upto(g, b, 1, 1))
                if h >= 2:
                    pe.wait_ge(scores_done, upto(g, b, G, h - 1))
                q = slice(h * S, (h + 1) * S)
                qh, ql = qT_hi[b % 2], qT_lo[b % 2]
                for part, k in enumerate(slice(*p) for p in SCORE_PARTS):
                    if part == 1 and h == 0:
                        pe.wait_ge(kn_done, upto(g, b, 1, 1))
                    if part == 1 and h == 1 and not (first and b == 0):
                        pe.wait_ge(oT_done, upto(g, b, 1))
                    ins = three_pass(pe, slot(h)[:, k], qh[:, q], ql[:, q], kT_hi[:, k], kT_lo[:, k], True, True)
                ins.then_inc(scores_in_psum, 1)

            def probs_T(g, b, c):
                if c == 0:
                    pe.wait_ge(probs_done, upto(g, b, G, G))
                if c >= 2:
                    pe.wait_ge(pT_done, upto(g, b, KC, c - 1))
                for h in range(G):
                    ins = pe.transpose(bank([B_BANK, A_BANK][c % 2])[:, h * S:(h + 1) * S], probs[:, h, c * P:(c + 1) * P], ident[:])
                ins.then_inc(pT_in_psum, 1)

            def times_v(g, b, c):
                j = b % 2
                if c == 0:
                    pe.wait_ge(v_cache_done, upto(g, b, 1, 1))
                pe.wait_ge(pT_done, upto(g, b, KC, c + 1))
                three_pass(pe, bank(O_BANK), v_hi[j][:, c, :], v_lo[j][:, c, :], pT_hi[c % 3][:], pT_lo[c % 3][:], c == 0, c == KC - 1).then_inc(pv_done, 1)

            def output(g, b, hs):
                if hs[0] == 0:
                    pe.wait_ge(oT_done, upto(g, b, 1))
                for h in hs:
                    if b == 1:
                        pe.wait_ge(wo_done, g * WO_GROUPS + h + 1)
                    q = slice(h * S, (h + 1) * S)
                    ins = three_pass(pe, bank(KV_BANK), oT_hi[:, q], oT_lo[:, q], woT_hi[:, h, :], woT_lo[:, h, :], h == 0, h == G - 1)
                if h == G - 1:
                    ins.then_inc(y_in_psum, 1)

            for n in range(QKV_GROUPS):
                qkv_group(0, n)
            project_q(0, 0, range(DC), first=True)
            pe.wait_ge(wqkv_done, QKV_GROUPS)
            cached_keys(0, 0)
            project_kv(0, 0, first=True)
            queries(0, 0)
            project_q(0, 1, range(DC))
            new_keys(0, 0)

            def group(g, first, last):
                for b in range(B):
                    g1, b1 = following(g, b)
                    more, more2 = not (last and b == B - 1), not (last and b >= B - 2)

                    def weights(slot):
                        for n in weight_groups(b, slot, last):
                            if b < 2:
                                wo_group(g, n)
                            else:
                                qkv_group(g + 1, n)

                    def output_before(hs):
                        if not (first and b == 0):
                            output(g, b, hs)

                    def project_ahead(cs):
                        if more2:
                            project_q(*following(g1, b1), cs)

                    score(g, b, 0, first)
                    weights(0)
                    score(g, b, 1, first)
                    if more:
                        queries(g1, b1)
                    weights(1)
                    output_before(range(2))
                    weights(2)
                    score(g, b, 2, first)
                    score(g, b, 3, first)
                    weights(3)
                    output_before(range(2, G))
                    weights(4)
                    new_q = b == B - 2 and not last
                    if more:
                        if b == 1:
                            pe.wait_ge(wo_done, g * WO_GROUPS + WO_GROUPS)
                        if b >= B - 2 and not last:
                            pe.wait_ge(wqkv_done, (g + 1) * QKV_GROUPS + (DC - 1 if new_q else QKV_GROUPS - 1))
                        cached_keys(g1, b1)
                    if new_q:
                        project_kv(g1, b1)
                    else:
                        project_ahead(range(2))
                    if b == 0:
                        pe.wait_ge(wo_done, g * WO_GROUPS + 1)
                    if b >= B - 2 and not last:
                        pe.wait_ge(wqkv_done, (g + 1) * QKV_GROUPS + (DC if new_q else QKV_GROUPS))
                    probs_T(g, b, 0)
                    if more:
                        pe.wait_ge(kc_done, upto(g1, b1, 1, 1))
                    probs_T(g, b, 1)
                    if new_q:
                        project_ahead(range(2))
                    elif more:
                        project_kv(g1, b1)
                    times_v(g, b, 0)
                    probs_T(g, b, 2)
                    project_ahead(range(2, 3))
                    probs_T(g, b, 3)
                    times_v(g, b, 1)
                    probs_T(g, b, 4)
                    project_ahead(range(3, 4))
                    times_v(g, b, 2)
                    times_v(g, b, 3)
                    if more:
                        new_keys(g1, b1)
                    times_v(g, b, 4)

            group(0, True, False)
            with pe.Fori(1, HK - 1) as g:
                group(g, False, False)
            group(HK - 1, False, True)
            output(HK, 0, range(G))


def dense_signed(nc, x, w, bias, coeff, mask, x_out):
    with ExitStack() as ctx:
        def sb(name, shape, dt=F32):
            return ctx.enter_context(nc.sbuf_tensor("ds_" + name, shape, dt))

        def sem(name):
            return ctx.enter_context(nc.semaphore(name))

        ps = ctx.enter_context(nc.psum_tensor("ds_ps", [P, 8, NFREE], F32))
        X_BANK, OUT_BANK, W_BANK = 0, 2, 4

        ident = sb("ident", [P, P])
        w_raw = sb("w_raw", [P, DC, DM])
        wT = sb("wT", [P, DC, DM])
        bias_sb = sb("bias_sb", [P, DM])
        coeff_sb = sb("coeff_sb", [P, B])
        coeff2 = sb("coeff2", [P, B])
        neg_coeff = sb("neg_coeff", [P, B])
        x_raw = [sb(f"x_raw{j}", [P, DM]) for j in range(2)]
        x_bias = [sb(f"x_bias{j}", [P, DM]) for j in range(2)]
        mask_raw = [sb(f"mask_raw{j}", [P, DC, DM], I32) for j in range(2)]
        xT_hi = [sb(f"xT_hi{j}", [P, DC, S], F32R) for j in range(2)]
        xT_lo = [sb(f"xT_lo{j}", [P, DC, S], F32R) for j in range(2)]
        both = [sb(f"both{j}", [P, DC, DM]) for j in range(2)]
        m_hi = [sb(f"m_hi{j}", [P, DC, DM], F32R) for j in range(2)]
        m_lo = [sb(f"m_lo{j}", [P, DC, DM], F32R) for j in range(2)]
        result = sb("result", [P, B, DM])

        ident_step = sem("ds_ident_step")
        w_loaded = sem("ds_w_loaded")
        small_loaded = sem("ds_small_loaded")
        x_loaded = [sem(f"ds_x_loaded{j}") for j in range(2)]
        mask_loaded = [sem(f"ds_mask_loaded{j}") for j in range(2)]
        w_in_psum = sem("ds_w_in_psum")
        wT_done = sem("ds_wT_done")
        coeff_ready = sem("ds_coeff_ready")
        x_in_psum = sem("ds_x_in_psum")
        xT_hi_done = sem("ds_xT_hi_done")
        xT_done = sem("ds_xT_done")
        x_bias_done = sem("ds_x_bias_done")
        both_done = sem("ds_both_done")
        m_hi_done = sem("ds_m_hi_done")
        m_done = sem("ds_m_done")
        product_done = sem("ds_product_done")
        added = sem("ds_added")
        stored = sem("ds_stored")

        PAIRS = B // 2
        block = ctx.enter_context(nc.Block())

        @block.sync
        def _(sp):
            sp.dma_start(w_raw[:], w.rearrange("(c p) i -> p c i", p=P)).then_inc(w_loaded, 16)
            sp.dma_start(bias_sb[:], bias.rearrange("(o d) -> o d", o=1).broadcast_to([P, DM])).then_inc(small_loaded, 16)
            sp.dma_start(coeff_sb[:], coeff.rearrange("(o b) -> o b", o=1).broadcast_to([P, B])).then_inc(small_loaded, 16)

            def load_x(i, j):
                sp.dma_start(x_raw[j][:], x[bass.ds(i, 1)].rearrange("o s d -> (o s) d")).then_inc(x_loaded[j], 16)

            def load_mask(i, j):
                sp.dma_start(mask_raw[j][:], mask[bass.ds(i, 1)].rearrange("o (c p) n -> p (o c) n", p=P)).then_inc(mask_loaded[j], 16)

            for j in range(2):
                load_x(j, j)
                load_mask(j, j)
            with sp.Fori(0, PAIRS - 1) as p:
                for j in range(2):
                    sp.wait_ge(both_done, p * 2 + j + 1)
                    load_mask(p * 2 + j + 2, j)
                    sp.wait_ge(added, p * 2 + j + 1)
                    load_x(p * 2 + j + 2, j)
            for i in range(B):
                sp.wait_ge(added, i + 1)
                sp.dma_start(x_out[i], result[:, i, :]).then_inc(stored, 16)
            sp.wait_ge(stored, 16 * B)

        @block.gpsimd
        def _(pool):
            make_identity(nc, pool, ident[:], ident_step)
            pool.wait_ge(small_loaded, 32)
            pool.tensor_scalar(coeff2[:], coeff_sb[:], 2.0, None, ALU.mult).then_inc(coeff_ready, 1)
            pool.tensor_scalar(neg_coeff[:], coeff_sb[:], -1.0, None, ALU.mult).then_inc(coeff_ready, 1)
            with pool.Fori(0, PAIRS) as p:
                for j in range(2):
                    pool.wait_ge(x_loaded[j], p * 16 + 16)
                    pool.tensor_tensor(x_bias[j][:], x_raw[j][:], bias_sb[:], ALU.add).then_inc(x_bias_done, 1)

        @block.scalar
        def _(act):
            for c in range(DC):
                act.wait_ge(w_in_psum, c + 1)
                act.activation(wT[:, c, :], ps[:, W_BANK + c, :], ACT.Copy).then_inc(wT_done, 1)
            with act.Fori(0, PAIRS) as p:
                for j in range(2):
                    act.wait_ge(x_in_psum, p * 2 + j + 1)
                    act.activation(xT_hi[j][:].rearrange("p c s -> p (c s)"), ps[:, X_BANK + j, :], ACT.Copy).then_inc(xT_hi_done, 1)
                    act.wait_ge(both_done, p * 2 + j + 1)
                    act.activation(m_hi[j][:], both[j][:], ACT.Identity, bias=neg_coeff[:, bass.ds(p * 2 + j, 1)]).then_inc(m_hi_done, 1)

        @block.vector
        def _(dve):
            dve.wait_ge(coeff_ready, 2)
            dve.wait_ge(wT_done, DC)
            with dve.Fori(0, PAIRS) as p:
                for j in range(2):
                    at = bass.ds(p * 2 + j, 1)
                    dve.wait_ge(mask_loaded[j], p * 16 + 16)
                    dve.scalar_tensor_tensor(out=both[j][:].rearrange("p c n -> p (c n)"), in0=mask_raw[j][:].rearrange("p c n -> p (c n)"),
                                             scalar=coeff2[:, at], in1=wT[:].rearrange("p c n -> p (c n)"),
                                             op0=ALU.mult, op1=ALU.add).then_inc(both_done, 1)
                for j in range(2):
                    at = bass.ds(p * 2 + j, 1)
                    dve.wait_ge(xT_hi_done, p * 2 + j + 1)
                    dve.tensor_tensor(xT_lo[j][:].rearrange("p c s -> p (c s)"), ps[:, X_BANK + j, :],
                                      xT_hi[j][:].rearrange("p c s -> p (c s)").bitcast(F32), ALU.subtract).then_inc(xT_done, 1)
                    dve.wait_ge(m_hi_done, p * 2 + j + 1)
                    dve.scalar_tensor_tensor(out=m_lo[j][:].rearrange("p c n -> p (c n)"), in0=both[j][:].rearrange("p c n -> p (c n)"),
                                             scalar=neg_coeff[:, at], in1=m_hi[j][:].rearrange("p c n -> p (c n)").bitcast(F32),
                                             op0=ALU.add, op1=ALU.subtract).then_inc(m_done, 1)
                for j in range(2):
                    dve.wait_ge(product_done, p * 2 + j + 1)
                    dve.wait_ge(x_bias_done, p * 2 + j + 1)
                    dve.tensor_tensor(result[:, bass.ds(p * 2 + j, 1), :].rearrange("p o d -> p (o d)"), ps[:, OUT_BANK + j, :],
                                      x_bias[j][:], ALU.add).then_inc(added, 1)

        @block.tensor
        def _(pe):
            pe.wait_ge(ident_step, 2)
            pe.wait_ge(w_loaded, 16)
            for c in range(DC):
                for o in range(DC):
                    ins = pe.transpose(ps[:, W_BANK + c, o * P:(o + 1) * P], w_raw[:, o, c * P:(c + 1) * P], ident[:])
                ins.then_inc(w_in_psum, 1)
            with pe.Fori(0, PAIRS) as p:
                for j in range(2):
                    pe.wait_ge(x_loaded[j], p * 16 + 16)
                    for c in range(DC):
                        ins = pe.transpose(ps[:, X_BANK + j, c * S:(c + 1) * S], x_raw[j][:, c * P:(c + 1) * P], ident[:])
                    ins.then_inc(x_in_psum, 1)
                for j in range(2):
                    pe.wait_ge(xT_done, p * 2 + j + 1)
                    pe.wait_ge(m_done, p * 2 + j + 1)
                    for c in range(DC):
                        ins = three_pass(pe, ps[:, OUT_BANK + j, :], xT_hi[j][:, c, :], xT_lo[j][:, c, :],
                                         m_hi[j][:, c, :], m_lo[j][:, c, :], c == 0, c == DC - 1)
                    ins.then_inc(product_done, 1)


def swiglu_adapters(nc, x, w_gate, w_up, w_down, a_gate, b_gate, a_up, b_up, a_down, b_down, lora_idx, weight, ids, out):
    with ExitStack() as ctx:
        def sb(name, shape, dt=F32):
            return ctx.enter_context(nc.sbuf_tensor("sw_" + name, shape, dt))

        def sem(name):
            return ctx.enter_context(nc.semaphore("sw_" + name))

        ps = ctx.enter_context(nc.psum_tensor("sw_ps", [P, 8, NFREE], F32))
        ident = sb("ident", [P, P])
        gT_hi = sb("gT_hi", [P, DC, F], F32R)
        gT_lo = sb("gT_lo", [P, DC, F], F32R)
        uT_hi = sb("uT_hi", [P, DC, F], F32R)
        uT_lo = sb("uT_lo", [P, DC, F], F32R)
        dT_hi = sb("dT_hi", [P, FC, DM], F32R)
        dT_lo = sb("dT_lo", [P, FC, DM], F32R)
        ident_step = sem("ident_step")

        with ExitStack() as prep:
            raws = [prep.enter_context(nc.sbuf_tensor(f"sw_raw{m}", [P, FC, DM], F32)) for m in range(2)]
            down_raw = raws[0][:].rearrange("p c d -> p (c d)")[:, 0:DC * F].rearrange("p (c f) -> p c f", c=DC)
            raw_loaded = [sem(f"raw_loaded{m}") for m in range(3)]
            tile_in_psum = sem("tile_in_psum")
            tile_hi_done = sem("tile_hi_done")
            tile_done = sem("tile_done")
            tiles = [(m, c, n, k) for m in range(2) for c in range(DC) for n, k in FN] + [(2, c, 0, DM) for c in range(FC)]

            def place(t):
                m, c, n, k = tiles[t]
                rows = P if m < 2 or c < FC - 1 else FR
                hi, lo = ((gT_hi, gT_lo), (uT_hi, uT_lo), (dT_hi, dT_lo))[m]
                return hi[0:rows, c, n:n + k], lo[0:rows, c, n:n + k], ps[0:rows, t % 8, 0:k]

            block = prep.enter_context(nc.Block())

            @block.sync
            def _(sp):
                for m, w in enumerate((w_gate, w_up)):
                    sp.dma_start(raws[m][:, 0:FC - 1, :], w[0:(FC - 1) * P].rearrange("(c p) d -> p c d", p=P)).then_inc(raw_loaded[m], 16)
                    sp.dma_start(raws[m][0:FR, FC - 1, :], w[(FC - 1) * P:F]).then_inc(raw_loaded[m], 16)
                sp.wait_ge(tile_in_psum, DC * len(FN))
                sp.dma_start(down_raw, w_down.rearrange("(c p) f -> p c f", p=P)).then_inc(raw_loaded[2], 16)

            @block.gpsimd
            def _(pool):
                make_identity(nc, pool, ident[:], ident_step)

            @block.tensor
            def _(pe):
                pe.wait_ge(ident_step, 2)
                for t, (m, c, n, k) in enumerate(tiles):
                    if t % (DC * len(FN)) == 0:
                        pe.wait_ge(raw_loaded[m], 32 if m < 2 else 16) if t <= 2 * DC * len(FN) else None
                    if t >= 8:
                        pe.wait_ge(tile_done, t - 7)
                    for at in range(n, n + k, P):
                        cols = min(P, n + k - at)
                        if m < 2:
                            src = raws[m][0:cols, at // P, c * P:(c + 1) * P]
                            ins = pe.transpose(ps[:, t % 8, at - n:at - n + cols], src, ident[0:cols, 0:cols])
                        else:
                            rows = P if c < FC - 1 else FR
                            ins = pe.transpose(ps[0:rows, t % 8, at:at + P], down_raw[:, at // P, c * P:c * P + rows], ident[:])
                    ins.then_inc(tile_in_psum, 1)

            @block.scalar
            def _(act):
                for t in range(len(tiles)):
                    hi, _, src = place(t)
                    act.wait_ge(tile_in_psum, t + 1)
                    act.activation(hi, src, ACT.Copy).then_inc(tile_hi_done, 1)

            @block.vector
            def _(dve):
                for t in range(len(tiles)):
                    hi, lo, src = place(t)
                    dve.wait_ge(tile_hi_done, t + 1)
                    dve.tensor_tensor(lo, src, hi.bitcast(F32), ALU.subtract).then_inc(tile_done, 1)

        FPAD = FC * P
        REPS = 4
        R2 = 2 * REPS * RANK
        x_next = sb("x_next", [P, DM])
        x_res = sb("x_res", [P, DM])
        xT_hi = sb("xT_hi", [P, DC, S], F32R)
        xT_lo = sb("xT_lo", [P, DC, S], F32R)
        act_t = sb("act_t", [P, FPAD])
        actT_hi = sb("actT_hi", [P, FC, S], F32R)
        actT_lo = sb("actT_lo", [P, FC, S], F32R)
        agu_raw = sb("agu_raw", [R2, DM])
        bgu_raw = sb("bgu_raw", [P, FC, 2, RANK])
        ad_raw = sb("ad_raw", [RANK, FPAD])
        bd_raw = sb("bd_raw", [P, DC, RANK])
        bgu_rep = sb("bgu_rep", [P, FC, 2, REPS, RANK])
        bd_rep = sb("bd_rep", [P, DC, 2, RANK])
        aguT_hi = sb("aguT_hi", [P, DC, R2], F32R)
        aguT_lo = sb("aguT_lo", [P, DC, R2], F32R)
        tgu = sb("tgu", [R2, S], F32R)
        bguT = sb("bguT", [R2, F], F32R)
        T_LO = [slice(r, r + RANK) for r in (0, R2 // 2)]
        B_LO = [slice(r, r + RANK) for r in (2 * RANK, R2 // 2 + 2 * RANK)]
        adT = sb("adT", [P, FC, 2, RANK], F32R)
        td_hi = sb("td_hi", [2 * RANK, S], F32R)
        td_lo = sb("td_lo", [2 * RANK, S], F32R)
        bdT_hi = sb("bdT_hi", [2 * RANK, DM], F32R)
        bdT_lo = sb("bdT_lo", [2 * RANK, DM], F32R)
        w_raw = [sb(f"w_raw{j}", [P, DC, P]) for j in range(2)]
        wT_hi = sb("wT_hi", [P, DC, DM], F32R)
        wT_lo = sb("wT_lo", [P, DC, DM], F32R)
        zT_hi, zT_lo = aguT_hi, aguT_lo

        zeroed = sem("zeroed")
        repeated = sem("repeated")
        pool_passed = sem("pool_passed")
        sp_passed = sem("sp_passed")
        x_loaded = sem("x_loaded")
        lora_loaded = sem("lora_loaded")
        res_loaded = sem("res_loaded")
        w_loaded = [sem(f"w_loaded{j}") for j in range(2)]
        in_psum = sem("in_psum")
        hi_done = sem("hi_done")
        out_done = sem("out_done")
        gu_in_psum = sem("gu_in_psum")
        silu_done = sem("silu_done")
        act_done = sem("act_done")
        down_in_psum = sem("down_in_psum")
        pe_passed = sem("pe_passed")
        added = sem("added")
        product_done = sem("product_done")
        result_done = sem("result_done")
        stored = sem("stored")

        W0, W1, Z, W2, W3, ACT0, ACT1, X, AGU, BGU0, ACT2, BGU1, BGU2, TGU, TD, AD, BD = range(17)
        ADAPTER = [W0, W1, Z, W2, W3]
        AHEAD = [X, AGU, BGU0, BGU1, BGU2, TGU, AD, BD]
        FIRST = list(range(ACT0, BD + 1))
        TURN = ADAPTER + FIRST
        LAST = ADAPTER + [ACT0, ACT1, ACT2, TD]
        TAIL = ADAPTER
        BANKS = [4, 5, 7]
        DOWN_BANK = 6

        def before(i, turn):
            if turn is AHEAD:
                return 0
            if turn is FIRST:
                return len(AHEAD)
            if turn is TAIL:
                return before(B - 1, LAST) + len(LAST)
            return (i - 1) * len(TURN) + (len(AHEAD) + len(FIRST))

        def number(i, step, turn):
            return before(i, turn) + turn.index(step)

        def step_bank(step, turn):
            first = 0 if turn is not AHEAD else 1
            return BANKS[(first + turn.index(step)) % 3]

        def leaving(step, turn):
            bk = ps[:, step_bank(step, turn), :]
            flat = lambda t: t.rearrange("p c s -> p (c s)")

            def whole(src, hi, lo, scale=1.0):
                return src, hi, scale, [(src, hi, lo)]

            if step in (ACT0, ACT1, ACT2):
                n = [ACT0, ACT1, ACT2].index(step)
                cs = slice(4 * n, min(4 * n + 4, FC))
                return whole(bk[:, 0:(cs.stop - cs.start) * S], flat(actT_hi[:, cs, :]), flat(actT_lo[:, cs, :]))
            if step == X:
                return whole(bk, flat(xT_hi[:]), flat(xT_lo[:]))
            if step == Z:
                return whole(bk, flat(zT_hi[:]), flat(zT_lo[:]))
            if step in (W0, W1, W2, W3):
                c = [W0, W1, W2, W3].index(step)
                return whole(bk, wT_hi[:, c, :], wT_lo[:, c, :])
            if step == AGU:
                return whole(bk[:, 0:DC * R2], flat(aguT_hi[:]), flat(aguT_lo[:]))
            if step in (BGU0, BGU1, BGU2):
                n, k = FN[[BGU0, BGU1, BGU2].index(step)]
                at = slice(n, n + k)
                return bk[:, 0:k], bguT[:, at], 1.0, [(bk[r, 0:k], bguT[r, at], bguT[r, at]) for r in B_LO]
            if step == TGU:
                return bk[:, 0:S], tgu[:], LORA_SCALE, [(bk[r, 0:S], tgu[r, :], tgu[r, :]) for r in T_LO]
            if step == TD:
                return whole(bk[0:2 * RANK, 0:S], td_hi[:], td_lo[:], LORA_SCALE)
            if step == AD:
                return whole(bk[:, 0:FC * RANK].rearrange("p (c r) -> p c r", c=FC), adT[:, :, 0, :], adT[:, :, 1, :])
            return whole(bk[0:2 * RANK, :], bdT_hi[:], bdT_lo[:])

        block = ctx.enter_context(nc.Block())

        @block.sync
        def _(sp):
            def load_next(i):
                sp.dma_start(x_next[:], x[bass.ds(i, 1)].rearrange("o s d -> (o s) d")).then_inc(x_loaded, 16)
                r = sp.value_load(lora_idx.rearrange("(o b) -> o b", o=1)[:, bass.ds(i, 1)], min_val=0, max_val=15)
                for m, (a, b_) in enumerate(((a_gate, b_gate), (a_up, b_up))):
                    for n in range(REPS - 1):
                        at = (m * REPS + n) * RANK
                        sp.dma_start(agu_raw[at:at + RANK, :], a[0, bass.ds(r, 1)].rearrange("o r d -> (o r) d")).then_inc(lora_loaded, 16)
                    bb = b_[0, bass.ds(r, 1)].rearrange("o f r -> (o f) r")
                    sp.dma_start(bgu_raw[:, 0:FC - 1, m, :], bb[0:(FC - 1) * P].rearrange("(c p) r -> p c r", p=P)).then_inc(lora_loaded, 16)
                    sp.dma_start(bgu_raw[0:FR, FC - 1, m, :], bb[(FC - 1) * P:F]).then_inc(lora_loaded, 16)
                sp.dma_start(ad_raw[:, 0:F], a_down[0, bass.ds(r, 1)].rearrange("o r f -> (o r) f")).then_inc(lora_loaded, 16)
                sp.dma_start(bd_raw[:], b_down[0, bass.ds(r, 1)].rearrange("o (c p) r -> p (o c) r", p=P)).then_inc(lora_loaded, 16)

            def load_res(i):
                sp.dma_start(x_res[:], x[bass.ds(i, 1)].rearrange("o s d -> (o s) d")).then_inc(res_loaded, 16)

            def load_w(i, cs):
                a = sp.value_load(ids.rearrange("(o b) -> o b", o=1)[:, bass.ds(i, 1)], min_val=0, max_val=7)
                for c in cs:
                    w = weight[bass.ds(a, 1)].rearrange("o (c p) d -> p (o c) d", p=P)
                    sp.dma_start(w_raw[c % 2][:], w[:, :, c * P:(c + 1) * P]).then_inc(w_loaded[c % 2], 16)

            def store(i):
                sp.wait_ge(result_done, i + 1)
                sp.dma_start(out[bass.ds(i, 1)].rearrange("o s d -> (o s) d"), x_res[:]).then_inc(stored, 16)
                sp.wait_ge(stored, i * 16 + 16)

            def turn_loads(i, turn):
                sp.wait_ge(in_psum, before(i, turn))
                if turn is not LAST:
                    load_next(i + 1)
                wait_apart(sp, in_psum, number(i, W1, turn) + 1, sp_passed)
                load_w(i - 1, (2, 3))
                store(i - 1)
                load_res(i)
                load_w(i, (0, 1))

            sp.wait_ge(zeroed, 3)
            load_next(0)
            load_res(0)
            load_w(0, (0, 1))
            sp.wait_ge(in_psum, len(AHEAD))
            load_next(1)
            with sp.Fori(1, B - 1) as i:
                turn_loads(i, TURN)
            turn_loads(B - 1, LAST)
            sp.wait_ge(in_psum, number(B, W1, TAIL) + 1)
            load_w(B - 1, (2, 3))
            store(B - 1)

        @block.gpsimd
        def _(pool):
            pool.memset(agu_raw[:], 0.0).then_inc(zeroed, 1)
            pool.memset(bgu_raw[:], 0.0).then_inc(zeroed, 1)
            pool.memset(ad_raw[:], 0.0).then_inc(zeroed, 1)
            pool.memset(act_t[:, F:FPAD], 0.0).then_inc(zeroed, 1)

            def repeat_ranks(loaded):
                wait_apart(pool, lora_loaded, loaded * 192 + 192, pool_passed)
                for m in range(2):
                    pool.tensor_copy(bgu_rep[:, :, m, :, :], bgu_raw[:, :, m, :].unsqueeze(2).broadcast_to([P, FC, REPS, RANK])).then_inc(repeated, 1)
                pool.tensor_copy(bd_rep[:], bd_raw[:].unsqueeze(2).broadcast_to([P, DC, 2, RANK])).then_inc(repeated, 1)

            repeat_ranks(0)
            pool.wait_ge(in_psum, len(AHEAD))
            repeat_ranks(1)
            with pool.Fori(1, B - 1) as i:
                wait_apart(pool, in_psum, before(i, TURN), pool_passed)
                repeat_ranks(i + 1)

        @block.scalar
        def _(act):
            def hi(i, steps, turn):
                for step in steps:
                    if step in turn:
                        src, out_hi, scale, _ = leaving(step, turn)
                        act.wait_ge(in_psum, number(i, step, turn) + 1)
                        act.activation(out_hi, src, ACT.Copy, scale=scale).then_inc(hi_done, 1)

            def silu_of(i, n):
                at, k = FN[n]
                act.wait_ge(gu_in_psum, i * len(FN) + n + 1)
                act.activation(act_t[:, at:at + k], ps[:, 2 * (n % 2), 0:k], ACT.Silu).then_inc(silu_done, 1)

            def batch(i, turn):
                silu_of(i, 0)
                hi(i, (W0, W1, Z), turn)
                silu_of(i, 1)
                hi(i, (W2, W3, ACT0), turn)
                silu_of(i, 2)
                hi(i, (ACT1, X, AGU, BGU0, ACT2, BGU1, BGU2, TGU, TD, AD, BD), turn)

            hi(0, AHEAD, AHEAD)
            batch(0, FIRST)
            with act.Fori(1, B - 1) as i:
                batch(i, TURN)
            batch(B - 1, LAST)
            hi(B, TAIL, TAIL)

        @block.vector
        def _(dve):
            def lo(i, steps, turn):
                for step in steps:
                    if step in turn:
                        _, _, scale, parts = leaving(step, turn)
                        dve.wait_ge(hi_done, number(i, step, turn) + 1)
                        for src, h, out_lo in parts:
                            ins = dve.scalar_tensor_tensor(out=out_lo, in0=src, scalar=scale, in1=h.bitcast(F32), op0=ALU.mult, op1=ALU.subtract)
                        ins.then_inc(out_done, 1)

            def times_up(i, n):
                at, k = FN[n]
                dve.wait_ge(silu_done, i * len(FN) + n + 1)
                dve.tensor_tensor(act_t[:, at:at + k], ps[:, 2 * (n % 2) + 1, 0:k], act_t[:, at:at + k], ALU.mult).then_inc(act_done, 1)

            def finish(i):
                dve.wait_ge(product_done, i + 1)
                dve.tensor_tensor(x_res[:], ps[:, DOWN_BANK, :], x_res[:], ALU.add).then_inc(result_done, 1)

            def batch(i, turn):
                times_up(i, 0)
                lo(i, (W0, W1, Z), turn)
                times_up(i, 1)
                lo(i, (W2, W3, ACT0), turn)
                times_up(i, 2)
                lo(i, (ACT1,), turn)
                if turn is not FIRST:
                    finish(i - 1)
                lo(i, (X, AGU, BGU0, ACT2, BGU1, BGU2, TGU, TD, AD), turn)
                dve.wait_ge(down_in_psum, i + 1)
                dve.wait_ge(res_loaded, i * 16 + 16)
                dve.tensor_tensor(x_res[:], ps[:, DOWN_BANK, :], x_res[:], ALU.add).then_inc(added, 1)
                lo(i, (BD,), turn)

            dve.wait_ge(zeroed, 4)
            lo(0, AHEAD, AHEAD)
            batch(0, FIRST)
            with dve.Fori(1, B - 1) as i:
                batch(i, TURN)
            batch(B - 1, LAST)
            lo(B, TAIL, TAIL)
            finish(B - 1)

        @block.tensor
        def _(pe):
            def parts_done(i, step, turn):
                pe.wait_ge(out_done, number(i, step, turn) + 1)

            def free_bank(i, step, turn):
                k = turn.index(step)
                if turn is not AHEAD or k >= 3:
                    wait_apart(pe, out_done, number(i, step, turn) - (2 if k >= 2 else 1), pe_passed)

            def act_transposed(i, step, turn):
                n = [ACT0, ACT1, ACT2].index(step)
                pe.wait_ge(act_done, i * len(FN) + n + 1)
                free_bank(i, step, turn)
                bk = ps[:, step_bank(step, turn), :]
                for c in range(4 * n, min(4 * n + 4, FC)):
                    ins = pe.transpose(bk[:, (c - 4 * n) * S:(c - 4 * n + 1) * S], act_t[:, c * P:(c + 1) * P], ident[:])
                ins.then_inc(in_psum, 1)

            def next_transposed(i, step, turn, loaded):
                if step == X:
                    pe.wait_ge(x_loaded, loaded * 16 + 16)
                if step == AGU:
                    pe.wait_ge(lora_loaded, loaded * 192 + 192)
                if step in (BGU0, BD):
                    pe.wait_ge(repeated, loaded * 3 + 3)
                free_bank(i, step, turn)
                bk = ps[:, step_bank(step, turn), :]
                if step == X:
                    for c in range(DC):
                        ins = pe.transpose(bk[:, c * S:(c + 1) * S], x_next[:, c * P:(c + 1) * P], ident[:])
                elif step == AGU:
                    for c in range(DC):
                        ins = pe.transpose(bk[:, c * R2:(c + 1) * R2], agu_raw[:, c * P:(c + 1) * P], ident[0:R2, 0:R2])
                elif step in (BGU0, BGU1, BGU2):
                    n, k = FN[[BGU0, BGU1, BGU2].index(step)]
                    for at in range(n, n + k, P):
                        rows = min(P, F - at)
                        src = bgu_rep[0:rows, at // P].rearrange("p m t r -> p (m t r)")
                        ins = pe.transpose(bk[:, at - n:at - n + rows], src, ident[0:rows, 0:rows])
                elif step == AD:
                    for c in range(FC):
                        ins = pe.transpose(bk[:, c * RANK:(c + 1) * RANK], ad_raw[:, c * P:(c + 1) * P], ident[0:RANK, 0:RANK])
                else:
                    for c in range(DC):
                        src = bd_rep[:, c].rearrange("p t r -> p (t r)")
                        ins = pe.transpose(bk[0:2 * RANK, c * P:(c + 1) * P], src, ident[:])
                ins.then_inc(in_psum, 1)

            def adapter_transposed(i, step, turn):
                c = [W0, W1, W2, W3].index(step) if step != Z else 0
                if step == Z:
                    pe.wait_ge(added, i)
                else:
                    pe.wait_ge(w_loaded[c % 2], (i - 1) * 32 + (c // 2 + 1) * 16)
                free_bank(i, step, turn)
                bk = ps[:, step_bank(step, turn), :]
                for n in range(DC):
                    src = x_res[:, n * P:(n + 1) * P] if step == Z else w_raw[c % 2][:, n, :]
                    ins = pe.transpose(bk[:, n * P:(n + 1) * P], src, ident[:])
                ins.then_inc(in_psum, 1)

            def adapter_product(i, turn):
                parts_done(i, W3, turn)
                for c in range(DC):
                    ins = three_pass(pe, ps[:, DOWN_BANK, :], zT_hi[:, c, :], zT_lo[:, c, :], wT_hi[:, c, :], wT_lo[:, c, :],
                                     c == 0, c == DC - 1)
                ins.then_inc(product_done, 1)

            def into_ranks(i, turn):
                parts_done(i, AGU, turn)
                free_bank(i, TGU, turn)
                for c in range(DC):
                    ins = three_pass(pe, ps[:, step_bank(TGU, turn), 0:S], aguT_hi[:, c, :], aguT_lo[:, c, :],
                                     xT_hi[:, c, :], xT_lo[:, c, :], c == 0, c == DC - 1)
                ins.then_inc(in_psum, 1)

            def gate_up(i, n):
                at, k = FN[n]
                cols = slice(at, at + k)
                if n == 2:
                    pe.wait_ge(act_done, i * len(FN) + 1)
                for m, (wh, wl) in enumerate(((gT_hi, gT_lo), (uT_hi, uT_lo))):
                    bk = ps[:, 2 * (n % 2) + m, 0:k]
                    for c in range(DC):
                        three_pass(pe, bk, xT_hi[:, c, :], xT_lo[:, c, :], wh[:, c, cols], wl[:, c, cols], c == 0, False)
                    r = slice(m * (R2 // 2), (m + 1) * (R2 // 2))
                    ins = pe.matmul(bk, tgu[r, :], bguT[r, cols], start=False, stop=True)
                ins.then_inc(gu_in_psum, 1)

            def batch(i, turn):
                gate_up(i, 0)
                if turn is not FIRST:
                    for step in (W0, W1, Z):
                        adapter_transposed(i, step, turn)
                gate_up(i, 1)
                if turn is not FIRST:
                    for step in (W2, W3):
                        adapter_transposed(i, step, turn)
                act_transposed(i, ACT0, turn)
                gate_up(i, 2)
                act_transposed(i, ACT1, turn)
                if turn is not FIRST:
                    adapter_product(i, turn)
                if turn is not LAST:
                    for step in (X, AGU, BGU0):
                        next_transposed(i, step, turn, i + 1)
                act_transposed(i, ACT2, turn)
                if turn is not LAST:
                    for step in (BGU1, BGU2):
                        next_transposed(i, step, turn, i + 1)
                    into_ranks(i, turn)
                parts_done(i, ACT2, turn)
                free_bank(i, TD, turn)
                for c in range(FC):
                    rows = P if c < FC - 1 else FR
                    ranks = adT[0:rows, c, :, :].rearrange("p t r -> p (t r)")
                    at = ps[0:2 * RANK, step_bank(TD, turn), 0:S]
                    pe.matmul(at, ranks, actT_hi[0:rows, c, :], start=c == 0, stop=False)
                    ins = pe.matmul(at, ranks, actT_lo[0:rows, c, :], start=False, stop=c == FC - 1)
                ins.then_inc(in_psum, 1)
                if turn is not FIRST:
                    pe.wait_ge(result_done, i)
                for c in range(FC):
                    rows = P if c < FC - 1 else FR
                    three_pass(pe, ps[:, DOWN_BANK, :], actT_hi[0:rows, c, :], actT_lo[0:rows, c, :],
                               dT_hi[0:rows, c, :], dT_lo[0:rows, c, :], c == 0, False)
                if turn is not LAST:
                    next_transposed(i, AD, turn, i + 1)
                parts_done(i, TD, turn)
                three_pass(pe, ps[:, DOWN_BANK, :], td_hi[:], td_lo[:], bdT_hi[:], bdT_lo[:], False, True).then_inc(down_in_psum, 1)
                if turn is not LAST:
                    next_transposed(i, BD, turn, i + 1)

            for step in AHEAD:
                if step == TGU:
                    into_ranks(0, AHEAD)
                else:
                    next_transposed(0, step, AHEAD, 0)
            pe.wait_ge(out_done, len(AHEAD))
            batch(0, FIRST)
            with pe.Fori(1, B - 1) as i:
                pe.wait_ge(out_done, before(i, TURN))
                batch(i, TURN)
            pe.wait_ge(out_done, before(B - 1, LAST))
            batch(B - 1, LAST)
            for step in TAIL:
                adapter_transposed(B, step, TAIL)
            adapter_product(B, TAIL)


_INS = ["x", "itok_Bx16_0_63", "itok_B_207_1644", "condB_coeff", "itok_B_2_6", "itok_B_3_7", "mask_Bx4096x4096_ik1",
        "L0_cond_Wq", "L0_cond_Wk", "L0_cond_Wv", "L0_cond_Wo", "L0_cond_q_norm_w", "L0_cond_k_norm_w",
        "L0_cond_k_cache", "L0_cond_v_cache", "L1_cond_W", "L1_cond_b", "L2_cond_W_gate", "L2_cond_W_up", "L2_cond_W_down",
        "L2_cond_A_gate", "L2_cond_B_gate", "L2_cond_A_up", "L2_cond_B_up", "L2_cond_A_down", "L2_cond_B_down",
        "L3_cond_weight"]


def kernel(**inputs):
    import concourse.bacc as bacc
    from concourse.bass_utils import run_bass_kernel_spmd

    nc = bacc.Bacc("TRN2", target_bir_lowering=False, num_devices=1)
    arrays, t = {}, {}
    for name in _INS:
        a = np.ascontiguousarray(inputs[name])
        arrays[f"in_{name}"] = a
        t[name] = nc.dram_tensor(f"in_{name}", a.shape, mybir.dt.from_np(a.dtype), kind="ExternalInput").ap()
    inv = (1.0 / np.power(np.float32(THETA), np.arange(0, D, 2, dtype=np.float32) / np.float32(D))).astype(np.float32)
    arrays["inv_freq"] = inv
    inv_freq = nc.dram_tensor("inv_freq", inv.shape, F32, kind="ExternalInput").ap()
    stage = [nc.dram_tensor(f"x_stage{n}", (B, S, DM), F32).ap() for n in range(2)]
    out = nc.dram_tensor("out", (B, S, DM), F32, kind="ExternalOutput").ap()

    attention(nc, t["x"], t["itok_Bx16_0_63"], t["itok_B_207_1644"], t["L0_cond_Wq"], t["L0_cond_Wk"], t["L0_cond_Wv"],
              t["L0_cond_Wo"], t["L0_cond_q_norm_w"], t["L0_cond_k_norm_w"], t["L0_cond_k_cache"], t["L0_cond_v_cache"],
              inv_freq, stage[0])
    dense_signed(nc, stage[0], t["L1_cond_W"], t["L1_cond_b"], t["condB_coeff"], t["mask_Bx4096x4096_ik1"], stage[1])
    swiglu_adapters(nc, stage[1], *[t[f"L2_cond_{n}"] for n in ("W_gate", "W_up", "W_down", "A_gate", "B_gate", "A_up", "B_up", "A_down", "B_down")],
                    t["itok_B_2_6"], t["L3_cond_weight"], t["itok_B_3_7"], out)
    r = run_bass_kernel_spmd(nc, [arrays], core_ids=[0])
    return r.results[0]["out"]
```

```python
from contextlib import ExitStack

import numpy as np

import concourse.bass as bass
from concourse import mybir

F32 = mybir.dt.float32
F32R = mybir.dt.float32r
BF16 = mybir.dt.bfloat16
I32 = mybir.dt.int32
U32 = mybir.dt.uint32
ALU = mybir.AluOpType
ACT = mybir.ActivationFunctionType

P = 128
B, S, DM = 8, 128, 512
DC = DM // P
D = 128
HK, G = 8, 4
PAGES, PSIZE, NPP = 64, 32, 16
L = NPP * PSIZE
LC = L // P
KEYS = L + S
KC = KEYS // P
EPS = 1e-6
SCALE = D ** -0.5
THETA = 10000.0
MASKED = 1e30
F = 1376
FC = -(-F // P)
FR = F - (FC - 1) * P
NFREE = 512
FN = [(n, min(NFREE, F - n)) for n in range(0, F, NFREE)]
RANK = 16
UP0 = 32
LORA_SCALE = 0.5

TWO_PI = 2 * np.pi
PI_A = 6.28125
PI_B = float(np.float32(np.round((TWO_PI - PI_A) * 2 ** 20) / 2 ** 20))
PI_C = float(np.float32(TWO_PI - PI_A - PI_B))
PI_F32 = 3.1415925
ROUND = 1.5 * 2 ** 23


def three_pass(pe, out, l_hi, l_lo, r_hi, r_lo, first, last):
    pe.matmul(out, l_hi, r_hi, start=first, stop=False)
    pe.matmul(out, l_hi, r_lo, start=False, stop=False)
    return pe.matmul(out, l_lo, r_hi, start=False, stop=last)


def wait_apart(eng, sem, count, passed):
    eng.wait_ge(sem, count)
    if not isinstance(count, int):
        eng.sem_inc(passed, 1)


def make_identity(nc, pool, ident, step):
    pool.memset(ident, 0.0).then_inc(step, 1)
    pool.wait_ge(step, 1)
    pool.affine_select(out=ident, in_=ident, compare_op=ALU.not_equal, fill=1.0, base=0,
                       pattern=[[-1, P]], channel_multiplier=1).then_inc(step, 1)


def attention(nc, x, block_table, seqlens, wq, wk, wv, wo, qw, kw, k_cache, v_cache, inv_freq, ident, xres, wq_raw, dense_w, dense_w_staged):
    with ExitStack() as ctx:
        def sb(name, shape, dt=F32):
            return ctx.enter_context(nc.sbuf_tensor("at_" + name, shape, dt))

        def sem(name):
            return ctx.enter_context(nc.semaphore(name))

        ps = ctx.enter_context(nc.psum_tensor("at_ps", [P, 8 * NFREE], F32))

        def bank(n, cols=NFREE):
            return ps[:, n * NFREE:n * NFREE + cols]

        SCORE_PARTS = [(0, KEYS // 2), (KEYS // 2, KEYS)]

        def slot(h):
            at = 2 * (h % 2) * NFREE + NFREE - SCORE_PARTS[1][0]
            return ps[:, at:at + KEYS]

        Q_BANK, KV_BANK, A_BANK, B_BANK, O_BANK = 4, 5, 6, 7, 3

        xT_hi = sb("xT_hi", [P, DC, B * S], F32R)
        xT_lo = sb("xT_lo", [P, DC, B * S], F32R)
        wkv_raw = sb("wkv_raw", [P, 2, DM])
        wo_raw = sb("wo_raw", [P, DC, G * D])
        wqT_hi = sb("wqT_hi", [P, DC, G * D], F32R)
        wqT_lo = sb("wqT_lo", [P, DC, G * D], F32R)
        wkvT_hi = sb("wkvT_hi", [P, DC, 2 * D], F32R)
        wkvT_lo = sb("wkvT_lo", [P, DC, 2 * D], F32R)
        woT_hi = sb("woT_hi", [P, G, DM], F32R)
        woT_lo = sb("woT_lo", [P, G, DM], F32R)
        q_cos = sb("q_cos", [P, B, D])
        q_sin = sb("q_sin", [P, B, D])
        k_cos = sb("k_cos", [P, B, D])
        k_sin = sb("k_sin", [P, B, D])
        mask = sb("mask", [P, B, KEYS], BF16)
        k_raw = [sb(f"k_raw{j}", [P, LC, D]) for j in range(2)]
        v_raw = [sb(f"v_raw{j}", [P, LC, D]) for j in range(2)]
        kT_hi = sb("kT_hi", [P, KEYS], F32R)
        kT_lo = sb("kT_lo", [P, KEYS], F32R)
        v_hi = [sb(f"v_hi{j}", [P, KC, D], F32R) for j in range(2)]
        v_lo = [sb(f"v_lo{j}", [P, KC, D], F32R) for j in range(2)]
        qT_hi = [sb(f"qT_hi{j}", [P, G * S], F32R) for j in range(2)]
        qT_lo = [sb(f"qT_lo{j}", [P, G * S], F32R) for j in range(2)]
        u_q = sb("u_q", [P, G, D])
        w_q = sb("w_q", [P, G, D])
        q_rot = sb("q_rot", [P, G, D])
        u_k = sb("u_k", [P, D])
        w_k = sb("w_k", [P, D])
        k_rot = sb("k_rot", [P, D])
        square = sb("square", [P, G + 1, D])
        sumsq = [sb(f"sumsq{j}", [P, G + 1]) for j in range(2)]
        d_eps = sb("d_eps", [P, G])
        minus_half = sb("minus_half", [P, G])
        inv_rms = [sb(f"inv_rms{j}", [P, G + 1]) for j in range(2)]
        scores = [sb(f"scores{j}", [P, KEYS]) for j in range(2)]
        neg_max = sb("neg_max", [P, G])
        row_sum = sb("row_sum", [P, G])
        row_inv = sb("row_inv", [P, G])
        probs = sb("probs", [P, G, KEYS])
        pT_hi = [sb(f"pT_hi{j}", [P, G * S], F32R) for j in range(3)]
        pT_lo = [sb(f"pT_lo{j}", [P, G * S], F32R) for j in range(3)]
        oT_hi = sb("oT_hi", [P, G * S], F32R)
        oT_lo = sb("oT_lo", [P, G * S], F32R)
        key_row = sb("key_row", [P, B * LC])
        key_idx = [sb(f"key_idx{j}", [P, LC], U32) for j in range(2)]
        head_no = sb("head_no", [P, 1])
        seq_i = sb("seq_i", [P, B], I32)
        seq_f = sb("seq_f", [P, B])
        in_page_f = sb("in_page_f", [P, 1])
        tok_i = sb("tok_i", [P, 1], I32)
        tok_f = sb("tok_f", [P, 1])
        HALF = D // 2
        qw_sb, kw_sb, invf_sb = u_q[:, 0, :], u_q[:, 1, :], u_q[:, 2, 0:HALF]
        table_sb = u_q[:, 3, 0:B * NPP].bitcast(I32)
        angle = probs[:, 0, 0:B * HALF]
        turns = probs[:, 1, 0:B * HALF]
        sin_t = probs[:, 2, 0:B * HALF]
        cos_t = probs[:, 3, 0:B * HALF]
        key_no_i = scores[0][:, 0:L].bitcast(I32)
        key_no = scores[1][:, 0:L]

        x_loaded = [sem(f"x_loaded{n}") for n in range(2)]
        small_loaded = sem("small_loaded")
        ident_step = sem("ident_step")
        iota_done = sem("iota_done")
        table_step = sem("table_step")
        angles_ready = sem("angles_ready")
        sincos_ready = sem("sincos_ready")
        tables_ready = sem("tables_ready")
        rows_ready = sem("rows_ready")
        xT_in_psum = sem("xT_in_psum")
        xT_hi_done = sem("xT_hi_done")
        xT_done = sem("xT_done")
        wqkv_loaded = sem("wqkv_loaded")
        wo_loaded = sem("wo_loaded")
        wqkv_in_psum = sem("wqkv_in_psum")
        wqkv_hi_done = sem("wqkv_hi_done")
        wqkv_done = sem("wqkv_done")
        wo_in_psum = sem("wo_in_psum")
        wo_hi_done = sem("wo_hi_done")
        wo_done = sem("wo_done")
        idx_ready = sem("idx_ready")
        head_step = sem("head_step")
        k_loaded = [sem(f"k_loaded{j}") for j in range(2)]
        v_loaded = [sem(f"v_loaded{j}") for j in range(2)]
        q_in_psum = sem("q_in_psum")
        kv_in_psum = sem("kv_in_psum")
        q_turned = sem("q_turned")
        q_squared = sem("q_squared")
        q_rot_done = sem("q_rot_done")
        kv_read = sem("kv_read")
        k_turned = sem("k_turned")
        v_new_done = sem("v_new_done")
        k_rot_done = sem("k_rot_done")
        scale_ready = sem("scale_ready")
        k_scale_ready = sem("k_scale_ready")
        v_hi_done = sem("v_hi_done")
        v_cache_done = sem("v_cache_done")
        kc_in_psum = sem("kc_in_psum")
        kc_hi_done = sem("kc_hi_done")
        kc_done = sem("kc_done")
        kn_in_psum = sem("kn_in_psum")
        kn_hi_done = sem("kn_hi_done")
        kn_done = sem("kn_done")
        qT_in_psum = sem("qT_in_psum")
        qT_hi_done = sem("qT_hi_done")
        qT_done = sem("qT_done")
        scores_in_psum = sem("scores_in_psum")
        scores_done = sem("scores_done")
        exp_done = sem("exp_done")
        inv_done = sem("inv_done")
        probs_done = sem("probs_done")
        pT_in_psum = sem("pT_in_psum")
        pT_hi_done = sem("pT_hi_done")
        pT_done = sem("pT_done")
        pv_done = sem("pv_done")
        oT_hi_done = sem("oT_hi_done")
        oT_done = sem("oT_done")
        y_in_psum = sem("y_in_psum")
        y_bank_free = sem("y_bank_free")
        pool_passed = sem("pool_passed")
        dve_passed = sem("dve_passed")

        QKV_GROUPS, WO_GROUPS = DC + DC // 2, G
        WEIGHT_BANKS = [A_BANK, B_BANK]

        def upto(g, b, per, k=0):
            return g * (B * per) + (b * per + k)

        def following(g, b):
            return (g, b + 1) if b + 1 < B else (g + 1, 0)

        def weight_groups(b, slot, last):
            groups = {0: {4: [0]}, 1: {0: [1], 1: [2], 2: [3]}}
            if not last:
                groups[B - 2] = {0: [0], 1: [1], 2: [2], 3: [3]}
                groups[B - 1] = {0: [4], 1: [5]}
            return groups.get(b, {}).get(slot, [])

        block = ctx.enter_context(nc.Block())

        @block.sync
        def _(sp):
            sp.dma_start(seq_i[:], seqlens.rearrange("(o b) -> o b", o=1).broadcast_to([P, B])).then_inc(small_loaded, 16)
            sp.dma_start(table_sb, block_table.rearrange("(o b) n -> o (b n)", o=1).broadcast_to([P, B * NPP])).then_inc(small_loaded, 16)
            sp.dma_start(qw_sb, qw.rearrange("(o d) -> o d", o=1).broadcast_to([P, D])).then_inc(small_loaded, 16)
            sp.dma_start(kw_sb, kw.rearrange("(o d) -> o d", o=1).broadcast_to([P, D])).then_inc(small_loaded, 16)
            sp.dma_start(invf_sb, inv_freq.rearrange("(o d) -> o d", o=1).broadcast_to([P, HALF])).then_inc(small_loaded, 16)

            def load_qkv(g):
                sp.dma_start(wq_raw[:], wq[bass.ds(g * (G * D), G * D), :].rearrange("(e p) d -> p e d", p=P)).then_inc(wqkv_loaded, 16)
                sp.dma_start(wkv_raw[:, 0, :], wk[bass.ds(g * D, D), :]).then_inc(wqkv_loaded, 16)
                sp.dma_start(wkv_raw[:, 1, :], wv[bass.ds(g * D, D), :]).then_inc(wqkv_loaded, 16)

            def load_wo(g):
                sp.dma_start(wo_raw[:], wo[:, bass.ds(g * (G * D), G * D)].rearrange("(n p) e -> p n e", p=P)).then_inc(wo_loaded, 16)

            for n, part in enumerate((slice(0, 2), slice(2, B))):
                sp.dma_start(xres[:, part, :], x[part].rearrange("b s d -> s b d")).then_inc(x_loaded[n], 16)
                if n == 0:
                    load_qkv(0)
            load_wo(0)
            with sp.Fori(0, HK - 1) as g:
                sp.wait_ge(wqkv_in_psum, g * QKV_GROUPS + QKV_GROUPS)
                sp.wait_ge(wo_in_psum, g * WO_GROUPS + WO_GROUPS)
                load_qkv(g + 1)
                load_wo(g + 1)
            sp.wait_ge(wqkv_in_psum, HK * QKV_GROUPS)
            sp.dma_start(wq_raw[:], dense_w.rearrange("(c p) i -> p c i", p=P)).then_inc(dense_w_staged, 16)

        @block.gpsimd
        def _(pool):
            make_identity(nc, pool, ident[:], ident_step)
            pool.wait_ge(ident_step, 2)
            pool.iota(tok_i[:], pattern=[[0, 1]], base=0, channel_multiplier=1).then_inc(iota_done, 1)
            pool.iota(key_no_i, pattern=[[1, L]], base=0, channel_multiplier=0).then_inc(iota_done, 1)
            pool.memset(d_eps[:], D * EPS).then_inc(iota_done, 1)
            pool.memset(minus_half[:], -0.5).then_inc(iota_done, 1)
            pool.memset(head_no[:], 0.0).then_inc(head_step, 1)
            pool.memset(mask[:, :, L:KEYS], 0.0).then_inc(iota_done, 1)

            def indices(b):
                return pool.tensor_scalar(key_idx[b % 2][:], key_row[:, b * LC:(b + 1) * LC], head_no[:, 0:1], None, ALU.add)

            def gather(b, cs, cache, raw, loaded):
                for c in cs:
                    pool.indirect_dma_start(
                        out=raw[b % 2][:, c, :], out_offset=None,
                        in_=cache.rearrange("a r h d -> (a r h) d"),
                        in_offset=bass.IndirectOffsetOnAxis(ap=key_idx[b % 2][:, c:c + 1], axis=0),
                    ).then_inc(loaded[b % 2], 16)

            def next_head(g):
                wait_apart(pool, idx_ready, upto(g, B - 1, 1, 1), pool_passed)
                pool.tensor_scalar(head_no[:], head_no[:], 1.0, None, ALU.add).then_inc(head_step, 1)

            def start_gather(g, b):
                wait_apart(pool, head_step, g + 1, pool_passed)
                indices(b).then_inc(idx_ready, 1)
                wait_apart(pool, idx_ready, upto(g, b, 1, 1), pool_passed)

            def rotate_k(g, b):
                pool.wait_ge(k_turned, upto(g, b, 1, 1))
                pool.tensor_tensor(k_rot[:, 0:HALF], u_k[:, 0:HALF], w_k[:, HALF:D], ALU.subtract)
                pool.tensor_tensor(k_rot[:, HALF:D], u_k[:, HALF:D], w_k[:, 0:HALF], ALU.add).then_inc(k_rot_done, 1)

            def rotate_q(g, b):
                pool.wait_ge(q_turned, upto(g, b, 1, 1))
                pool.tensor_tensor(q_rot[:, :, 0:HALF], u_q[:, :, 0:HALF], w_q[:, :, HALF:D], ALU.subtract)
                pool.tensor_tensor(q_rot[:, :, HALF:D], u_q[:, :, HALF:D], w_q[:, :, 0:HALF], ALU.add).then_inc(q_rot_done, 1)

            def key_scale(g, b):
                j = b % 2
                pool.wait_ge(kv_read, upto(g, b, 1, 1))
                pool.tensor_tensor(inv_rms[j][:, G:G + 1], sumsq[j][:, G:G + 1], d_eps[:, 0:1], ALU.add).then_inc(k_scale_ready, 1)
                pool.wait_ge(k_scale_ready, upto(g, b, 2, 1))
                pool.tensor_tensor(inv_rms[j][:, G:G + 1], inv_rms[j][:, G:G + 1], minus_half[:, 0:1], ALU.pow).then_inc(k_scale_ready, 1)

            def query_scale(g, b):
                j = b % 2
                pool.wait_ge(q_squared, upto(g, b, 1, 1))
                pool.tensor_tensor(inv_rms[j][:, 0:G], sumsq[j][:, 0:G], d_eps[:], ALU.add).then_inc(scale_ready, 1)
                pool.wait_ge(scale_ready, upto(g, b, 2, 1))
                pool.tensor_tensor(inv_rms[j][:, 0:G], inv_rms[j][:, 0:G], minus_half[:], ALU.pow).then_inc(scale_ready, 1)

            def normalise(g, b, h):
                wait_apart(pool, inv_done, upto(g, b, G, h + 1), pool_passed)
                pool.tensor_scalar(probs[:, h, :], probs[:, h, :], row_inv[:, h:h + 1], 1.0, ALU.mult, ALU.mult).then_inc(probs_done, 1)

            pool.wait_ge(iota_done, 5)
            pool.wait_ge(rows_ready, 4)
            for b in range(2):
                start_gather(0, b)
                gather(b, range(LC), k_cache, k_raw, k_loaded)
                if b == 0:
                    gather(b, range(LC), v_cache, v_raw, v_loaded)
            rotate_q(0, 0)
            key_scale(0, 0)
            rotate_k(0, 0)
            query_scale(0, 0)
            rotate_q(0, 1)
            gather(1, range(LC), v_cache, v_raw, v_loaded)

            def group(g, last):
                for b in range(B):
                    g1, b1 = following(g, b)
                    g2, b2 = following(g1, b1)
                    more, more2 = not (last and b == B - 1), not (last and b >= B - 2)

                    def keys(cs):
                        if more2:
                            gather(b2, cs, k_cache, k_raw, k_loaded)

                    def values(cs):
                        if more2:
                            gather(b2, cs, v_cache, v_raw, v_loaded)

                    if more2:
                        if b2 == 0:
                            next_head(g)
                        pool.wait_ge(kc_in_psum, upto(g, b, 1, 1))
                        pool.wait_ge(v_cache_done, upto(g, b, 1, 1))
                        start_gather(g2, b2)
                    values(range(1))
                    for h in range(G):
                        normalise(g, b, h)
                    values(range(1, LC))
                    if more:
                        query_scale(g1, b1)
                        key_scale(g1, b1)
                        rotate_k(g1, b1)
                    keys(range(2))
                    if more2:
                        rotate_q(g2, b2)
                    keys(range(2, LC))

            with pool.Fori(0, HK - 1) as g:
                group(g, False)
            group(HK - 1, True)

        @block.scalar
        def _(act):
            def tokens(b):
                act.wait_ge(xT_in_psum, b + 1)
                act.activation(xT_hi[:, :, b * S:(b + 1) * S], bank(b % 4).rearrange("p (c s) -> p c s", c=DC), ACT.Copy).then_inc(xT_hi_done, 1)

            tokens(0)
            tokens(1)
            for j, t in ((0, sin_t), (1, cos_t)):
                act.wait_ge(angles_ready, j + 1)
                act.activation(t, t, ACT.Sin).then_inc(sincos_ready, 1)

            def hi(out, src, ready, count, done):
                act.wait_ge(ready, count)
                act.activation(out, src, ACT.Copy).then_inc(done, 1)

            def qkv_group(g, n):
                out = wqT_hi[:, n, :] if n < DC else wkvT_hi[:, 2 * (n - DC):2 * (n - DC) + 2, :].rearrange("p c e -> p (c e)")
                hi(out, bank(WEIGHT_BANKS[n % 2]), wqkv_in_psum, g * QKV_GROUPS + n + 1, wqkv_hi_done)

            def wo_group(g, n):
                hi(woT_hi[:, n, :], bank(WEIGHT_BANKS[(n + 1) % 2]), wo_in_psum, g * WO_GROUPS + n + 1, wo_hi_done)

            def cached_values(g, b):
                j = b % 2
                hi(v_hi[j][:, 0:LC, :], v_raw[j][:], v_loaded[j], g * (B // 2 * LC * 16) + (b // 2 + 1) * LC * 16, v_hi_done)

            def cached_keys(g, b):
                hi(kT_hi[:, 0:L], bank(A_BANK), kc_in_psum, upto(g, b, 1, 1), kc_hi_done)

            def new_kv(g, b):
                j = b % 2
                act.wait_ge(kv_in_psum, upto(g, b, 1, 1))
                act.activation(square[:, G, :], bank(KV_BANK, D), ACT.Square, accum_out=sumsq[j][:, G:G + 1])
                act.activation(v_hi[j][:, LC, :], bank(KV_BANK)[:, D:2 * D], ACT.Copy).then_inc(kv_read, 1)

            def squares(g, b):
                j = b % 2
                act.wait_ge(q_turned, upto(g, b, 1, 1))
                for h in range(G):
                    ins = act.activation(square[:, h, :], bank(Q_BANK)[:, h * D:(h + 1) * D], ACT.Square, accum_out=sumsq[j][:, h:h + 1])
                ins.then_inc(q_squared, 1)

            def exps(g, b, h):
                act.wait_ge(scores_done, upto(g, b, G, h + 1))
                act.activation(probs[:, h, :], scores[h % 2][:], ACT.Exp, bias=neg_max[:, h:h + 1], scale=-1.0,
                               accum_out=row_sum[:, h:h + 1]).then_inc(exp_done, 1)

            def probs_T(g, b, c):
                if c >= 3:
                    act.wait_ge(pv_done, upto(g, b, KC, c - 2))
                hi(pT_hi[c % 3][:], bank([B_BANK, A_BANK][c % 2]), pT_in_psum, upto(g, b, KC, c + 1), pT_hi_done)

            def new_keys(g, b):
                hi(kT_hi[:, L:KEYS], bank(KV_BANK, S), kn_in_psum, upto(g, b, 1, 1), kn_hi_done)

            def queries(g, b):
                hi(qT_hi[b % 2][:], bank(Q_BANK), qT_in_psum, upto(g, b, 1, 1), qT_hi_done)

            for n in range(QKV_GROUPS):
                qkv_group(0, n)
            for b in range(2, B):
                tokens(b)
            squares(0, 0)
            queries(0, 0)
            cached_keys(0, 0)
            new_kv(0, 0)
            cached_values(0, 0)
            new_keys(0, 0)

            def group(g, last):
                for b in range(B):
                    g1, b1 = following(g, b)
                    more = not (last and b == B - 1)

                    def weights(slot):
                        for n in weight_groups(b, slot, last):
                            if b < 2:
                                wo_group(g, n)
                            else:
                                qkv_group(g + 1, n)

                    if more:
                        squares(g1, b1)
                    weights(0)
                    exps(g, b, 0)
                    if more:
                        queries(g1, b1)
                    exps(g, b, 1)
                    weights(1)
                    weights(2)
                    exps(g, b, 2)
                    exps(g, b, 3)
                    weights(3)
                    weights(4)
                    if more:
                        cached_keys(g1, b1)
                    probs_T(g, b, 0)
                    probs_T(g, b, 1)
                    if more:
                        cached_values(g1, b1)
                        new_kv(g1, b1)
                    probs_T(g, b, 2)
                    probs_T(g, b, 3)
                    probs_T(g, b, 4)
                    if more:
                        new_keys(g1, b1)
                    hi(oT_hi[:], bank(O_BANK), pv_done, upto(g, b, KC, KC), oT_hi_done)

            group(0, False)
            with act.Fori(1, HK - 1) as g:
                group(g, False)
            group(HK - 1, True)

        @block.vector
        def _(dve):
            steps = [0]

            def link(ins):
                steps[0] += 1
                ins.then_inc(table_step, 1)
                dve.wait_ge(table_step, steps[0])

            dve.memset(neg_max[:], 0.0).then_inc(y_bank_free, 1)
            dve.wait_ge(small_loaded, 16 * 5)
            dve.wait_ge(iota_done, 5)
            dve.tensor_copy(seq_f[:], seq_i[:])
            dve.tensor_copy(key_no, key_no_i)
            dve.tensor_scalar(qw_sb, qw_sb, -1.0, None, ALU.mult)
            dve.tensor_scalar(kw_sb, kw_sb, float(np.sqrt(D)), None, ALU.mult)
            link(dve.tensor_copy(tok_f[:], tok_i[:]))
            for j in range(4):
                q = slice(PSIZE * j, PSIZE * j + PSIZE)
                link(dve.tensor_scalar(in_page_f[q, :], tok_f[q, :], float(-PSIZE * j), float(HK), ALU.add, ALU.mult))
                dve.tensor_scalar(key_row[q, :], table_sb[q, :].rearrange("p (n j) -> p n j", j=4)[:, :, j],
                                  float(PSIZE * HK), in_page_f[q, 0:1], ALU.mult, ALU.add).then_inc(rows_ready, 1)
            link(dve.tensor_scalar(seq_f[:], seq_f[:], tok_f[:, 0:1], None, ALU.add))
            angle3 = angle.rearrange("p (b f) -> p b f", b=B)
            link(dve.tensor_tensor(angle3, seq_f[:].unsqueeze(2).broadcast_to([P, B, HALF]),
                                   invf_sb.unsqueeze(1).broadcast_to([P, B, HALF]), ALU.mult))
            link(dve.tensor_scalar(turns, angle, 1.0 / TWO_PI, ROUND, ALU.mult, ALU.add))
            link(dve.tensor_scalar(turns, turns, -ROUND, None, ALU.add))
            for part in (PI_A, PI_B, PI_C):
                link(dve.scalar_tensor_tensor(out=angle, in0=turns, scalar=-part, in1=angle, op0=ALU.mult, op1=ALU.add))
            dve.tensor_scalar(sin_t, angle, PI_F32, -PI_F32, ALU.min, ALU.max).then_inc(angles_ready, 1)
            link(dve.scalar_tensor_tensor(out=cos_t, in0=angle, scalar=-1.0, in1=angle, op0=ALU.mult, op1=ALU.max))
            dve.tensor_scalar(cos_t, cos_t, -1.0, float(np.pi / 2), ALU.mult, ALU.add).then_inc(angles_ready, 1)
            link(dve.tensor_scalar(seq_f[:], seq_f[:], tok_f[:, 0:1], None, ALU.subtract))

            def masks():
                for b in range(B):
                    ins = dve.tensor_scalar(mask[:, b, 0:L], key_no, seq_f[:, b:b + 1], MASKED, ALU.is_ge, ALU.mult)
                ins.then_inc(tables_ready, 1)

            def table(t, c_out, s_out):
                for half in range(2):
                    f = slice(half * HALF, (half + 1) * HALF)
                    wb = t[:, f].unsqueeze(1).broadcast_to([P, B, HALF])
                    dve.tensor_tensor(c_out[:, :, f], cos_t.rearrange("p (b f) -> p b f", b=B), wb, ALU.mult)
                    ins = dve.tensor_tensor(s_out[:, :, f], sin_t.rearrange("p (b f) -> p b f", b=B), wb, ALU.mult)
                ins.then_inc(tables_ready, 1)

            def lo(out, src, hi_part, hi_done, count, done):
                dve.wait_ge(hi_done, count)
                dve.tensor_tensor(out, src, hi_part.bitcast(F32), ALU.subtract).then_inc(done, 1)

            def tokens(b):
                at = slice(b * S, (b + 1) * S)
                lo(xT_lo[:, :, at], bank(b % 4).rearrange("p (c s) -> p c s", c=DC), xT_hi[:, :, at], xT_hi_done, b + 1, xT_done)

            def qkv_group(g, n):
                flat = lambda t: t[:, 2 * (n - DC):2 * (n - DC) + 2, :].rearrange("p c e -> p (c e)")
                out, h = (wqT_lo[:, n, :], wqT_hi[:, n, :]) if n < DC else (flat(wkvT_lo), flat(wkvT_hi))
                lo(out, bank(WEIGHT_BANKS[n % 2]), h, wqkv_hi_done, g * QKV_GROUPS + n + 1, wqkv_done)

            def wo_group(g, n):
                lo(woT_lo[:, n, :], bank(WEIGHT_BANKS[(n + 1) % 2]), woT_hi[:, n, :], wo_hi_done, g * WO_GROUPS + n + 1, wo_done)

            def cached_values(g, b):
                j = b % 2
                lo(v_lo[j][:, 0:LC, :], v_raw[j][:], v_hi[j][:, 0:LC, :], v_hi_done, upto(g, b, 1, 1), v_cache_done)

            def cached_keys(g, b):
                lo(kT_lo[:, 0:L], bank(A_BANK), kT_hi[:, 0:L], kc_hi_done, upto(g, b, 1, 1), kc_done)

            def turn_q(g, b, part):
                q3 = bank(Q_BANK).rearrange("p (h d) -> p h d", h=G)
                if part == 0:
                    dve.wait_ge(q_in_psum, upto(g, b, 1, 1))
                    dve.tensor_tensor(u_q[:], q3, q_cos[:, b:b + 1, :].broadcast_to([P, G, D]), ALU.mult)
                else:
                    dve.tensor_tensor(w_q[:], q3, q_sin[:, b:b + 1, :].broadcast_to([P, G, D]), ALU.mult).then_inc(q_turned, 1)

            def new_kv(g, b):
                j = b % 2
                scale = inv_rms[j][:, G:G + 1]
                dve.wait_ge(kv_read, upto(g, b, 1, 1))
                dve.tensor_tensor(v_lo[j][:, LC, :], bank(KV_BANK)[:, D:2 * D], v_hi[j][:, LC, :].bitcast(F32), ALU.subtract).then_inc(v_new_done, 1)
                dve.wait_ge(k_scale_ready, upto(g, b, 2, 2))
                dve.scalar_tensor_tensor(out=u_k[:], in0=bank(KV_BANK, D), scalar=scale, in1=k_cos[:, b, :], op0=ALU.mult, op1=ALU.mult)
                dve.scalar_tensor_tensor(out=w_k[:], in0=bank(KV_BANK, D), scalar=scale, in1=k_sin[:, b, :],
                                         op0=ALU.mult, op1=ALU.mult).then_inc(k_turned, 1)

            def mask_and_max(g, b, h):
                if h >= 2:
                    dve.wait_ge(exp_done, upto(g, b, G, h - 1))
                dve.wait_ge(scores_in_psum, upto(g, b, G, h + 1))
                wait_apart(dve, scale_ready, upto(g, b, 2, 2), dve_passed)
                dve.tensor_tensor_reduce(out=scores[h % 2][:], in0=slot(h), in1=mask[:, b, :],
                                         scale=inv_rms[b % 2][:, h:h + 1], scalar=3.0e38, op0=ALU.add, op1=ALU.min,
                                         accum_out=neg_max[:, h:h + 1]).then_inc(scores_done, 1)

            def inverse(g, b, h):
                dve.wait_ge(exp_done, upto(g, b, G, h + 1))
                dve.reciprocal(row_inv[:, h:h + 1], row_sum[:, h:h + 1]).then_inc(inv_done, 1)

            def add_y(g, b):
                at = (b - 1) % B
                dve.wait_ge(y_in_psum, upto(g, b, 1))
                dve.tensor_tensor(xres[:, at, :], bank(KV_BANK), xres[:, at, :], ALU.add).then_inc(y_bank_free, 1)

            def probs_T(g, b, c):
                lo(pT_lo[c % 3][:], bank([B_BANK, A_BANK][c % 2]), pT_hi[c % 3][:], pT_hi_done, upto(g, b, KC, c + 1), pT_done)

            def new_keys(g, b):
                lo(kT_lo[:, L:KEYS], bank(KV_BANK, S), kT_hi[:, L:KEYS], kn_hi_done, upto(g, b, 1, 1), kn_done)

            def queries(g, b):
                lo(qT_lo[b % 2][:], bank(Q_BANK), qT_hi[b % 2][:], qT_hi_done, upto(g, b, 1, 1), qT_done)

            tokens(0)
            tokens(1)
            for n in range(QKV_GROUPS):
                qkv_group(0, n)
            dve.wait_ge(sincos_ready, 2)
            table(kw_sb, k_cos, k_sin)
            table(qw_sb, q_cos, q_sin)
            dve.wait_ge(tables_ready, 2)
            turn_q(0, 0, 0)
            turn_q(0, 0, 1)
            for b in range(2, B):
                tokens(b)
            queries(0, 0)
            cached_keys(0, 0)
            new_kv(0, 0)
            cached_values(0, 0)
            turn_q(0, 1, 0)
            turn_q(0, 1, 1)
            new_keys(0, 0)
            masks()
            dve.wait_ge(tables_ready, 3)

            def group(g, first, last):
                for b in range(B):
                    g1, b1 = following(g, b)
                    more, more2 = not (last and b == B - 1), not (last and b >= B - 2)

                    def weights(slot):
                        for n in weight_groups(b, slot, last):
                            if b < 2:
                                wo_group(g, n)
                            else:
                                qkv_group(g + 1, n)

                    mask_and_max(g, b, 0)
                    weights(0)
                    mask_and_max(g, b, 1)
                    inverse(g, b, 0)
                    if more:
                        queries(g1, b1)
                    inverse(g, b, 1)
                    weights(1)
                    weights(2)
                    mask_and_max(g, b, 2)
                    mask_and_max(g, b, 3)
                    inverse(g, b, 2)
                    inverse(g, b, 3)
                    if not (first and b == 0):
                        add_y(g, b)
                    weights(3)
                    weights(4)
                    if more:
                        cached_keys(g1, b1)
                    probs_T(g, b, 0)
                    probs_T(g, b, 1)
                    if more:
                        cached_values(g1, b1)
                    probs_T(g, b, 2)
                    if more:
                        new_kv(g1, b1)
                    probs_T(g, b, 3)
                    probs_T(g, b, 4)
                    if more2:
                        turn_q(*following(g1, b1), 0)
                        turn_q(*following(g1, b1), 1)
                    if more:
                        new_keys(g1, b1)
                    lo(oT_lo[:], bank(O_BANK), oT_hi[:], oT_hi_done, upto(g, b, 1, 1), oT_done)

            group(0, True, False)
            with dve.Fori(1, HK - 1) as g:
                group(g, False, False)
            group(HK - 1, False, True)
            add_y(HK, 0)

        @block.tensor
        def _(pe):
            pe.wait_ge(ident_step, 2)

            def tokens(b):
                if b % 2 == 0 and b <= 2:
                    pe.wait_ge(x_loaded[b // 2], 16)
                if b >= 4:
                    pe.wait_ge(xT_done, b - 3)
                for c in range(DC):
                    ins = pe.transpose(bank(b % 4)[:, c * S:(c + 1) * S], xres[:, b, c * P:(c + 1) * P], ident[:])
                ins.then_inc(xT_in_psum, 1)

            tokens(0)
            tokens(1)

            def qkv_group(g, n):
                if n == 0:
                    pe.wait_ge(wqkv_loaded, g * 48 + 48)
                if n >= 2:
                    pe.wait_ge(wqkv_done, g * QKV_GROUPS + n - 1)
                out = bank(WEIGHT_BANKS[n % 2])
                if n < DC:
                    for e in range(G):
                        ins = pe.transpose(out[:, e * D:(e + 1) * D], wq_raw[:, e, n * P:(n + 1) * P], ident[:])
                else:
                    for m in range(4):
                        c = 2 * (n - DC) + m // 2
                        ins = pe.transpose(out[:, m * D:(m + 1) * D], wkv_raw[:, m % 2, c * P:(c + 1) * P], ident[:])
                ins.then_inc(wqkv_in_psum, 1)

            def wo_group(g, n):
                if n == 0:
                    pe.wait_ge(wo_loaded, g * 16 + 16)
                if n >= 2:
                    pe.wait_ge(wo_done, g * WO_GROUPS + n - 1)
                for c in range(DC):
                    ins = pe.transpose(bank(WEIGHT_BANKS[(n + 1) % 2])[:, c * P:(c + 1) * P], wo_raw[:, c, n * D:(n + 1) * D], ident[:])
                ins.then_inc(wo_in_psum, 1)

            def cached_keys(g, b):
                j = b % 2
                pe.wait_ge(k_loaded[j], g * (B // 2 * LC * 16) + (b // 2 + 1) * LC * 16)
                for c in range(LC):
                    ins = pe.transpose(bank(A_BANK)[:, c * P:(c + 1) * P], k_raw[j][:, c, :], ident[:])
                ins.then_inc(kc_in_psum, 1)

            def project_q(g, b, cs, first=False):
                at = slice(b * S, (b + 1) * S)
                if cs[0] == 0 and not first:
                    pe.wait_ge(qT_done, upto(g, b, 1))
                if cs[0] == 0 and b == 0:
                    pe.wait_ge(wqkv_done, g * QKV_GROUPS + DC)
                for c in cs:
                    ins = three_pass(pe, bank(Q_BANK), xT_hi[:, c, at], xT_lo[:, c, at], wqT_hi[:, c, :], wqT_lo[:, c, :], c == 0, c == DC - 1)
                if c == DC - 1:
                    ins.then_inc(q_in_psum, 1)

            def project_kv(g, b, first=False):
                at = slice(b * S, (b + 1) * S)
                if not first:
                    pe.wait_ge(y_bank_free, upto(g, b, 1))
                if b == 0:
                    pe.wait_ge(wqkv_done, g * QKV_GROUPS + QKV_GROUPS)
                for c in range(DC):
                    ins = three_pass(pe, bank(KV_BANK, 2 * D), xT_hi[:, c, at], xT_lo[:, c, at], wkvT_hi[:, c, :], wkvT_lo[:, c, :], c == 0, c == DC - 1)
                ins.then_inc(kv_in_psum, 1)

            def new_keys(g, b):
                pe.wait_ge(k_rot_done, upto(g, b, 1, 1))
                pe.wait_ge(v_new_done, upto(g, b, 1, 1))
                pe.transpose(bank(KV_BANK, S), k_rot[:], ident[:]).then_inc(kn_in_psum, 1)

            def queries(g, b):
                pe.wait_ge(q_rot_done, upto(g, b, 1, 1))
                pe.wait_ge(q_squared, upto(g, b, 1, 1))
                for h in range(G):
                    ins = pe.transpose(bank(Q_BANK)[:, h * S:(h + 1) * S], q_rot[:, h, :], ident[:])
                ins.then_inc(qT_in_psum, 1)

            def score(g, b, h, first):
                if h == 0:
                    pe.wait_ge(kc_done, upto(g, b, 1, 1))
                    pe.wait_ge(qT_done, upto(g, b, 1, 1))
                if h >= 2:
                    pe.wait_ge(scores_done, upto(g, b, G, h - 1))
                q = slice(h * S, (h + 1) * S)
                qh, ql = qT_hi[b % 2], qT_lo[b % 2]
                for part, k in enumerate(slice(*p) for p in SCORE_PARTS):
                    if part == 1 and h == 0:
                        pe.wait_ge(kn_done, upto(g, b, 1, 1))
                    if part == 1 and h == 1 and not (first and b == 0):
                        pe.wait_ge(oT_done, upto(g, b, 1))
                    ins = three_pass(pe, slot(h)[:, k], qh[:, q], ql[:, q], kT_hi[:, k], kT_lo[:, k], True, True)
                ins.then_inc(scores_in_psum, 1)

            def probs_T(g, b, c):
                if c == 0:
                    pe.wait_ge(probs_done, upto(g, b, G, G))
                if c >= 2:
                    pe.wait_ge(pT_done, upto(g, b, KC, c - 1))
                for h in range(G):
                    ins = pe.transpose(bank([B_BANK, A_BANK][c % 2])[:, h * S:(h + 1) * S], probs[:, h, c * P:(c + 1) * P], ident[:])
                ins.then_inc(pT_in_psum, 1)

            def times_v(g, b, c):
                j = b % 2
                if c == 0:
                    pe.wait_ge(v_cache_done, upto(g, b, 1, 1))
                pe.wait_ge(pT_done, upto(g, b, KC, c + 1))
                three_pass(pe, bank(O_BANK), v_hi[j][:, c, :], v_lo[j][:, c, :], pT_hi[c % 3][:], pT_lo[c % 3][:], c == 0, c == KC - 1).then_inc(pv_done, 1)

            def output(g, b, hs):
                if hs[0] == 0:
                    pe.wait_ge(oT_done, upto(g, b, 1))
                for h in hs:
                    if b == 1:
                        pe.wait_ge(wo_done, g * WO_GROUPS + h + 1)
                    q = slice(h * S, (h + 1) * S)
                    ins = three_pass(pe, bank(KV_BANK), oT_hi[:, q], oT_lo[:, q], woT_hi[:, h, :], woT_lo[:, h, :], h == 0, h == G - 1)
                if h == G - 1:
                    ins.then_inc(y_in_psum, 1)

            for n in range(QKV_GROUPS):
                qkv_group(0, n)
            pe.wait_ge(xT_done, 2)
            project_q(0, 0, range(DC), first=True)
            for b in range(2, B):
                tokens(b)
            pe.wait_ge(wqkv_done, QKV_GROUPS)
            cached_keys(0, 0)
            project_kv(0, 0, first=True)
            queries(0, 0)
            project_q(0, 1, range(DC))
            new_keys(0, 0)
            pe.wait_ge(xT_done, B)

            def group(g, first, last):
                for b in range(B):
                    g1, b1 = following(g, b)
                    more, more2 = not (last and b == B - 1), not (last and b >= B - 2)

                    def weights(slot):
                        for n in weight_groups(b, slot, last):
                            if b < 2:
                                wo_group(g, n)
                            else:
                                qkv_group(g + 1, n)

                    def output_before(hs):
                        if not (first and b == 0):
                            output(g, b, hs)

                    def project_ahead(cs):
                        if more2:
                            project_q(*following(g1, b1), cs)

                    score(g, b, 0, first)
                    weights(0)
                    score(g, b, 1, first)
                    if more:
                        queries(g1, b1)
                    weights(1)
                    output_before(range(2))
                    weights(2)
                    score(g, b, 2, first)
                    score(g, b, 3, first)
                    weights(3)
                    output_before(range(2, G))
                    weights(4)
                    new_q = b == B - 2 and not last
                    if more:
                        if b == 1:
                            pe.wait_ge(wo_done, g * WO_GROUPS + WO_GROUPS)
                        if b >= B - 2 and not last:
                            pe.wait_ge(wqkv_done, (g + 1) * QKV_GROUPS + (DC - 1 if new_q else QKV_GROUPS - 1))
                        cached_keys(g1, b1)
                    if new_q:
                        project_kv(g1, b1)
                    else:
                        project_ahead(range(2))
                    if b == 0:
                        pe.wait_ge(wo_done, g * WO_GROUPS + 1)
                    if b >= B - 2 and not last:
                        pe.wait_ge(wqkv_done, (g + 1) * QKV_GROUPS + (DC if new_q else QKV_GROUPS))
                    probs_T(g, b, 0)
                    if more:
                        pe.wait_ge(kc_done, upto(g1, b1, 1, 1))
                    probs_T(g, b, 1)
                    if new_q:
                        project_ahead(range(2))
                    elif more:
                        project_kv(g1, b1)
                    times_v(g, b, 0)
                    probs_T(g, b, 2)
                    project_ahead(range(2, 3))
                    probs_T(g, b, 3)
                    times_v(g, b, 1)
                    probs_T(g, b, 4)
                    project_ahead(range(3, 4))
                    times_v(g, b, 2)
                    times_v(g, b, 3)
                    if more:
                        new_keys(g1, b1)
                    times_v(g, b, 4)

            group(0, True, False)
            with pe.Fori(1, HK - 1) as g:
                group(g, False, False)
            group(HK - 1, False, True)
            output(HK, 0, range(G))


def dense_signed(nc, ident, xres, w_raw, w_loaded, bias, coeff, mask, x_out, stored, w_gate, gate_staged):
    with ExitStack() as ctx:
        def sb(name, shape, dt=F32):
            return ctx.enter_context(nc.sbuf_tensor("ds_" + name, shape, dt))

        def sem(name):
            return ctx.enter_context(nc.semaphore("ds_" + name))

        ps = ctx.enter_context(nc.psum_tensor("ds_ps", [P, 8, NFREE], F32))
        X_BANK, DENSE_BANK, SIGN_BANK, W_BANK = 0, 2, 4, 4

        wT_hi = sb("wT_hi", [P, DC, DM], F32R)
        wT_lo = sb("wT_lo", [P, DC, DM], F32R)
        bias_sb = sb("bias_sb", [P, DM])
        coeff_sb = sb("coeff_sb", [P, B])
        zero = sb("zero", [P, DM])
        x_copy = sb("x_copy", [P, B, DM])
        x_sum = sb("x_sum", [P, B])
        sign_bias = sb("sign_bias", [P, B])
        mask_raw = [sb(f"mask_raw{j}", [P, DC, DM], I32) for j in range(2)]
        xT_hi = [sb(f"xT_hi{j}", [P, DC, S], F32R) for j in range(2)]
        xT_lo = [sb(f"xT_lo{j}", [P, DC, S], F32R) for j in range(2)]
        x_in = [sb(f"x_in{j}", [P, DM]) for j in range(2)]
        x_bias = [sb(f"x_bias{j}", [P, DM]) for j in range(2)]
        signed = [sb(f"signed{j}", [P, DM]) for j in range(2)]
        m_hi = [sb(f"m_hi{j}", [P, DC, DM], F32R) for j in range(2)]
        m_lo = [sb(f"m_lo{j}", [P, DC, DM], F32R) for j in range(2)]

        zeroed = sem("zeroed")
        small_loaded = sem("small_loaded")
        mask_loaded = [sem(f"mask_loaded{j}") for j in range(2)]
        w_in_psum = sem("w_in_psum")
        wT_hi_done = sem("wT_hi_done")
        wT_done = sem("wT_done")
        sums_done = sem("sums_done")
        sign_bias_done = sem("sign_bias_done")
        x_copied = sem("x_copied")
        x_in_psum = sem("x_in_psum")
        xT_hi_done = sem("xT_hi_done")
        xT_done = sem("xT_done")
        x_bias_done = sem("x_bias_done")
        m_hi_done = sem("m_hi_done")
        m_done = sem("m_done")
        pool_passed = sem("pool_passed")
        dense_done = sem("dense_done")
        sign_done = sem("sign_done")
        signed_done = sem("signed_done")
        dense_added = sem("dense_added")
        added = sem("added")

        PAIRS = B // 2
        block = ctx.enter_context(nc.Block())

        @block.sync
        def _(sp):
            def load_mask(i, j):
                sp.dma_start(mask_raw[j][:], mask[bass.ds(i, 1)].rearrange("o (c p) n -> p (o c) n", p=P)).then_inc(mask_loaded[j], 16)

            sp.dma_start(bias_sb[:], bias.rearrange("(o d) -> o d", o=1).broadcast_to([P, DM])).then_inc(small_loaded, 16)
            sp.dma_start(coeff_sb[:], coeff.rearrange("(o b) -> o b", o=1).broadcast_to([P, B])).then_inc(small_loaded, 16)
            for j in range(2):
                load_mask(j, j)
            sp.wait_ge(w_in_psum, DC)
            sp.dma_start(w_raw[:], w_gate[0:DC * P].rearrange("(c p) d -> p c d", p=P)).then_inc(gate_staged, 16)
            with sp.Fori(0, PAIRS - 1) as p:
                for j in range(2):
                    sp.wait_ge(m_done, p * 2 + j + 1)
                    load_mask(p * 2 + j + 2, j)
            for i in range(B):
                sp.wait_ge(added, i + 1)
                sp.dma_start(x_out[i], xres[:, i, :]).then_inc(stored, 16)

        @block.gpsimd
        def _(pool):
            pool.memset(zero[:], 0.0).then_inc(zeroed, 1)
            pool.wait_ge(zeroed, 1)

            def copy_in(p, j):
                if not isinstance(p, int) or p > 1:
                    wait_apart(pool, x_in_psum, p * 2 + j - 1, pool_passed)
                pool.tensor_tensor(x_in[j][:], xres[:, bass.ds(p * 2 + j, 1), :].rearrange("p o d -> p (o d)"), zero[:], ALU.add).then_inc(x_copied, 1)

            def add_bias(p, j):
                if not isinstance(p, int) or p > 0:
                    wait_apart(pool, added, p * 2 + j - 1, pool_passed)
                pool.tensor_tensor(x_bias[j][:], xres[:, bass.ds(p * 2 + j, 1), :].rearrange("p o d -> p (o d)"), bias_sb[:], ALU.add).then_inc(x_bias_done, 1)

            def add_up(p, j):
                pool.wait_ge(signed_done, p * 2 + j + 1)
                wait_apart(pool, dense_added, p * 2 + j + 1, pool_passed)
                pool.tensor_tensor(xres[:, bass.ds(p * 2 + j, 1), :].rearrange("p o d -> p (o d)"), x_bias[j][:], signed[j][:], ALU.add).then_inc(added, 1)

            for j in range(2):
                copy_in(1, j)
            pool.wait_ge(small_loaded, 32)
            for j in range(2):
                add_bias(0, j)
            pool.wait_ge(sums_done, B)
            with pool.Fori(1, PAIRS - 1) as p:
                for j in range(2):
                    add_up(p - 1, j)
                    add_bias(p, j)
                    copy_in(p + 1, j)
            for j in range(2):
                add_up(PAIRS - 2, j)
                add_bias(PAIRS - 1, j)
            for j in range(2):
                add_up(PAIRS - 1, j)

        @block.scalar
        def _(act):
            def x_and_mask(p, j):
                act.wait_ge(x_in_psum, p * 2 + j + 1)
                act.activation(xT_hi[j][:].rearrange("p c s -> p (c s)"), ps[:, X_BANK + j, :], ACT.Copy).then_inc(xT_hi_done, 1)

            def mask_hi(p, j, first=True):
                act.wait_ge(mask_loaded[j], p * 16 + 16)
                if not first:
                    act.wait_ge(sign_done, p * 2 + j - 1)
                act.activation(m_hi[j][:], mask_raw[j][:], ACT.Copy, scale=2.0).then_inc(m_hi_done, 1)

            def times_coeff(p, j):
                at = bass.ds(p * 2 + j, 1)
                act.wait_ge(sign_done, p * 2 + j + 1)
                if not isinstance(p, int) or p > 0:
                    act.wait_ge(added, p * 2 + j - 1)
                act.activation(signed[j][:], ps[:, SIGN_BANK + j, :], ACT.Identity, scale=coeff_sb[:, at], bias=sign_bias[:, at]).then_inc(signed_done, 1)

            for c in range(DC):
                act.wait_ge(w_in_psum, c + 1)
                act.activation(wT_hi[:, c, :], ps[:, W_BANK + c, :], ACT.Copy).then_inc(wT_hi_done, 1)
            for j in range(2):
                x_and_mask(0, j)
            for j in range(2):
                mask_hi(0, j)
            for i in range(B):
                act.activation(x_copy[:, i, :], xres[:, i, :], ACT.Copy, accum_out=x_sum[:, i:i + 1]).then_inc(sums_done, 1)
            act.wait_ge(sign_bias_done, 1)

            def turn(p):
                for j in range(2):
                    x_and_mask(p + 1, j)
                    mask_hi(p + 1, j, first=False)
                    times_coeff(p, j)

            turn(0)
            with act.Fori(1, PAIRS - 1) as p:
                turn(p)
            for j in range(2):
                times_coeff(PAIRS - 1, j)

        @block.vector
        def _(dve):
            flat = lambda t: t.rearrange("p c n -> p (c n)")
            for c in range(DC):
                dve.wait_ge(wT_hi_done, c + 1)
                dve.tensor_tensor(wT_lo[:, c, :], ps[:, W_BANK + c, :], wT_hi[:, c, :].bitcast(F32), ALU.subtract).then_inc(wT_done, 1)
            def x_lo(p, j):
                dve.wait_ge(xT_hi_done, p * 2 + j + 1)
                dve.tensor_tensor(flat(xT_lo[j][:]), ps[:, X_BANK + j, :], flat(xT_hi[j][:]).bitcast(F32), ALU.subtract).then_inc(xT_done, 1)

            def mask_lo(p, j):
                dve.wait_ge(m_hi_done, p * 2 + j + 1)
                dve.scalar_tensor_tensor(out=flat(m_lo[j][:]), in0=flat(mask_raw[j][:]), scalar=2.0, in1=flat(m_hi[j][:]).bitcast(F32),
                                         op0=ALU.mult, op1=ALU.subtract).then_inc(m_done, 1)

            def add_dense(p, j):
                dve.wait_ge(dense_done, p * 2 + j + 1)
                dve.wait_ge(x_bias_done, p * 2 + j + 1)
                dve.tensor_tensor(x_bias[j][:], ps[:, DENSE_BANK + j, :], x_bias[j][:], ALU.add).then_inc(dense_added, 1)

            for j in range(2):
                x_lo(0, j)
            for j in range(2):
                mask_lo(0, j)
            dve.wait_ge(small_loaded, 32)
            dve.wait_ge(sums_done, B)
            dve.scalar_tensor_tensor(out=sign_bias[:], in0=x_sum[:], scalar=-1.0, in1=coeff_sb[:], op0=ALU.mult, op1=ALU.mult).then_inc(sign_bias_done, 1)
            with dve.Fori(0, PAIRS - 1) as p:
                for j in range(2):
                    add_dense(p, j)
                    x_lo(p + 1, j)
                    mask_lo(p + 1, j)
            for j in range(2):
                add_dense(PAIRS - 1, j)

        @block.tensor
        def _(pe):
            def tokens(p, j):
                first = isinstance(p, int) and p == 0
                if not first:
                    pe.wait_ge(x_copied, p * 2 + j - 1)
                for c in range(DC):
                    src = xres[:, j, c * P:(c + 1) * P] if first else x_in[j][:, c * P:(c + 1) * P]
                    ins = pe.transpose(ps[:, X_BANK + j, c * S:(c + 1) * S], src, ident[:])
                ins.then_inc(x_in_psum, 1)

            def product(bank, j, hi, lo):
                for c in range(DC):
                    ins = three_pass(pe, ps[:, bank + j, :], xT_hi[j][:, c, :], xT_lo[j][:, c, :], hi[:, c, :], lo[:, c, :], c == 0, c == DC - 1)
                return ins

            def batch(p, j):
                pe.wait_ge(xT_done, p * 2 + j + 1)
                if not isinstance(p, int) or p > 0:
                    pe.wait_ge(dense_added, p * 2 + j - 1)
                    pe.wait_ge(signed_done, p * 2 + j - 1)
                product(DENSE_BANK, j, wT_hi, wT_lo).then_inc(dense_done, 1)
                pe.wait_ge(m_done, p * 2 + j + 1)
                product(SIGN_BANK, j, m_hi[j], m_lo[j]).then_inc(sign_done, 1)

            for j in range(2):
                tokens(0, j)
            pe.wait_ge(w_loaded, 16)
            for c in range(DC):
                for o in range(DC):
                    ins = pe.transpose(ps[:, W_BANK + c, o * P:(o + 1) * P], w_raw[:, o, c * P:(c + 1) * P], ident[:])
                ins.then_inc(w_in_psum, 1)
            pe.wait_ge(wT_done, DC)
            batch(0, 0)
            tokens(1, 0)
            batch(0, 1)
            tokens(1, 1)
            with pe.Fori(1, PAIRS - 1) as p:
                for j in range(2):
                    batch(p, j)
                    tokens(p + 1, j)
            for j in range(2):
                batch((PAIRS - 1), j)


def swiglu_adapters(nc, ident, x, w_gate, w_up, w_down, a_gate, b_gate, a_up, b_up, a_down, b_down, lora_idx, weight, ids, out, free, tokens_stored, staging, gate_staged):
    with ExitStack() as ctx:
        def sb(name, shape, dt=F32):
            return ctx.enter_context(nc.sbuf_tensor("sw_" + name, shape, dt))

        def sem(name):
            return ctx.enter_context(nc.semaphore("sw_" + name))

        ps = ctx.enter_context(nc.psum_tensor("sw_ps", [P, 8, NFREE], F32))
        gT_hi = sb("gT_hi", [P, DC, F], F32R)
        gT_lo = sb("gT_lo", [P, DC, F], F32R)
        uT_hi = sb("uT_hi", [P, DC, F], F32R)
        uT_lo = sb("uT_lo", [P, DC, F], F32R)
        dT_hi = sb("dT_hi", [P, FC, DM], F32R)
        dT_lo = sb("dT_lo", [P, FC, DM], F32R)

        FPAD = FC * P
        REPS = 4
        R2 = 2 * REPS * RANK

        carved = {"free": 0, "staging": 0}

        def carve(shape, name="free"):
            tile, at, size = {"free": free, "staging": staging}[name], carved[name], int(np.prod(shape))
            carved[name] += size
            names = "abcd"[:len(shape)]
            flat = tile[:].rearrange("p c d -> p (c d)")[:, at:at + size]
            return flat.rearrange(f"p ({' '.join(names)}) -> p {' '.join(names)}", **dict(zip(names, shape)))

        x_next = carve([DM])
        x_res = carve([DM])
        act_t = carve([FPAD])
        agu_raw = carve([DM], "staging")
        bgu_raw = sb("bgu_raw", [P, FC, 2, RANK])
        ad_raw = carve([FPAD], "staging")[0:RANK]
        bd_raw = carve([DC, RANK], "staging")
        bgu_rep = carve([FC, 2, REPS, RANK])
        bd_rep = carve([DC, 2, RANK])
        w_raw = [sb(f"w_raw{j}", [P, DC, P]) for j in range(2)]

        zeroed = sem("zeroed")
        repeated = sem("repeated")
        pool_passed = sem("pool_passed")
        x_loaded = sem("x_loaded")
        lora_loaded = sem("lora_loaded")
        res_loaded = sem("res_loaded")
        w_loaded = [sem(f"w_loaded{j}") for j in range(2)]

        def load_next(sp, i):
            sp.dma_start(x_next[:], x[bass.ds(i, 1)].rearrange("o s d -> (o s) d")).then_inc(x_loaded, 16)
            r = sp.value_load(lora_idx.rearrange("(o b) -> o b", o=1)[:, bass.ds(i, 1)], min_val=0, max_val=15)
            for m, (a, b_) in enumerate(((a_gate, b_gate), (a_up, b_up))):
                for n in range(REPS - 1):
                    at = (m * REPS + n) * RANK
                    sp.dma_start(agu_raw[at:at + RANK, :], a[0, bass.ds(r, 1)].rearrange("o r d -> (o r) d")).then_inc(lora_loaded, 16)
                bb = b_[0, bass.ds(r, 1)].rearrange("o f r -> (o f) r")
                sp.dma_start(bgu_raw[:, 0:FC - 1, m, :], bb[0:(FC - 1) * P].rearrange("(c p) r -> p c r", p=P)).then_inc(lora_loaded, 16)
                sp.dma_start(bgu_raw[0:FR, FC - 1, m, :], bb[(FC - 1) * P:F]).then_inc(lora_loaded, 16)
            sp.dma_start(ad_raw[:, 0:F], a_down[0, bass.ds(r, 1)].rearrange("o r f -> (o r) f")).then_inc(lora_loaded, 16)
            sp.dma_start(bd_raw[:], b_down[0, bass.ds(r, 1)].rearrange("o (c p) r -> p (o c) r", p=P)).then_inc(lora_loaded, 16)

        def load_res(sp, i):
            sp.dma_start(x_res[:], x[bass.ds(i, 1)].rearrange("o s d -> (o s) d")).then_inc(res_loaded, 16)

        def load_w(sp, i, cs):
            a = sp.value_load(ids.rearrange("(o b) -> o b", o=1)[:, bass.ds(i, 1)], min_val=0, max_val=7)
            for c in cs:
                w = weight[bass.ds(a, 1)].rearrange("o (c p) d -> p (o c) d", p=P)
                sp.dma_start(w_raw[c % 2][:], w[:, :, c * P:(c + 1) * P]).then_inc(w_loaded[c % 2], 16)

        def repeat_ranks(pool, loaded):
            wait_apart(pool, lora_loaded, loaded * 192 + 192, pool_passed)
            for m in range(2):
                pool.tensor_copy(bgu_rep[:, :, m, :, :], bgu_raw[:, :, m, :].unsqueeze(2).broadcast_to([P, FC, REPS, RANK])).then_inc(repeated, 1)
            pool.tensor_copy(bd_rep[:], bd_raw[:].unsqueeze(2).broadcast_to([P, DC, 2, RANK])).then_inc(repeated, 1)

        with ExitStack() as prep:
            AHEAD_ROWS = FN[0][1] // P
            gate_raw = prep.enter_context(nc.sbuf_tensor("sw_gate_raw", [P, FC - AHEAD_ROWS, DM], F32))
            up_raw = prep.enter_context(nc.sbuf_tensor("sw_up_raw", [P, FC, DM], F32))
            down_raw = prep.enter_context(nc.sbuf_tensor("sw_down_raw", [P, DC, FN[0][1]], F32))
            raw_loaded = [gate_staged] + [sem(f"raw_loaded{n}") for n in range(1, 3 * len(FN))]
            tile_in_psum = sem("tile_in_psum")
            tile_hi_done = sem("tile_hi_done")
            tile_done = sem("tile_done")
            tiles = [(m, c, n, k, m * len(FN) + g) for m in range(2) for g, (n, k) in enumerate(FN) for c in range(DC)]
            tiles += [(2, c, 0, DM, 2 * len(FN) + c // 4) for c in range(FC)]

            def down_piece(g):
                n, k = FN[g]
                if g == 0:
                    return down_raw[:]
                at = DC * (n - FN[0][1])
                return gate_raw[:].rearrange("p c d -> p (c d)")[:, at:at + DC * k].rearrange("p (c f) -> p c f", c=DC)

            def row_block(m, c):
                if m == 1:
                    return up_raw[:, c, :]
                return staging[:, c, :] if c < AHEAD_ROWS else gate_raw[:, c - AHEAD_ROWS, :]

            def load_down(eng, g):
                n, k = FN[g]
                eng.dma_start(down_piece(g), w_down.rearrange("(c p) f -> p c f", p=P)[:, :, n:n + k]).then_inc(raw_loaded[2 * len(FN) + g], 16)

            def place(t):
                m, c, n, k, _ = tiles[t]
                rows = P if m < 2 or c < FC - 1 else FR
                hi, lo = ((gT_hi, gT_lo), (uT_hi, uT_lo), (dT_hi, dT_lo))[m]
                return hi[0:rows, c, n:n + k], lo[0:rows, c, n:n + k], ps[0:rows, t % 8, 0:k]

            block = prep.enter_context(nc.Block())

            @block.sync
            def _(sp):
                for m, w in enumerate((w_gate, w_up)):
                    for g, (n, k) in enumerate(FN):
                        if (m, g) == (0, 0):
                            continue
                        done, full = raw_loaded[m * len(FN) + g], k // P
                        tile, at = (gate_raw, n // P - AHEAD_ROWS) if m == 0 else (up_raw, n // P)
                        sp.dma_start(tile[:, at:at + full, :], w[n:n + full * P].rearrange("(c p) d -> p c d", p=P)).then_inc(done, 16)
                        if k % P:
                            sp.dma_start(tile[0:k % P, at + full, :], w[n + full * P:n + k]).then_inc(done, 16)
                load_down(sp, 0)
                sp.wait_ge(tokens_stored, 16 * B)
                sp.wait_ge(zeroed, 3)
                load_next(sp, 0)
                load_res(sp, 0)
                load_w(sp, 0, (0, 1))

            @block.gpsimd
            def _(pool):
                pool.memset(bgu_raw[:], 0.0).then_inc(zeroed, 1)
                pool.wait_ge(tile_in_psum, DC)
                pool.memset(agu_raw, 0.0).then_inc(zeroed, 1)
                pool.memset(ad_raw, 0.0).then_inc(zeroed, 1)
                pool.wait_ge(tokens_stored, 16 * B)
                pool.memset(act_t[:, F:FPAD], 0.0).then_inc(zeroed, 1)
                repeat_ranks(pool, 0)

            @block.tensor
            def _(pe):
                for t, (m, c, n, k, piece) in enumerate(tiles):
                    if c % DC == 0:
                        pe.wait_ge(raw_loaded[piece], 32 if m < 2 and k % P else 16)
                    if t >= 8:
                        pe.wait_ge(tile_done, t - 7)
                    rows = P if m < 2 or c < FC - 1 else FR
                    for at in range(n, n + k, P):
                        cols = min(P, n + k - at)
                        if m < 2:
                            src = row_block(m, at // P)[0:cols, c * P:(c + 1) * P]
                        else:
                            src = down_piece(c // 4)[:, at // P, (c % 4) * P:(c % 4) * P + rows]
                        ins = pe.transpose(ps[0:rows, t % 8, at - n:at - n + cols], src, ident[0:cols, 0:cols])
                    ins.then_inc(tile_in_psum, 1)

            @block.scalar
            def _(act):
                for t in range(len(tiles)):
                    hi, _, src = place(t)
                    act.wait_ge(tile_in_psum, t + 1)
                    if t == DC * len(FN) - 1:
                        for g in range(1, len(FN)):
                            load_down(act, g)
                    act.activation(hi, src, ACT.Copy).then_inc(tile_hi_done, 1)

            @block.vector
            def _(dve):
                for t in range(len(tiles)):
                    hi, lo, src = place(t)
                    dve.wait_ge(tile_hi_done, t + 1)
                    dve.tensor_tensor(lo, src, hi.bitcast(F32), ALU.subtract).then_inc(tile_done, 1)

        xT_hi = sb("xT_hi", [P, DC, S], F32R)
        xT_lo = sb("xT_lo", [P, DC, S], F32R)
        actT_hi = sb("actT_hi", [P, FC, S], F32R)
        actT_lo = sb("actT_lo", [P, FC, S], F32R)
        aguT_hi = sb("aguT_hi", [P, DC, R2], F32R)
        aguT_lo = sb("aguT_lo", [P, DC, R2], F32R)
        tgu = sb("tgu", [R2, S], F32R)
        bguT = sb("bguT", [R2, F], F32R)
        T_LO = [slice(r, r + RANK) for r in (0, R2 // 2)]
        B_LO = [slice(r, r + RANK) for r in (2 * RANK, R2 // 2 + 2 * RANK)]
        adT = sb("adT", [P, FC, 2, RANK], F32R)
        td_hi = sb("td_hi", [2 * RANK, S], F32R)
        td_lo = sb("td_lo", [2 * RANK, S], F32R)
        bdT_hi = sb("bdT_hi", [2 * RANK, DM], F32R)
        bdT_lo = sb("bdT_lo", [2 * RANK, DM], F32R)
        wT_hi = sb("wT_hi", [P, DC, DM], F32R)
        wT_lo = sb("wT_lo", [P, DC, DM], F32R)
        zT_hi, zT_lo = aguT_hi, aguT_lo

        sp_passed = sem("sp_passed")
        in_psum = sem("in_psum")
        hi_done = sem("hi_done")
        out_done = sem("out_done")
        gu_in_psum = sem("gu_in_psum")
        silu_done = sem("silu_done")
        act_done = sem("act_done")
        down_in_psum = sem("down_in_psum")
        pe_passed = sem("pe_passed")
        added = sem("added")
        product_done = sem("product_done")
        result_done = sem("result_done")
        stored = sem("stored")

        W0, W1, Z, W2, W3, ACT0, ACT1, X, ACT2, AGU, BGU0, BGU1, TD, BGU2, TGU, AD, BD = range(17)
        ADAPTER = [W0, W1, Z, W2, W3]
        AHEAD = [X, AGU, BGU0, BGU1, BGU2, TGU, AD, BD]
        FIRST = list(range(ACT0, BD + 1))
        TURN = ADAPTER + FIRST
        LAST = ADAPTER + [ACT0, ACT1, ACT2, TD]
        TAIL = ADAPTER
        BANKS = [4, 5, 7]
        DOWN_BANK = 6

        def before(i, turn):
            if turn is AHEAD:
                return 0
            if turn is FIRST:
                return len(AHEAD)
            if turn is TAIL:
                return before(B - 1, LAST) + len(LAST)
            return (i - 1) * len(TURN) + (len(AHEAD) + len(FIRST))

        def number(i, step, turn):
            return before(i, turn) + turn.index(step)

        def step_bank(step, turn):
            first = 0 if turn is not AHEAD else 1
            return BANKS[(first + turn.index(step)) % 3]

        def leaving(step, turn):
            bk = ps[:, step_bank(step, turn), :]
            flat = lambda t: t.rearrange("p c s -> p (c s)")

            def whole(src, hi, lo, scale=1.0):
                return src, hi, scale, [(src, hi, lo)]

            if step in (ACT0, ACT1, ACT2):
                n = [ACT0, ACT1, ACT2].index(step)
                cs = slice(4 * n, min(4 * n + 4, FC))
                return whole(bk[:, 0:(cs.stop - cs.start) * S], flat(actT_hi[:, cs, :]), flat(actT_lo[:, cs, :]))
            if step == X:
                return whole(bk, flat(xT_hi[:]), flat(xT_lo[:]))
            if step == Z:
                return whole(bk, flat(zT_hi[:]), flat(zT_lo[:]))
            if step in (W0, W1, W2, W3):
                c = [W0, W1, W2, W3].index(step)
                return whole(bk, wT_hi[:, c, :], wT_lo[:, c, :])
            if step == AGU:
                return whole(bk[:, 0:DC * R2], flat(aguT_hi[:]), flat(aguT_lo[:]))
            if step in (BGU0, BGU1, BGU2):
                n, k = FN[[BGU0, BGU1, BGU2].index(step)]
                at = slice(n, n + k)
                return bk[:, 0:k], bguT[:, at], 1.0, [(bk[r, 0:k], bguT[r, at], bguT[r, at]) for r in B_LO]
            if step == TGU:
                return bk[:, 0:S], tgu[:], LORA_SCALE, [(bk[r, 0:S], tgu[r, :], tgu[r, :]) for r in T_LO]
            if step == TD:
                return whole(bk[0:2 * RANK, 0:S], td_hi[:], td_lo[:], LORA_SCALE)
            if step == AD:
                return whole(bk[:, 0:FC * RANK].rearrange("p (c r) -> p c r", c=FC), adT[:, :, 0, :], adT[:, :, 1, :])
            return whole(bk[0:2 * RANK, :], bdT_hi[:], bdT_lo[:])

        block = ctx.enter_context(nc.Block())

        @block.sync
        def _(sp):
            def store(i):
                sp.wait_ge(result_done, i + 1)
                sp.dma_start(out[bass.ds(i, 1)].rearrange("o s d -> (o s) d"), x_res[:]).then_inc(stored, 16)
                sp.wait_ge(stored, i * 16 + 16)

            def turn_loads(i, turn):
                sp.wait_ge(in_psum, before(i, turn))
                if turn is not LAST:
                    load_next(sp, i + 1)
                wait_apart(sp, in_psum, number(i, W1, turn) + 1, sp_passed)
                load_w(sp, i - 1, (2, 3))
                store(i - 1)
                load_res(sp, i)
                load_w(sp, i, (0, 1))

            sp.wait_ge(in_psum, len(AHEAD))
            load_next(sp, 1)
            with sp.Fori(1, B - 1) as i:
                turn_loads(i, TURN)
            turn_loads(B - 1, LAST)
            sp.wait_ge(in_psum, number(B, W1, TAIL) + 1)
            load_w(sp, B - 1, (2, 3))
            store(B - 1)

        @block.gpsimd
        def _(pool):
            pool.wait_ge(in_psum, len(AHEAD))
            repeat_ranks(pool, 1)
            with pool.Fori(1, B - 1) as i:
                wait_apart(pool, in_psum, before(i, TURN), pool_passed)
                repeat_ranks(pool, i + 1)

        @block.scalar
        def _(act):
            def hi(i, steps, turn):
                for step in steps:
                    if step in turn:
                        src, out_hi, scale, _ = leaving(step, turn)
                        act.wait_ge(in_psum, number(i, step, turn) + 1)
                        act.activation(out_hi, src, ACT.Copy, scale=scale).then_inc(hi_done, 1)

            def silu_of(i, n):
                at, k = FN[n]
                act.wait_ge(gu_in_psum, i * len(FN) + n + 1)
                act.activation(act_t[:, at:at + k], ps[:, 2 * (n % 2), 0:k], ACT.Silu).then_inc(silu_done, 1)

            def batch(i, turn):
                silu_of(i, 0)
                hi(i, (W0, W1, Z), turn)
                silu_of(i, 1)
                hi(i, (W2, W3, ACT0), turn)
                silu_of(i, 2)
                hi(i, (ACT1, X, ACT2, AGU, BGU0, BGU1, TD, BGU2, TGU, AD, BD), turn)

            hi(0, AHEAD, AHEAD)
            batch(0, FIRST)
            with act.Fori(1, B - 1) as i:
                batch(i, TURN)
            batch(B - 1, LAST)
            hi(B, TAIL, TAIL)

        @block.vector
        def _(dve):
            def lo(i, steps, turn):
                for step in steps:
                    if step in turn:
                        _, _, scale, parts = leaving(step, turn)
                        dve.wait_ge(hi_done, number(i, step, turn) + 1)
                        for src, h, out_lo in parts:
                            ins = dve.scalar_tensor_tensor(out=out_lo, in0=src, scalar=scale, in1=h.bitcast(F32), op0=ALU.mult, op1=ALU.subtract)
                        ins.then_inc(out_done, 1)

            def times_up(i, n):
                at, k = FN[n]
                dve.wait_ge(silu_done, i * len(FN) + n + 1)
                dve.tensor_tensor(act_t[:, at:at + k], ps[:, 2 * (n % 2) + 1, 0:k], act_t[:, at:at + k], ALU.mult).then_inc(act_done, 1)

            def finish(i):
                dve.wait_ge(product_done, i + 1)
                dve.tensor_tensor(x_res[:], ps[:, DOWN_BANK, :], x_res[:], ALU.add).then_inc(result_done, 1)

            def batch(i, turn):
                times_up(i, 0)
                lo(i, (W0, W1, Z), turn)
                times_up(i, 1)
                lo(i, (W2, W3, ACT0), turn)
                times_up(i, 2)
                lo(i, (ACT1,), turn)
                if turn is not FIRST:
                    finish(i - 1)
                lo(i, (X, ACT2, AGU, BGU0, BGU1, TD, BGU2, TGU, AD), turn)
                dve.wait_ge(down_in_psum, i + 1)
                dve.wait_ge(res_loaded, i * 16 + 16)
                dve.tensor_tensor(x_res[:], ps[:, DOWN_BANK, :], x_res[:], ALU.add).then_inc(added, 1)
                lo(i, (BD,), turn)

            dve.wait_ge(zeroed, 4)
            lo(0, AHEAD, AHEAD)
            batch(0, FIRST)
            with dve.Fori(1, B - 1) as i:
                batch(i, TURN)
            batch(B - 1, LAST)
            lo(B, TAIL, TAIL)
            finish(B - 1)

        @block.tensor
        def _(pe):
            def parts_done(i, step, turn):
                pe.wait_ge(out_done, number(i, step, turn) + 1)

            def free_bank(i, step, turn):
                k = turn.index(step)
                if turn is not AHEAD or k >= 3:
                    wait_apart(pe, out_done, number(i, step, turn) - (2 if k >= 2 else 1), pe_passed)

            def act_transposed(i, step, turn):
                n = [ACT0, ACT1, ACT2].index(step)
                pe.wait_ge(act_done, i * len(FN) + n + 1)
                free_bank(i, step, turn)
                bk = ps[:, step_bank(step, turn), :]
                for c in range(4 * n, min(4 * n + 4, FC)):
                    ins = pe.transpose(bk[:, (c - 4 * n) * S:(c - 4 * n + 1) * S], act_t[:, c * P:(c + 1) * P], ident[:])
                ins.then_inc(in_psum, 1)

            def next_transposed(i, step, turn, loaded):
                if step == X:
                    pe.wait_ge(x_loaded, loaded * 16 + 16)
                if step == AGU:
                    pe.wait_ge(lora_loaded, loaded * 192 + 192)
                if step in (BGU0, BD):
                    pe.wait_ge(repeated, loaded * 3 + 3)
                free_bank(i, step, turn)
                bk = ps[:, step_bank(step, turn), :]
                if step == X:
                    for c in range(DC):
                        ins = pe.transpose(bk[:, c * S:(c + 1) * S], x_next[:, c * P:(c + 1) * P], ident[:])
                elif step == AGU:
                    for c in range(DC):
                        ins = pe.transpose(bk[:, c * R2:(c + 1) * R2], agu_raw[:, c * P:(c + 1) * P], ident[0:R2, 0:R2])
                elif step in (BGU0, BGU1, BGU2):
                    n, k = FN[[BGU0, BGU1, BGU2].index(step)]
                    for at in range(n, n + k, P):
                        rows = min(P, F - at)
                        src = bgu_rep[0:rows, at // P].rearrange("p m t r -> p (m t r)")
                        ins = pe.transpose(bk[:, at - n:at - n + rows], src, ident[0:rows, 0:rows])
                elif step == AD:
                    for c in range(FC):
                        ins = pe.transpose(bk[:, c * RANK:(c + 1) * RANK], ad_raw[:, c * P:(c + 1) * P], ident[0:RANK, 0:RANK])
                else:
                    for c in range(DC):
                        src = bd_rep[:, c].rearrange("p t r -> p (t r)")
                        ins = pe.transpose(bk[0:2 * RANK, c * P:(c + 1) * P], src, ident[:])
                ins.then_inc(in_psum, 1)

            def adapter_transposed(i, step, turn):
                c = [W0, W1, W2, W3].index(step) if step != Z else 0
                if step == Z:
                    pe.wait_ge(added, i)
                else:
                    pe.wait_ge(w_loaded[c % 2], (i - 1) * 32 + (c // 2 + 1) * 16)
                free_bank(i, step, turn)
                bk = ps[:, step_bank(step, turn), :]
                for n in range(DC):
                    src = x_res[:, n * P:(n + 1) * P] if step == Z else w_raw[c % 2][:, n, :]
                    ins = pe.transpose(bk[:, n * P:(n + 1) * P], src, ident[:])
                ins.then_inc(in_psum, 1)

            def adapter_product(i, turn):
                parts_done(i, W3, turn)
                for c in range(DC):
                    ins = three_pass(pe, ps[:, DOWN_BANK, :], zT_hi[:, c, :], zT_lo[:, c, :], wT_hi[:, c, :], wT_lo[:, c, :],
                                     c == 0, c == DC - 1)
                ins.then_inc(product_done, 1)

            def into_ranks(i, turn):
                parts_done(i, AGU, turn)
                free_bank(i, TGU, turn)
                for c in range(DC):
                    ins = three_pass(pe, ps[:, step_bank(TGU, turn), 0:S], aguT_hi[:, c, :], aguT_lo[:, c, :],
                                     xT_hi[:, c, :], xT_lo[:, c, :], c == 0, c == DC - 1)
                ins.then_inc(in_psum, 1)

            def gate_up(i, n):
                at, k = FN[n]
                cols = slice(at, at + k)
                if n == 2:
                    pe.wait_ge(act_done, i * len(FN) + 1)
                for m, (wh, wl) in enumerate(((gT_hi, gT_lo), (uT_hi, uT_lo))):
                    bk = ps[:, 2 * (n % 2) + m, 0:k]
                    for c in range(DC):
                        three_pass(pe, bk, xT_hi[:, c, :], xT_lo[:, c, :], wh[:, c, cols], wl[:, c, cols], c == 0, False)
                    r = slice(m * (R2 // 2), (m + 1) * (R2 // 2))
                    ins = pe.matmul(bk, tgu[r, :], bguT[r, cols], start=False, stop=True)
                ins.then_inc(gu_in_psum, 1)

            def down(cs):
                for c in cs:
                    rows = P if c < FC - 1 else FR
                    three_pass(pe, ps[:, DOWN_BANK, :], actT_hi[0:rows, c, :], actT_lo[0:rows, c, :],
                               dT_hi[0:rows, c, :], dT_lo[0:rows, c, :], c == 0, False)

            def follow(i, steps, turn):
                if turn is not LAST:
                    for step in steps:
                        next_transposed(i, step, turn, i + 1)

            def batch(i, turn):
                gate_up(i, 0)
                if turn is not FIRST:
                    for step in (W0, W1, Z):
                        adapter_transposed(i, step, turn)
                gate_up(i, 1)
                if turn is not FIRST:
                    for step in (W2, W3):
                        adapter_transposed(i, step, turn)
                act_transposed(i, ACT0, turn)
                gate_up(i, 2)
                act_transposed(i, ACT1, turn)
                if turn is not FIRST:
                    adapter_product(i, turn)
                follow(i, (X,), turn)
                act_transposed(i, ACT2, turn)
                follow(i, (AGU,), turn)
                if turn is not FIRST:
                    pe.wait_ge(result_done, i)
                down(range(0, 4))
                follow(i, (BGU0,), turn)
                parts_done(i, ACT1, turn)
                down(range(4, 8))
                follow(i, (BGU1,), turn)
                parts_done(i, ACT2, turn)
                free_bank(i, TD, turn)
                for c in range(FC):
                    rows = P if c < FC - 1 else FR
                    ranks = adT[0:rows, c, :, :].rearrange("p t r -> p (t r)")
                    at = ps[0:2 * RANK, step_bank(TD, turn), 0:S]
                    pe.matmul(at, ranks, actT_hi[0:rows, c, :], start=c == 0, stop=False)
                    ins = pe.matmul(at, ranks, actT_lo[0:rows, c, :], start=False, stop=c == FC - 1)
                ins.then_inc(in_psum, 1)
                follow(i, (BGU2,), turn)
                down(range(8, FC))
                if turn is not LAST:
                    into_ranks(i, turn)
                follow(i, (AD,), turn)
                parts_done(i, TD, turn)
                three_pass(pe, ps[:, DOWN_BANK, :], td_hi[:], td_lo[:], bdT_hi[:], bdT_lo[:], False, True).then_inc(down_in_psum, 1)
                follow(i, (BD,), turn)

            for step in AHEAD:
                if step == TGU:
                    into_ranks(0, AHEAD)
                else:
                    next_transposed(0, step, AHEAD, 0)
            pe.wait_ge(out_done, len(AHEAD))
            batch(0, FIRST)
            with pe.Fori(1, B - 1) as i:
                pe.wait_ge(out_done, before(i, TURN) - 2)
                batch(i, TURN)
            pe.wait_ge(out_done, before(B - 1, LAST) - 2)
            batch(B - 1, LAST)
            for step in TAIL:
                adapter_transposed(B, step, TAIL)
            adapter_product(B, TAIL)


def stages(nc, t, inv_freq, x_mid, out):
    with ExitStack() as ctx:
        xres = ctx.enter_context(nc.sbuf_tensor("xres", [P, B, DM], F32))
        staging = ctx.enter_context(nc.sbuf_tensor("staging", [P, DC, DM], F32))
        ident = ctx.enter_context(nc.sbuf_tensor("ident", [P, P], F32))
        dense_w_staged = ctx.enter_context(nc.semaphore("dense_w_staged"))
        gate_staged = ctx.enter_context(nc.semaphore("gate_staged"))
        tokens_stored = ctx.enter_context(nc.semaphore("tokens_stored"))
        attention(nc, t["x"], t["itok_Bx16_0_63"], t["itok_B_207_1644"], t["L0_cond_Wq"], t["L0_cond_Wk"], t["L0_cond_Wv"],
                  t["L0_cond_Wo"], t["L0_cond_q_norm_w"], t["L0_cond_k_norm_w"], t["L0_cond_k_cache"], t["L0_cond_v_cache"],
                  inv_freq, ident, xres, staging, t["L1_cond_W"], dense_w_staged)
        dense_signed(nc, ident, xres, staging, dense_w_staged, t["L1_cond_b"], t["condB_coeff"], t["mask_Bx4096x4096_ik1"], x_mid,
                     tokens_stored, t["L2_cond_W_gate"], gate_staged)
        swiglu_adapters(nc, ident, x_mid, *[t[f"L2_cond_{n}"] for n in ("W_gate", "W_up", "W_down", "A_gate", "B_gate", "A_up", "B_up", "A_down", "B_down")],
                        t["itok_B_2_6"], t["L3_cond_weight"], t["itok_B_3_7"], out, xres, tokens_stored, staging, gate_staged)


_INS = ["x", "itok_Bx16_0_63", "itok_B_207_1644", "condB_coeff", "itok_B_2_6", "itok_B_3_7", "mask_Bx4096x4096_ik1",
        "L0_cond_Wq", "L0_cond_Wk", "L0_cond_Wv", "L0_cond_Wo", "L0_cond_q_norm_w", "L0_cond_k_norm_w",
        "L0_cond_k_cache", "L0_cond_v_cache", "L1_cond_W", "L1_cond_b", "L2_cond_W_gate", "L2_cond_W_up", "L2_cond_W_down",
        "L2_cond_A_gate", "L2_cond_B_gate", "L2_cond_A_up", "L2_cond_B_up", "L2_cond_A_down", "L2_cond_B_down",
        "L3_cond_weight"]


def kernel(**inputs):
    import concourse.bacc as bacc
    from concourse.bass_utils import run_bass_kernel_spmd

    nc = bacc.Bacc("TRN2", target_bir_lowering=False, num_devices=1)
    arrays, t = {}, {}
    for name in _INS:
        a = np.ascontiguousarray(inputs[name])
        arrays[f"in_{name}"] = a
        t[name] = nc.dram_tensor(f"in_{name}", a.shape, mybir.dt.from_np(a.dtype), kind="ExternalInput").ap()
    inv = (1.0 / np.power(np.float32(THETA), np.arange(0, D, 2, dtype=np.float32) / np.float32(D))).astype(np.float32)
    arrays["inv_freq"] = inv
    inv_freq = nc.dram_tensor("inv_freq", inv.shape, F32, kind="ExternalInput").ap()
    x_mid = nc.dram_tensor("x_mid", (B, S, DM), F32).ap()
    out = nc.dram_tensor("out", (B, S, DM), F32, kind="ExternalOutput").ap()
    stages(nc, t, inv_freq, x_mid, out)
    r = run_bass_kernel_spmd(nc, [arrays], core_ids=[0])
    return r.results[0]["out"]
```
